# Optimizing a Trainium2 kernel written in Bass

```python
import numpy as np
import jax
import jax.numpy as jnp

def _softmax(x, axis=-1):
    return jax.nn.softmax(x, axis=axis)

def _gelu(x):
    return jax.nn.gelu(x, approximate=True)

def _silu(x):
    return jax.nn.silu(x)

def _sigmoid(x):
    return jax.nn.sigmoid(x)

def _layernorm(x, axis=-1, eps=1e-05):
    m = jnp.mean(x, axis=axis, keepdims=True)
    v = jnp.var(x, axis=axis, keepdims=True)
    return (x - m) / jnp.sqrt(v + eps)

def _scatter_add(tgt, idx, src, axis=0):
    return tgt.at[idx].add(src)

def _segment_sum(src, seg, n):
    return jax.ops.segment_sum(src, seg, n)
kernel_name = 'mk_cond_seq_d2_seqx_r4_2cb022'

def setup_inputs(seed: int=0):
    np.random.seed(seed)
    _w = jnp.asarray

    def _rec_inputs():
        import jax
        import jax.numpy as jnp
        _rk = jax.random.key(seed)
        x = -0.0002928 + 1 * jax.random.normal(jax.random.fold_in(_rk, 1), (128, 64, 256), jnp.float32)
        _lenS = 64 - jax.random.randint(jax.random.fold_in(_rk, 7), (128,), 0, max(1, 64 // 4) + 1, jnp.int32)
        _lenS2 = 64 - jax.random.randint(jax.random.fold_in(_rk, 8), (128,), 0, max(1, 64 // 4) + 1, jnp.int32)
        cond_1024 = 0.0061147 + 1.02565 * jax.random.normal(jax.random.fold_in(_rk, 11), (128, 256), jnp.float32)
        _validS = jnp.arange(64)[None, :] < _lenS[:, None]
        _validS2 = jnp.arange(64)[None, :] < _lenS2[:, None]
        _causal = jnp.tril(jnp.ones((64, 64), dtype=bool))
        mask_BxS_bf1 = jnp.ones((128, 64), dtype=bool)
        return (x, cond_1024, mask_BxS_bf1)
    x, cond_1024, mask_BxS_bf1 = _rec_inputs()

    def _L0_cond_setup():
        import jax, jax.numpy as jnp
        import numpy as np
        B, N, D, H = (4, 256, 256, 16)
        DFF = 4 * D
        GATE_SCALE = 0.1
        LN_EPS = 1e-05

        def _layernorm(v, g, b):
            mu = jnp.mean(v, axis=-1, keepdims=True)
            var = jnp.mean(jnp.square(v - mu), axis=-1, keepdims=True)
            return (v - mu) * jax.lax.rsqrt(var + LN_EPS) * g + b

        def _attention(y, qkv_w, qkv_b, proj_w, proj_b):
            Bq, Nq, C = y.shape
            dh = C // H
            qkv = (y @ qkv_w + qkv_b).reshape(Bq, Nq, 3, H, dh)
            q, k, v = jnp.moveaxis(qkv, 2, 0)
            scale = dh ** (-0.5)
            attn = jnp.einsum('bqhd,bkhd->bhqk', q, k) * scale
            attn = jax.nn.softmax(attn, axis=-1)
            out = jnp.einsum('bhqk,bkhd->bqhd', attn, v).reshape(Bq, Nq, C)
            return out @ proj_w + proj_b
        key = jax.random.key(seed)
        ks = jax.random.split(key, 32)
        s = 0.02

        def w(k, shape):
            return jax.random.normal(k, shape, dtype=jnp.float32) * s
        inp = {'x': jax.random.normal(ks[0], (B, N, D), dtype=jnp.float32), 'cond': jax.random.normal(ks[1], (B, D), dtype=jnp.float32), 'g1_w': w(ks[2], (D, D)), 'g1_b': w(ks[3], (D,)), 'b1_w': w(ks[4], (D, D)), 'b1_b': w(ks[5], (D,)), 'a1_w': w(ks[6], (D, D)), 'a1_b': w(ks[7], (D,)), 'g2_w': w(ks[8], (D, D)), 'g2_b': w(ks[9], (D,)), 'b2_w': w(ks[10], (D, D)), 'b2_b': w(ks[11], (D,)), 'a2_w': w(ks[12], (D, D)), 'a2_b': w(ks[13], (D,)), 'ln1_g': jnp.ones((D,), jnp.float32), 'ln1_b': jnp.zeros((D,), jnp.float32), 'ln2_g': jnp.ones((D,), jnp.float32), 'ln2_b': jnp.zeros((D,), jnp.float32), 'qkv_w': w(ks[14], (D, 3 * D)), 'qkv_b': w(ks[15], (3 * D,)), 'proj_w': w(ks[16], (D, D)), 'proj_b': w(ks[17], (D,)), 'fc1_w': w(ks[18], (D, DFF)), 'fc1_b': w(ks[19], (DFF,)), 'fc2_w': w(ks[20], (DFF, D)), 'fc2_b': w(ks[21], (D,))}
        return inp
    _L0_cond_all = _L0_cond_setup()
    _L0_cond_in = {k: v for k, v in _L0_cond_all.items() if k in ('g1_w', 'g1_b', 'b1_w', 'b1_b', 'a1_w', 'a1_b', 'g2_w', 'g2_b', 'b2_w', 'b2_b', 'a2_w', 'a2_b', 'ln1_g', 'ln1_b', 'ln2_g', 'ln2_b', 'qkv_w', 'qkv_b', 'proj_w', 'proj_b', 'fc1_w', 'fc1_b', 'fc2_w', 'fc2_b')}
    del _L0_cond_all

    def _L1_cond_setup():
        import jax, jax.numpy as jnp
        import numpy as np
        B, S, H, NH = (2, 512, 256, 16)
        HD = H // NH
        ROT = HD // 2
        COND, FF = (256, 4 * H)
        BASE = 10000.0
        EPS = 1e-05

        def _layer_norm(x, g, b):
            mu = jnp.mean(x, axis=-1, keepdims=True)
            var = jnp.mean(jnp.square(x - mu), axis=-1, keepdims=True)
            return (x - mu) * jax.lax.rsqrt(var + EPS) * g + b

        def _ada_norm(x, cond, g, b, w, bw):
            shift, scale = jnp.split(cond @ w + bw, 2, axis=-1)
            return _layer_norm(x, g, b) * (1.0 + scale[:, None, :]) + shift[:, None, :]

        def _rotary_sin_cos(seq_len):
            inv_freq = 1.0 / BASE ** (jnp.arange(ROT, dtype=jnp.float32) / ROT)
            freqs = jnp.arange(seq_len, dtype=jnp.float32)[:, None] * inv_freq[None, :]
            return (jnp.sin(freqs), jnp.cos(freqs))

        def _apply_rotary(x, sin, cos):
            xe, xo = (x[..., ::2], x[..., 1::2])
            re = xe * cos - xo * sin
            ro = xo * cos + xe * sin
            return jnp.stack((re, ro), axis=-1).reshape(x.shape)

        def _split_heads(x):
            b, s, _ = x.shape
            return x.reshape(b, s, NH, HD).transpose(0, 2, 1, 3)
        key = jax.random.key(seed)
        ks = jax.random.split(key, 16)
        w = lambda k, shape: jax.random.normal(k, shape, dtype=jnp.float32) * 0.02
        z = lambda shape: jnp.zeros(shape, dtype=jnp.float32)
        o = lambda shape: jnp.ones(shape, dtype=jnp.float32)
        return {'x': jax.random.normal(ks[0], (B, S, H), dtype=jnp.float32), 'cond': jax.random.normal(ks[1], (B, COND), dtype=jnp.float32), 'attn_mask': jnp.ones((B, S), dtype=bool), 'wq': w(ks[2], (H, H)), 'bq': z((H,)), 'wk': w(ks[3], (H, H)), 'bk': z((H,)), 'wv': w(ks[4], (H, H)), 'bv': z((H,)), 'wo': w(ks[5], (H, H)), 'bo': z((H,)), 'ln1_g': o((H,)), 'ln1_b': z((H,)), 'ada1_w': w(ks[6], (COND, 2 * H)), 'ada1_b': z((2 * H,)), 'ln2_g': o((H,)), 'ln2_b': z((H,)), 'ada2_w': w(ks[7], (COND, 2 * H)), 'ada2_b': z((2 * H,)), 'ff_w1': w(ks[8], (H, FF)), 'ff_b1': z((FF,)), 'ff_w2': w(ks[9], (FF, H)), 'ff_b2': z((H,))}
    _L1_cond_all = _L1_cond_setup()
    _L1_cond_in = {k: v for k, v in _L1_cond_all.items() if k in ('wq', 'bq', 'wk', 'bk', 'wv', 'bv', 'wo', 'bo', 'ln1_g', 'ln1_b', 'ada1_w', 'ada1_b', 'ln2_g', 'ln2_b', 'ada2_w', 'ada2_b', 'ff_w1', 'ff_b1', 'ff_w2', 'ff_b2')}
    del _L1_cond_all
    return {'x': x, 'cond_1024': cond_1024, 'mask_BxS_bf1': mask_BxS_bf1, 'L0_cond_g1_w': _L0_cond_in['g1_w'], 'L0_cond_g1_b': _L0_cond_in['g1_b'], 'L0_cond_b1_w': _L0_cond_in['b1_w'], 'L0_cond_b1_b': _L0_cond_in['b1_b'], 'L0_cond_a1_w': _L0_cond_in['a1_w'], 'L0_cond_a1_b': _L0_cond_in['a1_b'], 'L0_cond_g2_w': _L0_cond_in['g2_w'], 'L0_cond_g2_b': _L0_cond_in['g2_b'], 'L0_cond_b2_w': _L0_cond_in['b2_w'], 'L0_cond_b2_b': _L0_cond_in['b2_b'], 'L0_cond_a2_w': _L0_cond_in['a2_w'], 'L0_cond_a2_b': _L0_cond_in['a2_b'], 'L0_cond_ln1_g': _L0_cond_in['ln1_g'], 'L0_cond_ln1_b': _L0_cond_in['ln1_b'], 'L0_cond_ln2_g': _L0_cond_in['ln2_g'], 'L0_cond_ln2_b': _L0_cond_in['ln2_b'], 'L0_cond_qkv_w': _L0_cond_in['qkv_w'], 'L0_cond_qkv_b': _L0_cond_in['qkv_b'], 'L0_cond_proj_w': _L0_cond_in['proj_w'], 'L0_cond_proj_b': _L0_cond_in['proj_b'], 'L0_cond_fc1_w': _L0_cond_in['fc1_w'], 'L0_cond_fc1_b': _L0_cond_in['fc1_b'], 'L0_cond_fc2_w': _L0_cond_in['fc2_w'], 'L0_cond_fc2_b': _L0_cond_in['fc2_b'], 'L1_cond_wq': _L1_cond_in['wq'], 'L1_cond_bq': _L1_cond_in['bq'], 'L1_cond_wk': _L1_cond_in['wk'], 'L1_cond_bk': _L1_cond_in['bk'], 'L1_cond_wv': _L1_cond_in['wv'], 'L1_cond_bv': _L1_cond_in['bv'], 'L1_cond_wo': _L1_cond_in['wo'], 'L1_cond_bo': _L1_cond_in['bo'], 'L1_cond_ln1_g': _L1_cond_in['ln1_g'], 'L1_cond_ln1_b': _L1_cond_in['ln1_b'], 'L1_cond_ada1_w': _L1_cond_in['ada1_w'], 'L1_cond_ada1_b': _L1_cond_in['ada1_b'], 'L1_cond_ln2_g': _L1_cond_in['ln2_g'], 'L1_cond_ln2_b': _L1_cond_in['ln2_b'], 'L1_cond_ada2_w': _L1_cond_in['ada2_w'], 'L1_cond_ada2_b': _L1_cond_in['ada2_b'], 'L1_cond_ff_w1': _L1_cond_in['ff_w1'], 'L1_cond_ff_b1': _L1_cond_in['ff_b1'], 'L1_cond_ff_w2': _L1_cond_in['ff_w2'], 'L1_cond_ff_b2': _L1_cond_in['ff_b2']}

def reference(x, cond_1024, mask_BxS_bf1, L0_cond_g1_w, L0_cond_g1_b, L0_cond_b1_w, L0_cond_b1_b, L0_cond_a1_w, L0_cond_a1_b, L0_cond_g2_w, L0_cond_g2_b, L0_cond_b2_w, L0_cond_b2_b, L0_cond_a2_w, L0_cond_a2_b, L0_cond_ln1_g, L0_cond_ln1_b, L0_cond_ln2_g, L0_cond_ln2_b, L0_cond_qkv_w, L0_cond_qkv_b, L0_cond_proj_w, L0_cond_proj_b, L0_cond_fc1_w, L0_cond_fc1_b, L0_cond_fc2_w, L0_cond_fc2_b, L1_cond_wq, L1_cond_bq, L1_cond_wk, L1_cond_bk, L1_cond_wv, L1_cond_bv, L1_cond_wo, L1_cond_bo, L1_cond_ln1_g, L1_cond_ln1_b, L1_cond_ada1_w, L1_cond_ada1_b, L1_cond_ln2_g, L1_cond_ln2_b, L1_cond_ada2_w, L1_cond_ada2_b, L1_cond_ff_w1, L1_cond_ff_b1, L1_cond_ff_w2, L1_cond_ff_b2):
    import jax
    import jax.numpy as jnp

    def _L0_cond_ref(x, cond, g1_w, g1_b, b1_w, b1_b, a1_w, a1_b, g2_w, g2_b, b2_w, b2_b, a2_w, a2_b, ln1_g, ln1_b, ln2_g, ln2_b, qkv_w, qkv_b, proj_w, proj_b, fc1_w, fc1_b, fc2_w, fc2_b):
        import jax, jax.numpy as jnp
        import numpy as np
        B, N, D, H = (4, 256, 256, 16)
        DFF = 4 * D
        GATE_SCALE = 0.1
        LN_EPS = 1e-05

        def _layernorm(v, g, b):
            mu = jnp.mean(v, axis=-1, keepdims=True)
            var = jnp.mean(jnp.square(v - mu), axis=-1, keepdims=True)
            return (v - mu) * jax.lax.rsqrt(var + LN_EPS) * g + b

        def _attention(y, qkv_w, qkv_b, proj_w, proj_b):
            Bq, Nq, C = y.shape
            dh = C // H
            qkv = (y @ qkv_w + qkv_b).reshape(Bq, Nq, 3, H, dh)
            q, k, v = jnp.moveaxis(qkv, 2, 0)
            scale = dh ** (-0.5)
            attn = jnp.einsum('bqhd,bkhd->bhqk', q, k) * scale
            attn = jax.nn.softmax(attn, axis=-1)
            out = jnp.einsum('bhqk,bkhd->bqhd', attn, v).reshape(Bq, Nq, C)
            return out @ proj_w + proj_b
        gamma1 = cond @ g1_w + g1_b
        beta1 = cond @ b1_w + b1_b
        alpha1 = jnp.tanh(cond @ a1_w + a1_b) * GATE_SCALE
        gamma2 = cond @ g2_w + g2_b
        beta2 = cond @ b2_w + b2_b
        alpha2 = jnp.tanh(cond @ a2_w + a2_b) * GATE_SCALE
        y = _layernorm(x, ln1_g, ln1_b)
        y = y * (1.0 + gamma1[:, None, :]) + beta1[:, None, :]
        y = _attention(y, qkv_w, qkv_b, proj_w, proj_b)
        x = x + y * alpha1[:, None, :]
        z = _layernorm(x, ln2_g, ln2_b)
        z = z * (1.0 + gamma2[:, None, :]) + beta2[:, None, :]
        z = jax.nn.gelu(z @ fc1_w + fc1_b, approximate=False) @ fc2_w + fc2_b
        x = x + z * alpha2[:, None, :]
        return x

    def _L1_cond_ref(x, cond, attn_mask, wq, bq, wk, bk, wv, bv, wo, bo, ln1_g, ln1_b, ada1_w, ada1_b, ln2_g, ln2_b, ada2_w, ada2_b, ff_w1, ff_b1, ff_w2, ff_b2):
        import jax, jax.numpy as jnp
        import numpy as np
        B, S, H, NH = (2, 512, 256, 16)
        HD = H // NH
        ROT = HD // 2
        COND, FF = (256, 4 * H)
        BASE = 10000.0
        EPS = 1e-05

        def _layer_norm(x, g, b):
            mu = jnp.mean(x, axis=-1, keepdims=True)
            var = jnp.mean(jnp.square(x - mu), axis=-1, keepdims=True)
            return (x - mu) * jax.lax.rsqrt(var + EPS) * g + b

        def _ada_norm(x, cond, g, b, w, bw):
            shift, scale = jnp.split(cond @ w + bw, 2, axis=-1)
            return _layer_norm(x, g, b) * (1.0 + scale[:, None, :]) + shift[:, None, :]

        def _rotary_sin_cos(seq_len):
            inv_freq = 1.0 / BASE ** (jnp.arange(ROT, dtype=jnp.float32) / ROT)
            freqs = jnp.arange(seq_len, dtype=jnp.float32)[:, None] * inv_freq[None, :]
            return (jnp.sin(freqs), jnp.cos(freqs))

        def _apply_rotary(x, sin, cos):
            xe, xo = (x[..., ::2], x[..., 1::2])
            re = xe * cos - xo * sin
            ro = xo * cos + xe * sin
            return jnp.stack((re, ro), axis=-1).reshape(x.shape)

        def _split_heads(x):
            b, s, _ = x.shape
            return x.reshape(b, s, NH, HD).transpose(0, 2, 1, 3)
        residual = x
        h = _ada_norm(x, cond, ln1_g, ln1_b, ada1_w, ada1_b)
        q = _split_heads(h @ wq + bq)
        k = _split_heads(h @ wk + bk)
        v = _split_heads(h @ wv + bv)
        sin, cos = _rotary_sin_cos(x.shape[1])
        q = _apply_rotary(q, sin, cos)
        k = _apply_rotary(k, sin, cos)
        scores = jnp.einsum('bhqd,bhkd->bhqk', q, k) / np.sqrt(HD).astype(np.float32)
        scores = jnp.where(attn_mask[:, None, None, :], scores, -jnp.inf)
        attn = jax.nn.softmax(scores, axis=-1)
        out = jnp.einsum('bhqk,bhkd->bhqd', attn, v)
        out = out.transpose(0, 2, 1, 3).reshape(x.shape[0], x.shape[1], H)
        x = residual + out @ wo + bo
        residual = x
        h = _ada_norm(x, cond, ln2_g, ln2_b, ada2_w, ada2_b)
        ff = jax.nn.gelu(h @ ff_w1 + ff_b1, approximate=False) @ ff_w2 + ff_b2
        return residual + ff
    x = _L0_cond_ref(x, cond_1024, L0_cond_g1_w, L0_cond_g1_b, L0_cond_b1_w, L0_cond_b1_b, L0_cond_a1_w, L0_cond_a1_b, L0_cond_g2_w, L0_cond_g2_b, L0_cond_b2_w, L0_cond_b2_b, L0_cond_a2_w, L0_cond_a2_b, L0_cond_ln1_g, L0_cond_ln1_b, L0_cond_ln2_g, L0_cond_ln2_b, L0_cond_qkv_w, L0_cond_qkv_b, L0_cond_proj_w, L0_cond_proj_b, L0_cond_fc1_w, L0_cond_fc1_b, L0_cond_fc2_w, L0_cond_fc2_b)
    x = _L1_cond_ref(x, cond_1024, mask_BxS_bf1, L1_cond_wq, L1_cond_bq, L1_cond_wk, L1_cond_bk, L1_cond_wv, L1_cond_bv, L1_cond_wo, L1_cond_bo, L1_cond_ln1_g, L1_cond_ln1_b, L1_cond_ada1_w, L1_cond_ada1_b, L1_cond_ln2_g, L1_cond_ln2_b, L1_cond_ada2_w, L1_cond_ada2_b, L1_cond_ff_w1, L1_cond_ff_b1, L1_cond_ff_w2, L1_cond_ff_b2)
    return x

_drawn_inputs = setup_inputs


def setup_inputs(seed=0):
    import zlib

    import numpy as np

    out = dict(_drawn_inputs(seed))
    spreads = {'L0_cond_ln1_g': (1.0, 0.6),
     'L0_cond_ln1_b': (0.0, 0.8),
     'L0_cond_ln2_g': (1.0, 0.6),
     'L0_cond_ln2_b': (0.0, 0.8),
     'L1_cond_bq': (0.0, 2.0),
     'L1_cond_bk': (0.0, 2.0),
     'L1_cond_bv': (0.0, 0.8),
     'L1_cond_bo': (0.0, 0.434),
     'L1_cond_ln1_g': (1.0, 0.6),
     'L1_cond_ln1_b': (0.0, 2.0),
     'L1_cond_ada1_b': (0.0, 0.8),
     'L1_cond_ln2_g': (1.0, 0.6),
     'L1_cond_ln2_b': (0.0, 2.0),
     'L1_cond_ada2_b': (0.0, 2.0),
     'L1_cond_ff_b1': (0.0, 0.8),
     'L1_cond_ff_b2': (0.0, 0.384)}
    factors = {'L0_cond_g1_w': 8.0,
     'L0_cond_g1_b': 8.0,
     'L0_cond_b1_w': 8.0,
     'L0_cond_b1_b': 8.0,
     'L0_cond_a1_w': 8.0,
     'L0_cond_a1_b': 8.0,
     'L0_cond_g2_w': 8.0,
     'L0_cond_g2_b': 8.0,
     'L0_cond_b2_w': 8.0,
     'L0_cond_b2_b': 8.0,
     'L0_cond_a2_w': 8.0,
     'L0_cond_a2_b': 8.0,
     'L0_cond_qkv_w': 8.0,
     'L0_cond_qkv_b': 8.0,
     'L0_cond_proj_w': 8.0,
     'L0_cond_proj_b': 64.0,
     'L0_cond_fc1_w': 8.0,
     'L0_cond_fc1_b': 47.3,
     'L0_cond_fc2_w': 8.0,
     'L0_cond_fc2_b': 177.512,
     'L1_cond_wq': 22.233,
     'L1_cond_wk': 21.853,
     'L1_cond_ada1_w': 3.092,
     'L1_cond_ada2_w': 4.062}
    for name, (base, spread) in spreads.items():
        noise = np.random.default_rng([zlib.crc32(name.encode()), seed]).standard_normal(out[name].shape)
        drawn = base * np.exp(spread * noise) if base else spread * noise
        out[name] = jnp.asarray(drawn.astype(out[name].dtype))
    for name, factor in factors.items():
        out[name] = (out[name] * factor).astype(out[name].dtype)
    return out
```

```python
from contextlib import ExitStack

import concourse.bass as bass
from concourse import mybir

F32 = mybir.dt.float32
F32R = mybir.dt.float32r
U8 = mybir.dt.uint8
ALU = mybir.AluOpType
ACT = mybir.ActivationFunctionType
AX = mybir.AxisListType

P = 128
NB, S, D = 128, 64, 256
H, HD = 16, 16
FF = 4 * D
KC = D // P
MC = FF // P
TILE = 512
G = TILE // P
TB = TILE // S
NT = NB * S // TILE
NX, NJ = 2, 4
VB = HD + 1
VROW = H * VB
EPS = 1e-5
GATE = 0.1
SCORE_SCALE = HD ** -0.5
BIG = 2.0 ** 100
ROT = HD // 2

W_QKV, W_PROJ = 0, KC * 3 * D
W_FF1 = W_PROJ + KC * D
W_FF2 = W_FF1 + KC * FF
W_ALL = W_FF2 + MC * D
PASSES = ((0, 0), (1, 0), (0, 1))


def build(nc, t, out):
    ctx = ExitStack()
    with ctx:
        def sb(name, shape, dt=F32):
            return ctx.enter_context(nc.sbuf_tensor(name, shape, dt))

        def bank(name):
            return ctx.enter_context(nc.psum_tensor(name, [P, 512], F32))

        def sem(name):
            return ctx.enter_context(nc.semaphore(name))

        x_tiles = t["x"].rearrange("b s d -> (b s) d").rearrange("(t g p) d -> t p g d", g=G, p=P)
        mid = nc.dram_tensor("mid", [NB * S, D], F32, kind="Internal").ap()
        mid_tiles = mid.rearrange("(t g p) d -> t p g d", g=G, p=P)
        out_tiles = out.rearrange("b s d -> (b s) d").rearrange("(t g p) d -> t p g d", g=G, p=P)
        gates = [nc.dram_tensor(f"gates{n}", [NB, D], F32, kind="Internal").ap() for n in range(2)]
        gate_tiles = [g.rearrange("(t g b) d -> t b g d", g=G, b=2) for g in gates]
        mask_rows = nc.dram_tensor("mask_rows", [NB, S], F32, kind="Internal").ap()
        mask_tiles = mask_rows.rearrange("(t b) s -> t (b s)", b=TB)

        wgt = [sb("wgt_hi", [P, W_ALL], F32R), sb("wgt_lo", [P, W_ALL], F32R)]
        TE = G * D
        arena = sb("arena", [P, 9 * TE])

        def view(n, k=1):
            return arena[:, n * TE:(n + k) * TE]

        def tokens(n):
            return view(n).rearrange("p (g d) -> p g d", g=G)

        x_in, xn, x_res, x1m, zn = (tokens(n) for n in range(5))
        aff = view(5).rearrange("p (c n) -> p c n", c=KC)
        exps = view(6).rearrange("p (b n) -> p b n", b=2)
        gate_bc = [tokens(7), tokens(8)]
        rot_t = view(7).rearrange("p (r n) -> p r n", r=2)
        rot_s = view(8).rearrange("p (r n) -> p r n", r=2)
        w_raw = view(0, 6)
        mod_raw = [view(6, 3)[:, n * KC * D:(n + 1) * KC * D].rearrange("p (k n) -> p k n", k=KC)
                   for n in range(6)]
        yb = [sb("y_hi", [P, KC, TILE], F32R), sb("y_lo", [P, KC, TILE], F32R)]
        zb = [sb("z_hi", [P, KC, TILE], F32R), sb("z_lo", [P, KC, TILE], F32R)]
        qb = [sb("q_hi", [P, KC, TB, NX, S], F32R), sb("q_lo", [P, KC, TB, NX, S], F32R)]
        kflat = sb("k_flat", [P, KC, 2, TILE], F32R)
        kb = sb("k_blocks", [P, KC, 2, NJ, TILE], F32R)
        vb = [sb("v_hi", [P, TB, VROW], F32R), sb("v_lo", [P, TB, VROW], F32R)]
        pt = [sb("pt_hi", [P, 2, 512], F32R), sb("pt_lo", [P, 2, 512], F32R)]
        o_sb = sb("o_sb", [P, 2, P])
        ot = [sb("ot_hi", [P, NX, P], F32R), sb("ot_lo", [P, NX, P], F32R)]
        hact = sb("hact", [P, 2, TILE])
        hb = [sb("h_hi", [P, 2, TILE], F32R), sb("h_lo", [P, 2, TILE], F32R)]
        mod = sb("mod", [P, 2, KC, 2, NB])
        ident = sb("ident", [P, P])
        ones = sb("ones", [1, P])
        mod_tile = sb("mod_tile", [P, 2, KC, 2, TB])
        bo_bc = sb("bo_bc", [P, D])
        b2_bc = sb("b2_bc", [P, D])
        qk_bias = sb("qk_bias", [P, 2 * KC])
        v_bias = sb("v_bias", [P, NX])
        b1_col = sb("b1_col", [P, MC])
        ln_col = sb("ln_col", [P, 2, 2, KC])
        mod_col = sb("mod_col", [P, 2, 2, KC])
        mx = sb("mx", [P, 2, 8])
        rden = sb("rden", [P, 2, 8])
        st1 = sb("st1", [P, G, 6])
        mv1 = sb("mv1", [P, G, 2])
        rs1 = sb("rs1", [P, G])
        st2 = sb("st2", [P, G, 6])
        mv2 = sb("mv2", [P, G, 2])
        rs2 = sb("rs2", [P, G])
        minus_half = sb("minus_half", [P, G])
        rtab = sb("rtab", [P, 2, S])
        mrow = sb("mrow", [P, TILE], F32R)
        mean_w = sb("mean_w", [P, P], F32R)
        mask_u8 = sb("mask_u8", [P, S], U8)
        mask01 = view(8)[:, 0:2 * S].rearrange("p (a s) -> p a s", a=2)
        maskT = sb("maskT", [P, NB])
        cond_sb = hact[:, 0, 0:D]
        condT = hact[:, 0, D:2 * D].rearrange("p (k b) -> p k b", k=KC)
        gate_row = hact[0:1, 1, :].rearrange("p (n d) -> p n d", n=2)
        gate_rows = hact[:, 1, :].rearrange("p (n d) -> p n d", n=2)
        mask_add = hact[:, 1, 0:S]

        A = [bank("A0"), bank("A1")]
        B = [bank("B0"), bank("B1")]
        C = bank("C")
        Dk = [bank("D0"), bank("D1")]
        E = bank("E")

        sem_in = sem("setup_loaded")
        sem_ident = sem("consts_ready")
        sem_zero = sem("zeros_ready")
        w_hi, w_lo = sem("w_hi"), sem("w_lo")
        pe_setup, dve_setup, act_setup = sem("pe_setup"), sem("dve_setup"), sem("act_setup")
        gates_out = sem("gates_out")
        x_loaded, x_stored = sem("x_loaded"), sem("x_stored")
        gate1_in, gate2_in, mrow_in = sem("gate1_in"), sem("gate2_in"), sem("mrow_in")
        kb_in = sem("kb_in")
        swapped = [sem("swapped0"), sem("swapped1")]
        xn_ready, ln1_chain, ln1_rstd = sem("xn_ready"), sem("ln1_chain"), sem("ln1_rstd")
        pe_yt, y_aff, y_hi, y_lo = sem("pe_yt"), sem("y_aff"), sem("y_hi"), sem("y_lo")
        pe_qk, qk_hi, qk_lo = sem("pe_qk"), sem("qk_hi"), sem("qk_lo")
        rot_ready, rot_cos, rot_sin, rot_sum = sem("rot_ready"), sem("rot_cos"), sem("rot_sin"), sem("rot_sum")
        pe_v, v_hi, v_lo, v_ones = sem("pe_v"), sem("v_hi"), sem("v_lo"), sem("v_ones")
        pe_s, s_max, s_sub, s_exp = sem("pe_s"), sem("s_max"), sem("s_sub"), sem("s_exp")
        pe_pt, pt_hi, pt_lo = sem("pe_pt"), sem("pt_hi"), sem("pt_lo")
        pe_pv, pv_rden, pv_norm = sem("pe_pv"), sem("pv_rden"), sem("pv_norm")
        pe_ot, ot_hi, ot_lo = sem("pe_ot"), sem("ot_hi"), sem("ot_lo")
        pe_proj, proj_read, x1_added = sem("pe_proj"), sem("proj_read"), sem("x1_added")
        ln2_chain, zn_ready, ln2_rstd = sem("ln2_chain"), sem("zn_ready"), sem("ln2_rstd")
        xres_chain, xres_ready, x1m_chain, x1m_ready = (sem("xres_chain"), sem("xres_ready"),
                                                        sem("x1m_chain"), sem("x1m_ready"))
        pe_zt, z_aff, z_hi, z_lo = sem("pe_zt"), sem("z_aff"), sem("z_hi"), sem("z_lo")
        pe_f1, gelu, h_hi, h_lo, pe_f2 = sem("pe_f1"), sem("gelu"), sem("h_hi"), sem("h_lo"), sem("pe_f2")
        f2_read, f2_added = sem("f2_read"), sem("f2_added")
        sp_passed, dve_passed = sem("sp_passed"), sem("dve_passed")
        mod_ready = [sem("mod1_ready"), sem("mod2_ready")]
        x1_done = [x1_added, proj_read]
        f2_done = [f2_added, f2_read]

        block = ctx.enter_context(nc.Block())

        def upto(u, n, k):
            return u * n + k

        def known(u):
            return isinstance(u, int)

        def wait_apart(eng, passed, *waits):
            for semaphore, count in waits:
                eng.wait_ge(semaphore, count)
                eng.sem_inc(passed, 1)

        def w_slice(part, base, width, k, lo, n):
            return wgt[part][:, base + k * width + lo:base + k * width + lo + n]

        def by_seq(ap):
            return ap.rearrange("p (b s) -> p b s", s=S)

        def value_views(part, pair, b, h):
            dst = vb[part][h * S:(h + 1) * S, 4 * pair + b:4 * pair + b + 3:2, :].rearrange(
                "p g (n e) -> p g n e", e=2 * VB)[:, :, :, h * VB:h * VB + HD]
            src = A[pair][b * S:(b + 1) * S, :].rearrange("p (g n h d) -> p g n h d", g=2, h=2, d=HD)[:, :, :, h, :]
            return dst, src

        def head_rows(x):
            return E[:, 0:2 * P].rearrange("p (b x q) -> p b x q", b=2, x=NX)[:, :, x, :]

        def first(u):
            return known(u) and u == 0

        def layer_steps(eng, layer, setup, front, step):
            u0 = layer * NT
            setup(layer)
            front(u0, layer)
            step(u0, layer, True, False, True)
            step(u0 + 1, layer, True, True, True)
            with eng.Fori(u0 + 2, u0 + NT - 1) as u:
                step(u, layer, True, True, True)
            step(u0 + NT - 1, layer, True, True, False)
            step(u0 + NT, layer, False, True, False)

        LOADS = (29, 29)
        NZERO = 9
        NSPLIT = 4
        SPLIT = W_ALL // NSPLIT
        NMOD = 16
        SET_CONDT, SET_MOD0, SET_GATES = 1, 1 + NMOD, 2 + NMOD
        SET_MASK, SET_CONDT1 = SET_GATES + 3, SET_GATES + 4
        SET_MASKT = SET_CONDT1 + NMOD + 1
        NKB = 16 * KC * NX * NJ

        def loads_in(eng, layer):
            eng.wait_ge(sem_in, 16 * sum(LOADS[:layer + 1]))

        @block.sync
        def _(sp):
            def setup(layer):
                if layer == 1:
                    sp.wait_ge(f2_added, 2 * NT)
                    sp.wait_ge(x_stored, 16 * NT)
                count = 0

                def ld(dst, src, **kw):
                    nonlocal count
                    sp.dma_start(dst, src, **kw).then_inc(sem_in, 16)
                    count += 1

                def rows(m):
                    return m.rearrange("(k p) n -> p k n", p=P)

                def ld_column(dst, vec, p=P):
                    ld(dst, vec.rearrange("(c p) -> p c", p=p), allow_slow_non_contiguous=True)

                def row(vec):
                    return vec.rearrange("(o n) -> o n", o=1)

                w = {k[8:]: v for k, v in t.items() if k.startswith(f"L{layer}_cond_")}
                qkv = w_raw[:, W_QKV:W_PROJ].rearrange("p (k n) -> p k n", k=KC)
                ld(cond_sb, t["cond_1024"])
                if layer == 0:
                    for n, m in enumerate(("g1", "b1", "g2", "b2", "a1", "a2")):
                        ld(mod_raw[n], rows(w[m + "_w"]))
                    for n in range(2):
                        ld(gate_row[:, n, :], row(w[f"a{n + 1}_b"]))
                    mod_bias = [[w["g1_b"], w["b1_b"]], [w["g2_b"], w["b2_b"]]]
                    ld(qkv, rows(w["qkv_w"]))
                    qbias, kbias, vbias = (w["qkv_b"][n * D:(n + 1) * D] for n in range(3))
                    proj_w, proj_b, w1, b1, w2, b2 = (w[n] for n in ("proj_w", "proj_b", "fc1_w", "fc1_b", "fc2_w",
                                                                     "fc2_b"))
                else:
                    for n in range(2):
                        for k in range(2):
                            ld(mod_raw[2 * n + k], rows(w[f"ada{n + 1}_w"][:, (1 - k) * D:(2 - k) * D]))
                    mod_bias = [[w[f"ada{n}_b"][D:2 * D], w[f"ada{n}_b"][0:D]] for n in (1, 2)]
                    for n, m in enumerate("qkv"):
                        ld(qkv[:, :, n * D:(n + 1) * D], rows(w["w" + m]))
                    qbias, kbias, vbias = w["bq"], w["bk"], w["bv"]
                    proj_w, proj_b, w1, b1, w2, b2 = (w[n] for n in ("wo", "bo", "ff_w1", "ff_b1", "ff_w2", "ff_b2"))
                    ld(mask_u8[:, :], t["mask_BxS_bf1"])
                    ld(rtab[:, :, :], t["rotary"])
                half = NJ * HD
                for c in range(KC):
                    ld(w_raw[c * half:(c + 1) * half, W_PROJ:W_FF1].rearrange("r (x n) -> r x n", x=NX),
                       proj_w[c * P:(c + 1) * P, :].rearrange("(x r) n -> r x n", x=NX))
                    ld_column(v_bias[c * half:(c + 1) * half, :], vbias[c * P:(c + 1) * P], half)
                ld(w_raw[:, W_FF1:W_FF2].rearrange("p (k n) -> p k n", k=KC), rows(w1))
                ld(w_raw[:, W_FF2:W_ALL].rearrange("p (k n) -> p k n", k=MC), rows(w2))
                ld_column(qk_bias[:, 0:KC], qbias)
                ld_column(qk_bias[:, KC:2 * KC], kbias)
                ld_column(b1_col[:, :], b1)
                ld(bo_bc[:, :], proj_b.partition_broadcast(P))
                ld(b2_bc[:, :], b2.partition_broadcast(P))
                for n in range(2):
                    for k, what in enumerate("gb"):
                        ld_column(ln_col[:, n, k, :], w[f"ln{n + 1}_{what}"])
                        ld_column(mod_col[:, n, k, :], mod_bias[n][k])
                assert count == LOADS[layer], (layer, count)
                if layer == 0:
                    sp.wait_ge(dve_setup, SET_GATES)
                    for n in range(2):
                        sp.dma_start(gates[n], gate_rows[:, n, :]).then_inc(gates_out, 16)
                    sp.wait_ge(gates_out, 32)
                else:
                    sp.wait_ge(dve_setup, SET_MASK)
                    sp.dma_start(mask_rows, mask_add).then_inc(gates_out, 16)
                    sp.wait_ge(gates_out, 48)
                sp.wait_ge(w_lo, NSPLIT * (layer + 1))
                sp.wait_ge(pe_setup, (2, 5)[layer])

            def front(u, layer):
                sp.dma_start(x_in, x_tiles[u] if layer == 0 else mid_tiles[u - NT]).then_inc(x_loaded, 16)

            def spread_keys(u, c):
                waits = [(qk_hi, upto(u, 4, c + 1)), (qk_lo, upto(u, 4, c + 1))]
                waits.append((sem_zero, NZERO) if first(u) else (pe_s, upto(u, 2 * G, 0)))
                wait_apart(sp, sp_passed, *waits)
                for r in range(0, P, HD):
                    sp.dma_start(kb[r:r + HD, c, :, r // HD % NJ, :].bitcast(F32),
                                 kflat[r:r + HD, c, :, :].bitcast(F32)).then_inc(kb_in, 16)

            def step(u, layer, attn, ffn, nxt):
                v = u - 1
                if attn and layer == 0:
                    if not first(u):
                        wait_apart(sp, sp_passed, (x1_added, upto(u, G, 0)))
                    for b in range(2):
                        sp.dma_start(gate_bc[0][b * S:(b + 1) * S, :, :],
                                     gate_tiles[0][u, b].partition_broadcast(S)).then_inc(gate1_in, 16)
                if ffn and layer == 0:
                    if not first(v):
                        wait_apart(sp, sp_passed, (f2_added, upto(v, 2, 0)))
                    for b in range(2):
                        sp.dma_start(gate_bc[1][b * S:(b + 1) * S, :, :],
                                     gate_tiles[1][v, b].partition_broadcast(S)).then_inc(gate2_in, 16)
                if attn and layer == 1:
                    wait_apart(sp, sp_passed, (pe_s, upto(u, 2 * G, 0)))
                    sp.dma_start(mrow[:, :].bitcast(F32), mask_tiles[u - NT].partition_broadcast(P))\
                      .then_inc(mrow_in, 16)
                    for i in range(2 * KC):
                        waits = [(rot_ready, upto(u - NT, 4, i + 1))]
                        if not (known(u) and u == NT and i < 2):
                            waits.append((rot_sum, upto(u - NT, 4, i - 1)))
                        wait_apart(sp, sp_passed, *waits)
                        for e in range(2):
                            sp.dma_start(rot_s[e:P:2, i % 2, :], rot_t[1 - e:P:2, i % 2, :])\
                              .then_inc(swapped[i % 2], 16)
                        if i >= 2:
                            spread_keys(u, i - 2)
                if attn and layer == 0:
                    for c in range(KC):
                        spread_keys(u, c)
                if nxt:
                    wait_apart(sp, sp_passed, (xn_ready, upto(u, G, G)), (xres_ready, upto(u, 1, 1)))
                    front(u + 1, layer)
                if ffn:
                    wait_apart(sp, sp_passed, (f2_done[layer], upto(v, 2, 2)))
                    sp.dma_start(mid_tiles[v] if layer == 0 else out_tiles[v - NT], x1m).then_inc(x_stored, 16)

            for layer in range(2):
                layer_steps(sp, layer, setup, front, step)
            sp.wait_ge(x_stored, 16 * 2 * NT)

        @block.gpsimd
        def _(pool):
            pool.memset(ident[:, :], 0.0).then_inc(sem_ident, 1)
            pool.wait_ge(sem_ident, 1)
            pool.affine_select(out=ident[:, :], in_=ident[:, :], compare_op=ALU.not_equal, fill=1.0, base=0,
                               pattern=[[-1, P]], channel_multiplier=1).then_inc(sem_ident, 1)
            pool.memset(minus_half[:, :], -0.5).then_inc(sem_ident, 1)
            pool.wait_ge(sem_ident, 3)

            def setup(layer):
                pass

            def first_rstd(u):
                pool.wait_ge(ln1_chain, upto(u, 9, 9))
                pool.tensor_tensor(rs1[:, :], rs1[:, :], minus_half[:, :], ALU.pow).then_inc(ln1_rstd, 1)

            def second_rstd(u, g):
                pool.wait_ge(ln2_chain, upto(u, 3 * G, 3 * g + 3))
                pool.tensor_tensor(rs2[:, g:g + 1], rs2[:, g:g + 1], minus_half[:, g:g + 1], ALU.pow)\
                    .then_inc(ln2_rstd, 1)

            def low_part(u, c, hi_sem, dst, done):
                pool.wait_ge(hi_sem, upto(u, KC, c + 1))
                pool.tensor_tensor(dst[1][:, c, :], aff[:, c, :], dst[0][:, c, :].bitcast(F32), ALU.subtract)\
                    .then_inc(done, 1)

            def front(u, layer, c=None):
                if c is None:
                    first_rstd(u)
                for c in range(KC) if c is None else (c,):
                    low_part(u, c, y_hi, yb, y_lo)

            def biased(dst, src, gate, bias, chain, done, count):
                bc = bias[:, :].rearrange("p (o d) -> p o d", o=1).to_broadcast([P, G, D])
                if gate is not None:
                    pool.tensor_tensor(dst, gate, bc, ALU.mult).then_inc(chain, 1)
                    pool.wait_ge(chain, count)
                    pool.tensor_tensor(dst, dst, src, ALU.add).then_inc(done, 1)
                else:
                    pool.tensor_tensor(dst, src, bc, ALU.add).then_inc(done, 1)

            def sine(u, i):
                pool.wait_ge(swapped[i % 2], upto(u - NT, 64, 32 * (i // 2) + 32))
                part = rot_s[:, i % 2, :].rearrange("p (b s) -> p b s", b=TB)
                pool.tensor_tensor(part, part, rtab[:, 1:2, :].to_broadcast([P, TB, S]), ALU.mult)\
                    .then_inc(rot_sin, 1)

            def hidden_low(v, m):
                if not (first(v) and m < 2):
                    pool.wait_ge(pe_f2, upto(v, MC, max(m - 1, 0)))
                pool.wait_ge(h_hi, upto(v, MC, m + 1))
                pool.tensor_tensor(hb[1][:, m % 2, :], hact[:, m % 2, :], hb[0][:, m % 2, :].bitcast(F32),
                                   ALU.subtract).then_inc(h_lo, 1)

            def step(u, layer, attn, ffn, nxt):
                v = u - 1
                if ffn:
                    low_part(v, 0, z_hi, zb, z_lo)
                if attn and layer == 1:
                    for i in range(KC):
                        sine(u, i)
                if ffn:
                    low_part(v, 1, z_hi, zb, z_lo)
                if attn and layer == 1:
                    for i in range(KC, 2 * KC):
                        sine(u, i)
                    pool.wait_ge(pe_pv, upto(u, 2 * G, 0))
                    if known(u) and u == NT:
                        pool.wait_ge(dve_setup, SET_MASKT)
                    pool.wait_ge(rot_sin, upto(u - NT, 4, 2 * KC))
                    for h in range(2):
                        r = slice(h * S, (h + 1) * S)
                        dst = vb[0][r, :, :].rearrange("p b (n e) -> p b n e", e=2 * VB)[:, :, :, h * VB + HD]
                        src = maskT[r, bass.ds((u - NT) * TB, TB)].rearrange("p (b o) -> p b o", o=1)
                        pool.tensor_copy(dst, src.to_broadcast([S, TB, H // 2])).then_inc(v_ones, 1)
                        pool.wait_ge(v_ones, upto(u - NT, 2, h + 1))
                if ffn:
                    pool.wait_ge(x1_done[layer], upto(v, G, G))
                    pool.wait_ge(zn_ready, upto(v, G, G))
                    if not first(v):
                        pool.wait_ge(x_stored, upto(v, 16, 0))
                    if layer == 0:
                        pool.wait_ge(gate2_in, upto(v, 32, 32))
                    biased(x1m, x_res, gate_bc[1] if layer == 0 else None, b2_bc, x1m_chain, x1m_ready,
                           upto(v, 1, 1))
                if attn:
                    pool.wait_ge(x_loaded, upto(u, 16, 16))
                    if layer == 0:
                        pool.wait_ge(gate1_in, upto(u, 32, 32))
                    if ffn:
                        pool.wait_ge(x1m_ready, upto(v, 1, 1))
                    biased(x_res, x_in, gate_bc[0] if layer == 0 else None, bo_bc, xres_chain, xres_ready,
                           upto(u, 1, 1))
                if ffn:
                    for m in range(3):
                        hidden_low(v, m)
                for g in range(G):
                    if g == 0 and nxt:
                        first_rstd(u + 1)
                    if attn and g > 0:
                        second_rstd(u, g - 1)
                    if ffn:
                        hidden_low(v, 3 + g)
                    if nxt and g >= G - KC:
                        front(u + 1, layer, g - (G - KC))
                if ffn:
                    hidden_low(v, MC - 1)
                if attn:
                    second_rstd(u, G - 1)

            for layer in range(2):
                layer_steps(pool, layer, setup, front, step)

        @block.scalar
        def _(act):
            def setup(layer):
                loads_in(act, layer)
                for n in range(NSPLIT):
                    s = slice(n * SPLIT, (n + 1) * SPLIT)
                    nc.scalar.copy(wgt[0][:, s], w_raw[:, s]).then_inc(w_hi, 1)
                if layer == 0:
                    act.wait_ge(pe_setup, 2)
                    nc.scalar.activation(hact[:, 1, :], C[:, :], ACT.Tanh).then_inc(act_setup, 1)

            def modulate(u, n, c, turned, done):
                act.wait_ge(mod_ready[n], upto(u, 1, 1))
                act.wait_ge(turned, upto(u, KC, c + 1))
                for b in range(TB):
                    s = slice(b * S, (b + 1) * S)
                    ins = nc.scalar.activation(aff[:, c, s], E[:, s], ACT.Identity, bias=mod_tile[:, n, c, 1, b:b + 1],
                                               scale=mod_tile[:, n, c, 0, b:b + 1])
                ins.then_inc(done, 1)

            def front(u, layer, c=None):
                for c in range(KC) if c is None else (c,):
                    if c == 0 and not (known(u) and u % NT < 2):
                        act.wait_ge(z_lo, upto(u - 2, KC, KC))
                    if c == 0 and known(u) and u % NT == 1:
                        act.wait_ge(y_lo, upto(u, KC, 0))
                    modulate(u, 0, c, pe_yt, y_aff)
                    act.wait_ge(y_aff, upto(u, KC, c + 1))
                    if not first(u):
                        act.wait_ge(pe_v, upto(u, 2, 0))
                    nc.scalar.copy(yb[0][:, c, :], aff[:, c, :]).then_inc(y_hi, 1)

            def second_norm(v, c, attn):
                if c == 0:
                    act.wait_ge(y_lo, upto(v, KC, 2 * KC if attn else KC))
                modulate(v, 1, c, pe_zt, z_aff)
                act.wait_ge(z_aff, upto(v, KC, c + 1))
                if not first(v):
                    act.wait_ge(pe_f1, upto(v, MC, 0))
                nc.scalar.copy(zb[0][:, c, :], aff[:, c, :]).then_inc(z_hi, 1)

            def chunk(i):
                return (i % KC, i < KC)

            def before_rotation(u, i):
                c, keys = chunk(i)
                act.wait_ge(pe_qk, upto(u, 4, i + 1))
                if i >= 2:
                    act.wait_ge(qk_lo, upto(u, 4, i - 1))
                elif not (known(u) and u == NT):
                    act.wait_ge(qk_lo, upto(u, 4, 0))
                col = KC * keys + c
                nc.scalar.activation(rot_t[:, i % 2, :], (A + B)[i][:, :], ACT.Identity,
                                     bias=qk_bias[:, col:col + 1]).then_inc(rot_ready, 1)

            def high_qk(u, layer, i):
                c, keys = chunk(i)
                if layer == 0:
                    act.wait_ge(pe_qk, upto(u, 4, i + 1))
                    src = (A + B)[i]
                    bias = qk_bias[:, KC * keys + c:KC * keys + c + 1]
                else:
                    act.wait_ge(rot_sum, upto(u - NT, 4, i + 1))
                    src = rot_t[:, i % 2, :]
                    bias = None
                if keys:
                    if not first(u):
                        act.wait_ge(kb_in, upto(u, NKB, 0))
                    parts = [(slice(0, P), by_seq(kflat[:, c, 0, :]))]
                else:
                    if not first(u):
                        act.wait_ge(pe_s, upto(u, 2 * G, 0))
                    if first(u) and i == KC:
                        act.wait_ge(sem_zero, NZERO)
                    parts = [(slice(x * 64, x * 64 + 64), qb[0][x * 64:x * 64 + 64, c, :, x, :]) for x in range(NX)]
                for n, (r, dst) in enumerate(parts):
                    if bias is not None:
                        ins = nc.scalar.activation(dst, by_seq(src[r, :]), ACT.Identity, bias=bias[r, :])
                    else:
                        ins = nc.scalar.copy(dst, by_seq(src[r, :]))
                    if n == len(parts) - 1:
                        ins.then_inc(qk_hi, 1)

            def values(u):
                if first(u):
                    act.wait_ge(sem_zero, NZERO)
                else:
                    act.wait_ge(pe_pv, upto(u, 2 * G, 0))
                for pair in range(2):
                    act.wait_ge(pe_v, upto(u, 2, pair + 1))
                    for b in range(2):
                        for h in range(2):
                            dst, src = value_views(0, pair, b, h)
                            nc.scalar.copy(dst, src).then_inc(v_hi, 1)

            def hidden(v, m):
                act.wait_ge(pe_f1, upto(v, MC, m + 1))
                if not (first(v) and m < 2):
                    act.wait_ge(h_lo, upto(v, MC, max(m - 1, 0)))
                nc.scalar.activation(hact[:, m % 2, :], C[:, :], ACT.Gelu, bias=b1_col[:, m:m + 1])\
                    .then_inc(gelu, 1)
                act.wait_ge(gelu, upto(v, MC, m + 1))
                if not (first(v) and m < 2):
                    act.wait_ge(pe_f2, upto(v, MC, max(m - 1, 0)))
                nc.scalar.copy(hb[0][:, m % 2, :], hact[:, m % 2, :]).then_inc(h_hi, 1)

            def exponentials(u, g):
                for b in range(2):
                    act.wait_ge(s_sub, upto(u, 2 * G, 2 * g + b + 1))
                    nc.scalar.activation(exps[:, b, :], exps[:, b, :], ACT.Exp, scale=SCORE_SCALE)\
                        .then_inc(s_exp, 1)

            def high_probs(u, g):
                for b in range(2):
                    act.wait_ge(pe_pt, upto(u, 2 * G, 2 * g + b + 1))
                    if not (first(u) and g == 0):
                        act.wait_ge(pe_pv, upto(u, 2 * G, max(2 * (g - 1) + b + 1, 0)))
                    nc.scalar.copy(pt[0][:, b, :], B[b][:, :]).then_inc(pt_hi, 1)

            def high_heads(u, g):
                act.wait_ge(pe_ot, upto(u, G, g + 1))
                if not (first(u) and g == 0):
                    act.wait_ge(pe_proj, upto(u, G, g))
                for x in range(NX):
                    nc.scalar.activation(ot[0][:, x, :].rearrange("p (b q) -> p b q", b=2), head_rows(x), ACT.Identity,
                                         bias=v_bias[:, x:x + 1]).then_inc(ot_hi, 1)

            def step(u, layer, attn, ffn, nxt):
                v = u - 1
                if attn and layer == 0:
                    high_qk(u, layer, 0)
                    high_qk(u, layer, 1)
                if attn and layer == 1:
                    before_rotation(u, 0)
                    before_rotation(u, 1)
                if ffn:
                    second_norm(v, 0, attn)
                if attn and layer == 0:
                    high_qk(u, layer, 2)
                if attn and layer == 1:
                    high_qk(u, layer, 0)
                    before_rotation(u, 2)
                if ffn:
                    second_norm(v, 1, attn)
                if attn and layer == 0:
                    high_qk(u, layer, 3)
                if attn and layer == 1:
                    high_qk(u, layer, 1)
                    before_rotation(u, 3)
                    high_qk(u, layer, 2)
                    high_qk(u, layer, 3)
                if attn:
                    values(u)
                if ffn:
                    hidden(v, 0)
                    hidden(v, 1)
                if attn:
                    exponentials(u, 0)
                if ffn:
                    hidden(v, 2)
                for g in range(G):
                    if attn:
                        high_probs(u, g)
                    if attn and g > 0:
                        high_heads(u, g - 1)
                    if attn and g < G - 1:
                        exponentials(u, g + 1)
                    if ffn:
                        hidden(v, 3 + g)
                    if nxt and g >= G - KC:
                        front(u + 1, layer, g - (G - KC))
                if ffn:
                    hidden(v, MC - 1)
                if attn:
                    high_heads(u, G - 1)

            for layer in range(2):
                layer_steps(act, layer, setup, front, step)

        @block.tensor
        def _(pe):
            def product(dst, pairs, first_start=True, last_stop=True, **kw):
                todo = [(l[p], r[q]) for l, r in pairs for p, q in PASSES]
                for n, (l, r) in enumerate(todo):
                    ins = nc.tensor.matmul(dst, l, r, start=first_start and n == 0,
                                           stop=last_stop and n == len(todo) - 1, **kw)
                return ins

            def w(base, width, k, lo, n):
                return [w_slice(p, base, width, k, lo, n) for p in range(2)]

            def setup(layer):
                if layer == 0:
                    pe.wait_ge(sem_ident, 2)
                loads_in(pe, layer)
                for k in range(KC):
                    ins = nc.tensor.transpose(E[:, k * P:(k + 1) * P], cond_sb[:, k * P:(k + 1) * P], ident[:, :])
                ins.then_inc(pe_setup, 1)
                pe.wait_ge(dve_setup, (SET_CONDT, SET_CONDT1)[layer])
                if layer == 1:
                    nc.tensor.transpose(E[:, 0:P], mask01[:, :, :].rearrange("p a s -> p (a s)"), ident[:, :])\
                        .then_inc(pe_setup, 1)
                for n in range(2):
                    for k in range(2):
                        for c in range(KC):
                            dst = Dk[n][:, (2 * k + c) * P:(2 * k + c + 1) * P]
                            for q in range(KC):
                                ins = nc.tensor.matmul(dst, mod_raw[2 * n + k][:, q, c * P:(c + 1) * P], condT[:, q, :],
                                                       start=(q == 0), stop=(q == KC - 1))
                if layer == 0:
                    pe.wait_ge(sem_zero, NZERO)
                    for n in range(2):
                        dst = C[:, n * D:(n + 1) * D]
                        for q in range(KC):
                            nc.tensor.matmul(dst, condT[:, q, :], mod_raw[4 + n][:, q, :], start=(q == 0), stop=False)
                        ins = nc.tensor.matmul(dst, ones[:, :], gate_row[:, n, :], start=False, stop=True)
                ins.then_inc(pe_setup, 1)
                pe.wait_ge(w_hi, NSPLIT * (layer + 1))
                pe.wait_ge(w_lo, NSPLIT * (layer + 1))
                pe.wait_ge(dve_setup, (SET_MOD0, SET_MASKT)[layer])

            def front(u, layer, c=None):
                for c in range(KC) if c is None else (c,):
                    pe.wait_ge(xn_ready, upto(u, G, G))
                    if c == 1:
                        pe.wait_ge(y_aff, upto(u, KC, 1))
                    if not (known(u) and u % NT == 0):
                        pe.wait_ge(proj_read, upto(u - 1, G, G - KC + c))
                    for g in range(G):
                        ins = nc.tensor.transpose(E[:, g * P:(g + 1) * P], xn[:, g, c * P:(c + 1) * P], ident[:, :])
                    ins.then_inc(pe_yt, 1)

            def second_norm(v, c, attn):
                pe.wait_ge(zn_ready, upto(v, G, G))
                if c == 0:
                    pe.wait_ge(proj_read, upto(v, G, G))
                    if attn:
                        pe.wait_ge(y_aff, upto(v + 1, KC, KC))
                else:
                    pe.wait_ge(z_aff, upto(v, KC, 1))
                for g in range(G):
                    ins = nc.tensor.transpose(E[:, g * P:(g + 1) * P], zn[:, g, c * P:(c + 1) * P], ident[:, :])
                ins.then_inc(pe_zt, 1)

            def queries_keys(u, i):
                c, keys = i % KC, i < KC
                if i == 0:
                    pe.wait_ge(y_hi, upto(u, KC, KC))
                    pe.wait_ge(y_lo, upto(u, KC, KC))
                if not first(u):
                    if i < 2:
                        pe.wait_ge(s_sub, upto(u, 2 * G, 0))
                    else:
                        pe.wait_ge(pv_norm, upto(u, 2 * G, 0))
                product((A + B)[i][:, :], [(w(W_QKV, 3 * D, k, D * keys + c * P, P), [yb[q][:, k, :] for q in range(2)])
                                           for k in range(KC)]).then_inc(pe_qk, 1)

            def chunk_taken(u, layer, i):
                if layer == 0:
                    pe.wait_ge(qk_lo, upto(u, 4, i + 1))
                else:
                    pe.wait_ge(rot_ready, upto(u - NT, 4, i + 1))

            def values(u, layer, pair):
                chunk_taken(u, layer, pair)
                for g in (2 * pair, 2 * pair + 1):
                    ins = product(A[pair][:, (g % 2) * D:(g % 2 + 1) * D],
                                  [([yb[p][:, k, g * P:(g + 1) * P] for p in range(2)], w(W_QKV, 3 * D, k, 2 * D, D))
                                   for k in range(KC)])
                ins.then_inc(pe_v, 1)

            def scores(u, layer, g):
                if g == 0:
                    pe.wait_ge(qk_hi, upto(u, 4, 4))
                    pe.wait_ge(qk_lo, upto(u, 4, 4))
                    pe.wait_ge(kb_in, upto(u, NKB, NKB))
                    pe.wait_ge(v_hi, upto(u, 8, 8))
                    pe.wait_ge(v_lo, upto(u, 8, 8))
                    if layer == 1:
                        pe.wait_ge(mrow_in, upto(u - NT, 16, 16))
                for b in range(2):
                    if g > 0:
                        pe.wait_ge(s_sub, upto(u, 2 * G, 2 * g + b - 1))
                    s = slice((2 * g + b) * S, (2 * g + b + 1) * S)
                    for c in range(KC):
                        dst = A[b][:, c * 256:(c + 1) * 256]
                        ins = product(dst, [([qb[p][:, c, 2 * g + b, :, :].rearrange("p x s -> p (x s)") for p in range(2)],
                                             [kb[:, c, q, :, s] for q in range(2)])], last_stop=(layer == 0))
                        if layer == 1:
                            row = mrow[:, s].rearrange("p (o s) -> p o s", o=1).to_broadcast([P, NJ, S])
                            ins = nc.tensor.matmul(dst, mean_w[:, :], row, start=False, stop=True)
                    ins.then_inc(pe_s, 1)

            def turn_probs(u, layer, g):
                for b in range(2):
                    if g == 0:
                        chunk_taken(u, layer, 2 + b)
                    else:
                        pe.wait_ge(pv_norm, upto(u, 2 * G, 2 * g + b - 1))
                    pe.wait_ge(s_exp, upto(u, 2 * G, 2 * g + b + 1))
                    for n in range(4):
                        ins = nc.tensor.transpose(B[b][:, n * P:(n + 1) * P], exps[:, b, n * P:(n + 1) * P], ident[:, :])
                    ins.then_inc(pe_pt, 1)

            def weigh_values(u, layer, g):
                if layer == 1 and g == 0:
                    pe.wait_ge(v_ones, upto(u - NT, 2, 2))
                for b in range(2):
                    pe.wait_ge(pt_lo, upto(u, 2 * G, 2 * g + b + 1))
                    for c in range(KC):
                        for jp in range(2):
                            n = 2 * c + jp
                            moving = [vb[q][:, 2 * g + b, c * 136:(c + 1) * 136].rearrange("p (x e) -> p x e", x=NX)[
                                :, :, jp * 34:(jp + 1) * 34] for q in range(2)]
                            ins = product(B[b][:, n * 68:(n + 1) * 68],
                                          [([pt[p][:, b, n * P:(n + 1) * P] for p in range(2)], moving)])
                    ins.then_inc(pe_pv, 1)

            def turn_heads(u, g, ffn, nxt):
                if g == 0:
                    pe.wait_ge(y_aff, upto(u, KC, KC))
                    if ffn:
                        pe.wait_ge(z_aff, upto(u - 1, KC, KC))
                else:
                    pe.wait_ge(proj_read, upto(u, G, g))
                    if g >= G - KC and nxt:
                        pe.wait_ge(y_aff, upto(u + 1, KC, g - (G - KC) + 1))
                pe.wait_ge(pv_norm, upto(u, 2 * G, 2 * g + 2))
                for b in range(2):
                    ins = nc.tensor.transpose(E[:, b * P:(b + 1) * P], o_sb[:, b, :], ident[:, :])
                ins.then_inc(pe_ot, 1)

            def project(u, g):
                pe.wait_ge(ot_hi, upto(u, 8, 2 * g + 2))
                pe.wait_ge(ot_lo, upto(u, 8, 2 * g + 2))
                product(E[:, D:2 * D], [([ot[p][:, x, :] for p in range(2)], w(W_PROJ, D, x, 0, D)) for x in range(NX)])\
                    .then_inc(pe_proj, 1)

            def hidden(v, m):
                if m == 0:
                    pe.wait_ge(z_hi, upto(v, KC, KC))
                    pe.wait_ge(z_lo, upto(v, KC, KC))
                if not (first(v) and m == 0):
                    pe.wait_ge(gelu, upto(v, MC, m))
                product(C[:, :], [(w(W_FF1, FF, k, m * P, P), [zb[q][:, k, :] for q in range(2)]) for k in range(KC)])\
                    .then_inc(pe_f1, 1)

            def back(v, m):
                pe.wait_ge(h_lo, upto(v, MC, m + 1))
                if m == 0 and not first(v):
                    pe.wait_ge(f2_read, upto(v, 2, 0))
                for g in range(G):
                    ins = product(Dk[g // 2][:, (g % 2) * D:(g % 2 + 1) * D],
                                  [([hb[p][:, m % 2, g * P:(g + 1) * P] for p in range(2)], w(W_FF2, D, m, 0, D))],
                                  first_start=(m == 0 and g % 2 == 0), last_stop=(m == MC - 1), skip_group_check=True)
                ins.then_inc(pe_f2, 1)

            def step(u, layer, attn, ffn, nxt):
                v = u - 1
                if attn:
                    queries_keys(u, 0)
                    queries_keys(u, 1)
                if ffn:
                    second_norm(v, 0, attn)
                if attn:
                    queries_keys(u, 2)
                if ffn:
                    second_norm(v, 1, attn)
                if attn:
                    queries_keys(u, 3)
                    values(u, layer, 0)
                    values(u, layer, 1)
                if ffn:
                    hidden(v, 0)
                if attn:
                    scores(u, layer, 0)
                if ffn:
                    hidden(v, 1)
                    back(v, 0)
                    hidden(v, 2)
                    back(v, 1)
                for g in range(G):
                    if attn:
                        turn_probs(u, layer, g)
                    if attn and 0 < g < G - 1:
                        turn_heads(u, g - 1, ffn, nxt)
                    if attn and g < G - 1:
                        scores(u, layer, g + 1)
                    if ffn and g == G - 1:
                        hidden(v, 3 + g)
                    if attn and g == G - 1:
                        turn_heads(u, g - 1, ffn, nxt)
                    if attn:
                        weigh_values(u, layer, g)
                    if attn and g > 0:
                        project(u, g - 1)
                    if ffn and g < G - 1:
                        hidden(v, 3 + g)
                    if nxt and g == G - 2:
                        front(u + 1, layer, 0)
                    if ffn:
                        back(v, 2 + g)
                if nxt:
                    front(u + 1, layer, 1)
                if ffn:
                    hidden(v, MC - 1)
                    back(v, MC - 2)
                if attn:
                    turn_heads(u, G - 1, ffn, nxt)
                if ffn:
                    back(v, MC - 1)
                if attn:
                    project(u, G - 1)

            for layer in range(2):
                layer_steps(pe, layer, setup, front, step)

        @block.vector
        def _(dve):
            for buf in (qb[0], qb[1], kb, vb[0], vb[1]):
                nc.vector.memset(buf[...].bitcast(F32), 0.0).then_inc(sem_zero, 1)
            dve.wait_ge(sem_zero, 5)
            for h in range(2):
                dst = vb[0][h * S:(h + 1) * S, :, :].rearrange("p b (n e) -> p b n e", e=2 * VB)[:, :, :, h * VB + HD]
                nc.vector.memset(dst.bitcast(F32), 1.0).then_inc(sem_zero, 1)
            nc.vector.memset(mean_w[:, :].bitcast(F32), 1.0 / P).then_inc(sem_zero, 1)
            nc.vector.memset(ones[:, :], 1.0).then_inc(sem_zero, 1)

            def modulations(at):
                n_done = at
                for n in range(2):
                    for c in range(KC):
                        s_psum, t_psum = Dk[n][:, c * P:(c + 1) * P], Dk[n][:, (2 + c) * P:(3 + c) * P]
                        scale, shift = mod[:, n, c, 0, :], mod[:, n, c, 1, :]
                        nc.vector.tensor_scalar(scale, s_psum, mod_col[:, n, 0, c:c + 1], 1.0, ALU.add, ALU.add)\
                            .then_inc(dve_setup, 1)
                        nc.vector.tensor_scalar(shift, t_psum, mod_col[:, n, 1, c:c + 1], None, ALU.add)\
                            .then_inc(dve_setup, 1)
                        dve.wait_ge(dve_setup, n_done + 2)
                        nc.vector.scalar_tensor_tensor(out=shift, in0=scale, scalar=ln_col[:, n, 1, c:c + 1], in1=shift,
                                                       op0=ALU.mult, op1=ALU.add).then_inc(dve_setup, 1)
                        nc.vector.tensor_scalar(scale, scale, ln_col[:, n, 0, c:c + 1], None, ALU.mult)\
                            .then_inc(dve_setup, 1)
                        n_done += 4
                dve.wait_ge(dve_setup, n_done)

            def setup(layer):
                loads_in(dve, layer)
                if layer == 1:
                    nc.vector.tensor_scalar(mask_add, mask_u8[:, :], BIG, -BIG, ALU.mult, ALU.add)\
                        .then_inc(dve_setup, 1)
                    for n in range(2):
                        nc.vector.tensor_copy(mask01[:, n, :], mask_u8[:, :]).then_inc(dve_setup, 1)
                for n in range(NSPLIT):
                    s = slice(n * SPLIT, (n + 1) * SPLIT)
                    dve.wait_ge(w_hi, NSPLIT * layer + n + 1)
                    nc.vector.tensor_tensor(wgt[1][:, s], w_raw[:, s], wgt[0][:, s].bitcast(F32), ALU.subtract)\
                        .then_inc(w_lo, 1)
                dve.wait_ge(pe_setup, (1, 3)[layer])
                nc.vector.tensor_copy(condT, E[:, 0:KC * P].rearrange("p (k b) -> p k b", k=KC)).then_inc(dve_setup, 1)
                if layer == 0:
                    dve.wait_ge(pe_setup, 2)
                    modulations(SET_CONDT)
                    dve.wait_ge(act_setup, 1)
                    nc.vector.tensor_scalar(hact[:, 1, :], hact[:, 1, :], GATE, None, ALU.mult).then_inc(dve_setup, 1)
                else:
                    dve.wait_ge(pe_setup, 5)
                    modulations(SET_CONDT1)
                    nc.vector.tensor_copy(maskT[:, :], E[:, 0:P]).then_inc(dve_setup, 1)

            def normalise(dst, src, mean, rstd):
                return nc.vector.tensor_scalar(dst, src, mean, rstd, ALU.subtract, ALU.mult)

            def first_statistics(u):
                dve.wait_ge(x_loaded, upto(u, 16, 16))
                for g in range(G):
                    nc.vector.bn_stats(st1[:, g, :], x_in[:, g, :]).then_inc(ln1_chain, 1)
                wait_apart(dve, dve_passed, (ln1_chain, upto(u, 9, 4)))
                for g in range(G):
                    nc.vector.bn_aggr(mv1[:, g, :], st1[:, g, :]).then_inc(ln1_chain, 1)
                dve.wait_ge(ln1_chain, upto(u, 9, 8))
                nc.vector.tensor_scalar(rs1[:, :], mv1[:, :, 1], EPS, None, ALU.add).then_inc(ln1_chain, 1)

            def first_norm(u):
                dve.wait_ge(ln1_rstd, upto(u, 1, 1))
                if not first(u):
                    dve.wait_ge(pe_yt, upto(u, KC, 0))
                for g in range(G):
                    normalise(xn[:, g, :], x_in[:, g, :], mv1[:, g, 0:1], rs1[:, g:g + 1]).then_inc(xn_ready, 1)

            def tile_modulation(u, layer, n, done):
                if not first(u):
                    dve.wait_ge(done, upto(u, KC, 0))
                nc.vector.tensor_copy(mod_tile[:, n, :, :, :],
                                      mod[:, n, :, :, bass.ds((u - layer * NT) * TB, TB)]).then_inc(mod_ready[n], 1)

            def front(u, layer):
                tile_modulation(u, layer, 0, y_aff)
                first_statistics(u)
                first_norm(u)

            def low_qk(u, layer, i):
                c, keys = i % KC, i < KC
                col = KC * keys + c
                dve.wait_ge(qk_hi, upto(u, 4, i + 1))
                rows = [slice(0, P)] if keys else [slice(0, 64), slice(64, 128)]
                for x, r in enumerate(rows):
                    hi = by_seq(kflat[:, c, 0, :]) if keys else qb[0][r, c, :, x, :]
                    lo = by_seq(kflat[:, c, 1, :]) if keys else qb[1][r, c, :, x, :]
                    if layer == 0:
                        ins = nc.vector.scalar_tensor_tensor(out=lo, in0=by_seq((A + B)[i][r, :]), scalar=qk_bias[r, col:col + 1],
                                                             in1=hi.bitcast(F32), op0=ALU.add, op1=ALU.subtract)
                    else:
                        ins = nc.vector.tensor_tensor(lo, by_seq(rot_t[r, i % 2, :]), hi.bitcast(F32), ALU.subtract)
                ins.then_inc(qk_lo, 1)

            def cosine(u, i):
                dve.wait_ge(swapped[i % 2], upto(u - NT, 64, 32 * (i // 2) + 32))
                part = rot_t[:, i % 2, :].rearrange("p (b s) -> p b s", b=TB)
                nc.vector.tensor_tensor(part, part, rtab[:, 0:1, :].to_broadcast([P, TB, S]), ALU.mult)\
                    .then_inc(rot_cos, 1)

            def rotated(u, i):
                dve.wait_ge(rot_cos, upto(u - NT, 4, i + 1))
                dve.wait_ge(rot_sin, upto(u - NT, 4, i + 1))
                nc.vector.tensor_tensor(rot_t[:, i % 2, :], rot_t[:, i % 2, :], rot_s[:, i % 2, :], ALU.add)\
                    .then_inc(rot_sum, 1)

            def low_values(u):
                for pair in range(2):
                    dve.wait_ge(v_hi, upto(u, 8, 4 * pair + 4))
                    for b in range(2):
                        for h in range(2):
                            hi, src = value_views(0, pair, b, h)
                            lo, _ = value_views(1, pair, b, h)
                            nc.vector.tensor_tensor(lo, src, hi.bitcast(F32), ALU.subtract).then_inc(v_lo, 1)

            def subtract_max(u, g):
                for b in range(2):
                    dve.wait_ge(pe_s, upto(u, 2 * G, 2 * g + b + 1))
                    s = A[b][:, :].rearrange("p (h k) -> p h k", k=S)
                    nc.vector.tensor_reduce(mx[:, b, :], s, AX.X, ALU.max).then_inc(s_max, 1)
                    dve.wait_ge(s_max, upto(u, 2 * G, 2 * g + b + 1))
                    if not (first(u) and g == 0):
                        dve.wait_ge(pe_pt, upto(u, 2 * G, max(2 * (g - 1) + b + 1, 0)))
                    nc.vector.tensor_tensor(exps[:, b, :].rearrange("p (h k) -> p h k", k=S), s,
                                            mx[:, b, :].rearrange("p (h o) -> p h o", o=1).to_broadcast([P, 8, S]),
                                            ALU.subtract).then_inc(s_sub, 1)

            def low_probs(u, g):
                for b in range(2):
                    dve.wait_ge(pt_hi, upto(u, 2 * G, 2 * g + b + 1))
                    nc.vector.tensor_tensor(pt[1][:, b, :], B[b][:, :], pt[0][:, b, :].bitcast(F32), ALU.subtract)\
                        .then_inc(pt_lo, 1)

            def normalise_heads(u, g):
                if not (first(u) and g == 0):
                    dve.wait_ge(pe_ot, upto(u, G, g))
                for b in range(2):
                    dve.wait_ge(pe_pv, upto(u, 2 * G, 2 * g + b + 1))
                    sums = B[b][:, 0:4 * 68].rearrange("p (n x j e) -> p n x j e", n=4, x=NX, e=VB)
                    r = rden[:, b, :].rearrange("p (n j) -> p n j", n=4)
                    nc.vector.reciprocal(r, sums[:, :, 0, :, HD]).then_inc(pv_rden, 1)
                    dve.wait_ge(pv_rden, upto(u, 2 * G, 2 * g + b + 1))
                    for x in range(NX):
                        p = slice(x * 64, x * 64 + 64)
                        ins = nc.vector.tensor_tensor(
                            o_sb[p, b, :].rearrange("p (n j d) -> p n j d", n=4, j=2), sums[p, :, x, :, 0:HD],
                            rden[p, b, :].rearrange("p (n j o) -> p n j o", n=4, o=1).to_broadcast([64, 4, 2, HD]),
                            ALU.mult)
                    ins.then_inc(pv_norm, 1)

            def low_heads(u, g):
                dve.wait_ge(ot_hi, upto(u, 8, 2 * g + 2))
                for x in range(NX):
                    as_rows = [ot[p][:, x, :].rearrange("p (b q) -> p b q", b=2) for p in range(2)]
                    nc.vector.scalar_tensor_tensor(out=as_rows[1], in0=head_rows(x), scalar=v_bias[:, x:x + 1],
                                                   in1=as_rows[0].bitcast(F32), op0=ALU.add, op1=ALU.subtract)\
                        .then_inc(ot_lo, 1)

            def residual(u, layer, g):
                dve.wait_ge(pe_proj, upto(u, G, g + 1))
                if g == 0:
                    dve.wait_ge(xres_ready, upto(u, 1, 1))
                if layer == 0:
                    gate = gate_bc[0][:, g, :]
                    nc.vector.tensor_tensor(gate, E[:, D:2 * D], gate, ALU.mult).then_inc(proj_read, 1)
                    dve.wait_ge(proj_read, upto(u, G, g + 1))
                    nc.vector.tensor_tensor(x_res[:, g, :], gate, x_res[:, g, :], ALU.add).then_inc(x1_added, 1)
                else:
                    nc.vector.tensor_tensor(x_res[:, g, :], E[:, D:2 * D], x_res[:, g, :], ALU.add)\
                        .then_inc(proj_read, 1)
                dve.wait_ge(x1_done[layer], upto(u, G, g + 1))
                nc.vector.bn_stats(st2[:, g, :], x_res[:, g, :]).then_inc(ln2_chain, 1)
                wait_apart(dve, dve_passed, (ln2_chain, upto(u, 3 * G, 3 * g + 1)))
                nc.vector.bn_aggr(mv2[:, g, :], st2[:, g, :]).then_inc(ln2_chain, 1)
                dve.wait_ge(ln2_chain, upto(u, 3 * G, 3 * g + 2))
                nc.vector.tensor_scalar(rs2[:, g:g + 1], mv2[:, g, 1:2], EPS, None, ALU.add).then_inc(ln2_chain, 1)

            def second_normalise(u, g, ffn):
                dve.wait_ge(ln2_rstd, upto(u, G, g + 1))
                if g == 0 and ffn:
                    dve.wait_ge(pe_zt, upto(u, KC, 0))
                normalise(zn[:, g, :], x_res[:, g, :], mv2[:, g, 0:1], rs2[:, g:g + 1]).then_inc(zn_ready, 1)

            def layer_output(v, layer):
                dve.wait_ge(pe_f2, upto(v, MC, MC))
                dve.wait_ge(x1m_ready, upto(v, 1, 1))
                for h in range(2):
                    acc = Dk[h][:, :].rearrange("p (g d) -> p g d", g=2)
                    x = x1m[:, 2 * h:2 * h + 2, :]
                    if layer == 0:
                        gate = gate_bc[1][:, 2 * h:2 * h + 2, :]
                        nc.vector.tensor_tensor(gate, acc, gate, ALU.mult).then_inc(f2_read, 1)
                        dve.wait_ge(f2_read, upto(v, 2, h + 1))
                        nc.vector.tensor_tensor(x, gate, x, ALU.add).then_inc(f2_added, 1)
                    else:
                        nc.vector.tensor_tensor(x, acc, x, ALU.add).then_inc(f2_read, 1)

            def step(u, layer, attn, ffn, nxt):
                v = u - 1
                if ffn:
                    tile_modulation(v, layer, 1, z_aff)
                if attn and layer == 0:
                    for i in range(2 * KC):
                        low_qk(u, layer, i)
                if attn and layer == 1:
                    cosine(u, 0)
                    cosine(u, 1)
                    rotated(u, 0)
                    low_qk(u, layer, 0)
                    cosine(u, 2)
                    rotated(u, 1)
                    low_qk(u, layer, 1)
                    cosine(u, 3)
                    rotated(u, 2)
                    low_qk(u, layer, 2)
                    rotated(u, 3)
                    low_qk(u, layer, 3)
                if attn:
                    low_values(u)
                    subtract_max(u, 0)
                for g in range(G):
                    if attn:
                        low_probs(u, g)
                    if attn and g > 0:
                        low_heads(u, g - 1)
                    if attn and g > 1:
                        second_normalise(u, g - 2, ffn)
                    if attn and g < G - 1:
                        subtract_max(u, g + 1)
                    if attn:
                        normalise_heads(u, g)
                    if g == 0 and nxt:
                        tile_modulation(u + 1, layer, 0, y_aff)
                        first_statistics(u + 1)
                    if attn and g > 0:
                        residual(u, layer, g - 1)
                    if g == 1 and nxt:
                        first_norm(u + 1)
                if attn:
                    second_normalise(u, G - 2, ffn)
                    low_heads(u, G - 1)
                if ffn:
                    layer_output(v, layer)
                if attn:
                    residual(u, layer, G - 1)
                    second_normalise(u, G - 1, ffn)

            for layer in range(2):
                layer_steps(dve, layer, setup, front, step)


_INS = ["x", "cond_1024", "mask_BxS_bf1"] + [
    "L0_cond_" + n for n in ("g1_w", "g1_b", "b1_w", "b1_b", "a1_w", "a1_b", "g2_w", "g2_b", "b2_w", "b2_b", "a2_w",
                             "a2_b", "ln1_g", "ln1_b", "ln2_g", "ln2_b", "qkv_w", "qkv_b", "proj_w", "proj_b", "fc1_w",
                             "fc1_b", "fc2_w", "fc2_b")] + [
    "L1_cond_" + n for n in ("wq", "bq", "wk", "bk", "wv", "bv", "wo", "bo", "ln1_g", "ln1_b", "ada1_w", "ada1_b",
                             "ln2_g", "ln2_b", "ada2_w", "ada2_b", "ff_w1", "ff_b1", "ff_w2", "ff_b2")]


def rotary_table():
    import numpy as np
    inv = np.float32(1.0) / np.float32(10000.0) ** (np.arange(ROT, dtype=np.float32) / np.float32(ROT))
    angle = np.arange(S, dtype=np.float32)[:, None] * inv[None, :].astype(np.float32)
    d = np.arange(P) % HD
    sign = np.where(d % 2 == 0, -1.0, 1.0).astype(np.float32)
    cos, sin = np.cos(angle).T[d // 2], np.sin(angle).T[d // 2] * sign[:, None]
    return np.ascontiguousarray(np.stack([cos, sin], axis=1).astype(np.float32))


def kernel(**inputs):
    import numpy as np
    import concourse.bacc as bacc
    from concourse.bass_utils import run_bass_kernel_spmd

    nc = bacc.Bacc("TRN2", target_bir_lowering=False, num_devices=1)
    arrays, tensors = {}, {}
    for name in _INS + ["rotary"]:
        a = rotary_table() if name == "rotary" else np.ascontiguousarray(inputs[name])
        if a.dtype == np.bool_:
            a = a.view(np.uint8)
        arrays[f"in_{name}"] = a
        tensors[name] = nc.dram_tensor(f"in_{name}", a.shape, mybir.dt.from_np(a.dtype), kind="ExternalInput").ap()
    out = nc.dram_tensor("out", (NB, S, D), F32, kind="ExternalOutput").ap()
    build(nc, tensors, out)
    r = run_bass_kernel_spmd(nc, [arrays], core_ids=[0])
    return r.results[0]["out"]
```

```python
from contextlib import ExitStack

import concourse.bass as bass
from concourse import mybir

F32 = mybir.dt.float32
F32R = mybir.dt.float32r
U8 = mybir.dt.uint8
ALU = mybir.AluOpType
ACT = mybir.ActivationFunctionType
AX = mybir.AxisListType

P = 128
NB, S, D = 128, 64, 256
H, HD = 16, 16
FF = 4 * D
KC = D // P
MC = FF // P
TILE = 512
G = TILE // P
TB = TILE // S
NT = NB * S // TILE
NX, NJ = 2, 4
VB = HD + 1
VROW = H * VB
EPS = 1e-5
GATE = 0.1
SCORE_SCALE = HD ** -0.5
BIG = 2.0 ** 100
ROT = HD // 2

W_QKV, W_PROJ = 0, KC * 3 * D
W_FF1 = W_PROJ + KC * D
W_FF2 = W_FF1 + KC * FF
W_ALL = W_FF2 + MC * D
PASSES = ((0, 0), (1, 0), (0, 1))


def build(nc, t, out):
    ctx = ExitStack()
    with ctx:
        def sb(name, shape, dt=F32):
            return ctx.enter_context(nc.sbuf_tensor(name, shape, dt))

        def bank(name):
            return ctx.enter_context(nc.psum_tensor(name, [P, 512], F32))

        def sem(name):
            return ctx.enter_context(nc.semaphore(name))

        x_tiles = t["x"].rearrange("b s d -> (b s) d").rearrange("(t g p) d -> t p g d", g=G, p=P)
        mid = nc.dram_tensor("mid", [NB * S, D], F32, kind="Internal").ap()
        mid_tiles = mid.rearrange("(t g p) d -> t p g d", g=G, p=P)
        out_tiles = out.rearrange("b s d -> (b s) d").rearrange("(t g p) d -> t p g d", g=G, p=P)
        gates = [nc.dram_tensor(f"gates{n}", [NB, D], F32, kind="Internal").ap() for n in range(2)]
        gate_tiles = [g.rearrange("(t g b) d -> t b g d", g=G, b=2) for g in gates]
        mask_rows = nc.dram_tensor("mask_rows", [NB, S], F32, kind="Internal").ap()
        mask_tiles = mask_rows.rearrange("(t b) s -> t (b s)", b=TB)

        wgt = [sb("wgt_hi", [P, W_ALL], F32R), sb("wgt_lo", [P, W_ALL], F32R)]
        TE = G * D
        arena = sb("arena", [P, 11 * TE])
        gated_bo = sb("gated_bo", [P, G, D])

        def view(n, k=1):
            return arena[:, n * TE:(n + k) * TE]

        def tokens(n):
            return view(n).rearrange("p (g d) -> p g d", g=G)

        x_in, xn, x_res, x1m, zn = (tokens(n) for n in range(5))
        aff = view(5).rearrange("p (c n) -> p c n", c=KC)
        exps = view(6).rearrange("p (b n) -> p b n", b=2)
        gate_bc = [tokens(7), tokens(8)]
        rot_t = view(7, 2).rearrange("p (r n) -> p r n", r=4)
        rot_s = view(9, 2).rearrange("p (r n) -> p r n", r=4)
        w_raw = view(0, 6)
        mod_raw = [view(6, 3)[:, n * KC * D:(n + 1) * KC * D].rearrange("p (k n) -> p k n", k=KC)
                   for n in range(6)]
        yb = [sb("y_hi", [P, KC, TILE], F32R), sb("y_lo", [P, KC, TILE], F32R)]
        zb = [sb("z_hi", [P, KC, TILE], F32R), sb("z_lo", [P, KC, TILE], F32R)]
        qb = [sb("q_hi", [P, KC, TB, NX, S], F32R), sb("q_lo", [P, KC, TB, NX, S], F32R)]
        kflat = sb("k_flat", [P, KC, 2, TILE], F32R)
        kb = sb("k_blocks", [P, KC, 2, NJ, TILE], F32R)
        vb = sb("v_blocks", [P, TB, VROW])
        pt = sb("probs_turned", [P, 2, 512])
        o_sb = sb("o_sb", [P, 2, P])
        ot = [sb("ot_hi", [P, NX, P], F32R), sb("ot_lo", [P, NX, P], F32R)]
        hact = sb("hact", [P, 2, TILE])
        hb = [sb("h_hi", [P, 2, TILE], F32R), sb("h_lo", [P, 2, TILE], F32R)]
        mod = sb("mod", [P, 2, KC, 2, NB])
        ident = sb("ident", [P, P])
        ones = sb("ones", [1, P])
        mod_tile = sb("mod_tile", [P, 2, KC, 2, TB])
        bo_bc = sb("bo_bc", [P, D])
        b2_bc = sb("b2_bc", [P, D])
        qk_bias = sb("qk_bias", [P, 2 * KC])
        v_bias = sb("v_bias", [P, NX])
        b1_col = sb("b1_col", [P, MC])
        ln_col = sb("ln_col", [P, 2, 2, KC])
        mod_col = sb("mod_col", [P, 2, 2, KC])
        mx = sb("mx", [P, 2, 8])
        rden = sb("rden", [P, 2, 8])
        st1 = sb("st1", [P, G, 6])
        mv1 = sb("mv1", [P, G, 2])
        rs1 = sb("rs1", [P, G])
        st2 = sb("st2", [P, G, 6])
        mv2 = sb("mv2", [P, G, 2])
        rs2 = sb("rs2", [P, G])
        minus_half = sb("minus_half", [P, G])
        rtab = sb("rtab", [P, 2, S])
        mrow = sb("mrow", [P, TILE], F32R)
        mean_w = sb("mean_w", [P, P], F32R)
        mask_u8 = sb("mask_u8", [P, S], U8)
        mask01 = view(9)[:, 0:2 * S].rearrange("p (a s) -> p a s", a=2)
        maskT = sb("maskT", [P, NB])
        cond_sb = hact[:, 0, 0:D]
        condT = hact[:, 0, D:2 * D].rearrange("p (k b) -> p k b", k=KC)
        gate_row = hact[0:1, 1, :].rearrange("p (n d) -> p n d", n=2)
        gate_rows = hact[:, 1, :].rearrange("p (n d) -> p n d", n=2)
        mask_add = hact[:, 1, 0:S]

        A = [bank("A0"), bank("A1")]
        B = [bank("B0"), bank("B1")]
        C = bank("C")
        Dk = [bank("D0"), bank("D1")]
        E = bank("E")

        sem_in = sem("setup_loaded")
        sem_ident = sem("consts_ready")
        sem_zero = sem("zeros_ready")
        w_hi, w_lo = sem("w_hi"), sem("w_lo")
        pe_setup, dve_setup, act_setup = sem("pe_setup"), sem("dve_setup"), sem("act_setup")
        gates_out = sem("gates_out")
        x_loaded, xres_loaded, x_stored = sem("x_loaded"), sem("xres_loaded"), sem("x_stored")
        gate1_in, gate2_in, mrow_in = sem("gate1_in"), sem("gate2_in"), sem("mrow_in")
        kb_in = sem("kb_in")
        swapped = [sem(f"swapped{i}") for i in range(4)]
        xn_ready, ln1_chain, ln1_rstd = sem("xn_ready"), sem("ln1_chain"), sem("ln1_rstd")
        pe_yt, y_scaled, y_aff, y_hi, y_lo = sem("pe_yt"), sem("y_scaled"), sem("y_aff"), sem("y_hi"), sem("y_lo")
        pe_qk, qk_hi, qk_lo = sem("pe_qk"), sem("qk_hi"), sem("qk_lo")
        rot_ready, rot_cos, rot_sin, rot_sum = sem("rot_ready"), sem("rot_cos"), sem("rot_sin"), sem("rot_sum")
        pe_v, v_moved, v_ones = sem("pe_v"), sem("v_moved"), sem("v_ones")
        pe_s, s_max, s_sub, s_exp = sem("pe_s"), sem("s_max"), sem("s_sub"), sem("s_exp")
        pe_pt, pt_moved = sem("pe_pt"), sem("pt_moved")
        pe_pv, pv_rden, pv_norm = sem("pe_pv"), sem("pv_rden"), sem("pv_norm")
        pe_ot, ot_hi, ot_lo = sem("pe_ot"), sem("ot_hi"), sem("ot_lo")
        pe_proj, proj_read, x1_added = sem("pe_proj"), sem("proj_read"), sem("x1_added")
        ln2_chain, zn_ready, ln2_rstd = sem("ln2_chain"), sem("zn_ready"), sem("ln2_rstd")
        xres_chain, xres_ready, x1m_chain, x1m_ready = (sem("xres_chain"), sem("xres_ready"),
                                                        sem("x1m_chain"), sem("x1m_ready"))
        pe_zt, z_scaled, z_aff, z_hi, z_lo = sem("pe_zt"), sem("z_scaled"), sem("z_aff"), sem("z_hi"), sem("z_lo")
        pe_f1, gelu, h_hi, h_lo, pe_f2 = sem("pe_f1"), sem("gelu"), sem("h_hi"), sem("h_lo"), sem("pe_f2")
        f2_read, f2_added = sem("f2_read"), sem("f2_added")
        sp_passed, dve_passed = sem("sp_passed"), sem("dve_passed")
        mod_ready = [sem("mod1_ready"), sem("mod2_ready")]
        x1_done = [x1_added, proj_read]
        f2_done = [f2_added, f2_read]

        block = ctx.enter_context(nc.Block())

        def upto(u, n, k):
            return u * n + k

        def known(u):
            return isinstance(u, int)

        def wait_apart(eng, passed, *waits):
            for semaphore, count in waits:
                eng.wait_ge(semaphore, count)
                eng.sem_inc(passed, 1)

        def w_slice(part, base, width, k, lo, n):
            return wgt[part][:, base + k * width + lo:base + k * width + lo + n]

        def by_seq(ap):
            return ap.rearrange("p (b s) -> p b s", s=S)

        def value_views(pair, b, h):
            dst = vb[h * S:(h + 1) * S, 4 * pair + b:4 * pair + b + 3:2, :].rearrange(
                "p g (n e) -> p g n e", e=2 * VB)[:, :, :, h * VB:h * VB + HD]
            src = A[pair][b * S:(b + 1) * S, :].rearrange("p (g n h d) -> p g n h d", g=2, h=2, d=HD)[:, :, :, h, :]
            return dst, src

        def head_rows(x):
            return E[:, 0:2 * P].rearrange("p (b x q) -> p b x q", b=2, x=NX)[:, :, x, :]

        def first(u):
            return known(u) and u == 0

        def layer_steps(eng, layer, setup, front, step):
            u0 = layer * NT
            setup(layer)
            front(u0, layer)
            step(u0, layer, True, False, True)
            step(u0 + 1, layer, True, True, True)
            with eng.Fori(u0 + 2, u0 + NT - 1) as u:
                step(u, layer, True, True, True)
            step(u0 + NT - 1, layer, True, True, False)
            step(u0 + NT, layer, False, True, False)

        LOADS = (29, 29)
        NZERO = 8
        NSPLIT = 4
        SPLIT = W_ALL // NSPLIT
        NMOD = 16
        SET_CONDT, SET_MOD0, SET_GATES = 1, 1 + NMOD, 2 + NMOD
        SET_MASK, SET_CONDT1 = SET_GATES + 3, SET_GATES + 4
        SET_MASKT = SET_CONDT1 + NMOD + 1
        NKB = 16 * NX * NJ

        def loads_in(eng, layer):
            eng.wait_ge(sem_in, 16 * sum(LOADS[:layer + 1]))

        @block.sync
        def _(sp):
            def setup(layer):
                if layer == 1:
                    sp.wait_ge(f2_added, 2 * NT)
                    sp.wait_ge(x_stored, 16 * NT)
                count = 0

                def ld(dst, src, **kw):
                    nonlocal count
                    sp.dma_start(dst, src, **kw).then_inc(sem_in, 16)
                    count += 1

                def rows(m):
                    return m.rearrange("(k p) n -> p k n", p=P)

                def ld_column(dst, vec, p=P):
                    ld(dst, vec.rearrange("(c p) -> p c", p=p), allow_slow_non_contiguous=True)

                def row(vec):
                    return vec.rearrange("(o n) -> o n", o=1)

                w = {k[8:]: v for k, v in t.items() if k.startswith(f"L{layer}_cond_")}
                qkv = w_raw[:, W_QKV:W_PROJ].rearrange("p (k n) -> p k n", k=KC)
                ld(cond_sb, t["cond_1024"])
                if layer == 0:
                    for n, m in enumerate(("g1", "b1", "g2", "b2", "a1", "a2")):
                        ld(mod_raw[n], rows(w[m + "_w"]))
                    for n in range(2):
                        ld(gate_row[:, n, :], row(w[f"a{n + 1}_b"]))
                    mod_bias = [[w["g1_b"], w["b1_b"]], [w["g2_b"], w["b2_b"]]]
                    ld(qkv, rows(w["qkv_w"]))
                    qbias, kbias, vbias = (w["qkv_b"][n * D:(n + 1) * D] for n in range(3))
                    proj_w, proj_b, w1, b1, w2, b2 = (w[n] for n in ("proj_w", "proj_b", "fc1_w", "fc1_b", "fc2_w",
                                                                     "fc2_b"))
                else:
                    for n in range(2):
                        for k in range(2):
                            ld(mod_raw[2 * n + k], rows(w[f"ada{n + 1}_w"][:, (1 - k) * D:(2 - k) * D]))
                    mod_bias = [[w[f"ada{n}_b"][D:2 * D], w[f"ada{n}_b"][0:D]] for n in (1, 2)]
                    for n, m in enumerate("qkv"):
                        ld(qkv[:, :, n * D:(n + 1) * D], rows(w["w" + m]))
                    qbias, kbias, vbias = w["bq"], w["bk"], w["bv"]
                    proj_w, proj_b, w1, b1, w2, b2 = (w[n] for n in ("wo", "bo", "ff_w1", "ff_b1", "ff_w2", "ff_b2"))
                    ld(mask_u8[:, :], t["mask_BxS_bf1"])
                    ld(rtab[:, :, :], t["rotary"])
                half = NJ * HD
                for c in range(KC):
                    ld(w_raw[c * half:(c + 1) * half, W_PROJ:W_FF1].rearrange("r (x n) -> r x n", x=NX),
                       proj_w[c * P:(c + 1) * P, :].rearrange("(x r) n -> r x n", x=NX))
                    ld_column(v_bias[c * half:(c + 1) * half, :], vbias[c * P:(c + 1) * P], half)
                ld(w_raw[:, W_FF1:W_FF2].rearrange("p (k n) -> p k n", k=KC), rows(w1))
                ld(w_raw[:, W_FF2:W_ALL].rearrange("p (k n) -> p k n", k=MC), rows(w2))
                ld_column(qk_bias[:, 0:KC], qbias)
                ld_column(qk_bias[:, KC:2 * KC], kbias)
                ld_column(b1_col[:, :], b1)
                ld(bo_bc[:, :], proj_b.partition_broadcast(P))
                ld(b2_bc[:, :], b2.partition_broadcast(P))
                for n in range(2):
                    for k, what in enumerate("gb"):
                        ld_column(ln_col[:, n, k, :], w[f"ln{n + 1}_{what}"])
                        ld_column(mod_col[:, n, k, :], mod_bias[n][k])
                assert count == LOADS[layer], (layer, count)
                if layer == 0:
                    sp.wait_ge(dve_setup, SET_GATES)
                    for n in range(2):
                        sp.dma_start(gates[n], gate_rows[:, n, :]).then_inc(gates_out, 16)
                    sp.wait_ge(gates_out, 32)
                else:
                    sp.wait_ge(dve_setup, SET_MASK)
                    sp.dma_start(mask_rows, mask_add).then_inc(gates_out, 16)
                    sp.wait_ge(gates_out, 48)
                sp.wait_ge(w_lo, NSPLIT * (layer + 1))
                sp.wait_ge(pe_setup, (2, 5)[layer])

            def tokens_of(u, layer):
                return x_tiles[u] if layer == 0 else mid_tiles[u - NT]

            def front(u, layer):
                sp.dma_start(x_in, tokens_of(u, layer)).then_inc(x_loaded, 16)

            def spread_keys(u):
                waits = [(qk_hi, upto(u, 4, KC)), (qk_lo, upto(u, 4, KC))]
                waits.append((sem_zero, NZERO) if first(u) else (pe_s, upto(u, 2 * G, 0)))
                wait_apart(sp, sp_passed, *waits)
                for r in range(0, P, HD):
                    sp.dma_start(kb[r:r + HD, :, :, r // HD % NJ, :].rearrange("p c q n -> p (c q) n").bitcast(F32),
                                 kflat[r:r + HD, :, :, :].rearrange("p c q n -> p (c q) n").bitcast(F32))\
                      .then_inc(kb_in, 16)

            def step(u, layer, attn, ffn, nxt):
                v = u - 1
                if nxt:
                    wait_apart(sp, sp_passed, (xn_ready, upto(u, G, G)))
                    front(u + 1, layer)
                if attn and layer == 0:
                    if not first(u):
                        wait_apart(sp, sp_passed, (x1_added, upto(u, G, 0)))
                    for b in range(2):
                        sp.dma_start(gate_bc[0][b * S:(b + 1) * S, :, :],
                                     gate_tiles[0][u, b].partition_broadcast(S)).then_inc(gate1_in, 16)
                if attn and layer == 0:
                    spread_keys(u)
                if ffn and layer == 0:
                    if not first(v):
                        wait_apart(sp, sp_passed, (f2_added, upto(v, 2, 0)))
                    for b in range(2):
                        sp.dma_start(gate_bc[1][b * S:(b + 1) * S, :, :],
                                     gate_tiles[1][v, b].partition_broadcast(S)).then_inc(gate2_in, 16)
                if attn and layer == 1:
                    wait_apart(sp, sp_passed, (pe_s, upto(u, 2 * G, 0)))
                    sp.dma_start(mrow[:, :].bitcast(F32), mask_tiles[u - NT].partition_broadcast(P))\
                      .then_inc(mrow_in, 16)
                    for i in range(2 * KC):
                        waits = [(rot_ready, upto(u - NT, 4, i + 1))]
                        if not (known(u) and u == NT):
                            waits.append((rot_sum, upto(u - NT, 4, i - 3)))
                        wait_apart(sp, sp_passed, *waits)
                        for e in range(2):
                            sp.dma_start(rot_s[e:P:2, i, :], rot_t[1 - e:P:2, i, :]).then_inc(swapped[i], 16)
                    spread_keys(u)
                if attn:
                    if ffn:
                        wait_apart(sp, sp_passed, (x1m_ready, upto(v, 1, 1)))
                    sp.dma_start(x_res, tokens_of(u, layer)).then_inc(xres_loaded, 16)
                if ffn:
                    wait_apart(sp, sp_passed, (f2_done[layer], upto(v, 2, 2)))
                    sp.dma_start(mid_tiles[v] if layer == 0 else out_tiles[v - NT], x1m).then_inc(x_stored, 16)

            for layer in range(2):
                layer_steps(sp, layer, setup, front, step)
            sp.wait_ge(x_stored, 16 * 2 * NT)

        @block.gpsimd
        def _(pool):
            pool.memset(ident[:, :], 0.0).then_inc(sem_ident, 1)
            pool.wait_ge(sem_ident, 1)
            pool.affine_select(out=ident[:, :], in_=ident[:, :], compare_op=ALU.not_equal, fill=1.0, base=0,
                               pattern=[[-1, P]], channel_multiplier=1).then_inc(sem_ident, 1)
            pool.memset(minus_half[:, :], -0.5).then_inc(sem_ident, 1)
            pool.wait_ge(sem_ident, 3)

            def setup(layer):
                pass

            def first_rstd(u):
                pool.wait_ge(ln1_chain, upto(u, 9, 9))
                pool.tensor_tensor(rs1[:, :], rs1[:, :], minus_half[:, :], ALU.pow).then_inc(ln1_rstd, 1)

            def second_rstd(u, g):
                pool.wait_ge(ln2_chain, upto(u, 3 * G, 3 * g + 3))
                pool.tensor_tensor(rs2[:, g:g + 1], rs2[:, g:g + 1], minus_half[:, g:g + 1], ALU.pow)\
                    .then_inc(ln2_rstd, 1)

            def low_part(u, c, hi_sem, dst, done):
                pool.wait_ge(hi_sem, upto(u, KC, c + 1))
                pool.tensor_tensor(dst[1][:, c, :], aff[:, c, :], dst[0][:, c, :].bitcast(F32), ALU.subtract)\
                    .then_inc(done, 1)

            def front(u, layer, c=None):
                if c is None:
                    first_rstd(u)
                for c in range(KC) if c is None else (c,):
                    low_part(u, c, y_hi, yb, y_lo)

            def bias_rows(bias):
                return bias[:, :].rearrange("p (o d) -> p o d", o=1).to_broadcast([P, G, D])

            def gated_bias(dst, gate, bias, done):
                pool.tensor_tensor(dst, gate, bias_rows(bias), ALU.mult).then_inc(done, 1)

            def sine(u, i):
                pool.wait_ge(swapped[i], upto(u - NT, 32, 32))
                part = rot_s[:, i, :].rearrange("p (b s) -> p b s", b=TB)
                pool.tensor_tensor(part, part, rtab[:, 1:2, :].to_broadcast([P, TB, S]), ALU.mult)\
                    .then_inc(rot_sin, 1)

            def hidden_low(v, m):
                if not (first(v) and m < 2):
                    pool.wait_ge(pe_f2, upto(v, MC, max(m - 1, 0)))
                pool.wait_ge(h_hi, upto(v, MC, m + 1))
                pool.tensor_tensor(hb[1][:, m % 2, :], hact[:, m % 2, :], hb[0][:, m % 2, :].bitcast(F32),
                                   ALU.subtract).then_inc(h_lo, 1)

            def step(u, layer, attn, ffn, nxt):
                v = u - 1
                if ffn:
                    low_part(v, 0, z_hi, zb, z_lo)
                if attn and layer == 1:
                    sine(u, 0)
                if attn and layer == 1:
                    sine(u, 1)
                    sine(u, 2)
                if attn and layer == 0:
                    pool.wait_ge(gate1_in, upto(u, 32, 32))
                    if not first(u):
                        pool.wait_ge(xres_ready, upto(u, 1, 0))
                    gated_bias(gated_bo[...], gate_bc[0], bo_bc, xres_chain)
                if ffn:
                    hidden_low(v, 0)
                if attn and layer == 1:
                    sine(u, 3)
                if ffn:
                    hidden_low(v, 1)
                if nxt:
                    first_rstd(u + 1)
                if ffn:
                    pool.wait_ge(x1_done[layer], upto(v, G, G))
                    pool.wait_ge(zn_ready, upto(v, G, G))
                    if not first(v):
                        pool.wait_ge(x_stored, upto(v, 16, 0))
                    if layer == 0:
                        pool.wait_ge(gate2_in, upto(v, 32, 32))
                        gated_bias(x1m, gate_bc[1], b2_bc, x1m_chain)
                        pool.wait_ge(x1m_chain, upto(v, 1, 1))
                        pool.tensor_tensor(x1m, x1m, x_res, ALU.add).then_inc(x1m_ready, 1)
                    else:
                        pool.tensor_tensor(x1m, x_res, bias_rows(b2_bc), ALU.add).then_inc(x1m_ready, 1)
                    hidden_low(v, 2)
                if attn:
                    pool.wait_ge(xres_loaded, upto(u, 16, 16))
                    if layer == 0:
                        pool.wait_ge(xres_chain, upto(u, 1, 1))
                    pool.tensor_tensor(x_res, x_res, gated_bo[...] if layer == 0 else bias_rows(bo_bc), ALU.add)\
                        .then_inc(xres_ready, 1)
                if attn and layer == 1:
                    pool.wait_ge(pe_pv, upto(u, 2 * G, 0))
                    if known(u) and u == NT:
                        pool.wait_ge(dve_setup, SET_MASKT)
                    pool.wait_ge(xres_ready, upto(u, 1, 1))
                    if ffn:
                        pool.wait_ge(h_lo, upto(v, MC, 3))
                    for h in range(2):
                        r = slice(h * S, (h + 1) * S)
                        dst = vb[r, :, :].rearrange("p b (n e) -> p b n e", e=2 * VB)[:, :, :, h * VB + HD]
                        src = maskT[r, bass.ds((u - NT) * TB, TB)].rearrange("p (b o) -> p b o", o=1)
                        pool.tensor_copy(dst, src.to_broadcast([S, TB, H // 2])).then_inc(v_ones, 1)
                        pool.wait_ge(v_ones, upto(u - NT, 2, h + 1))
                for g in range(G):
                    if ffn:
                        hidden_low(v, 3 + g)
                    if attn and 0 < g < G - 1:
                        second_rstd(u, g - 1)
                    if nxt and g == G - 2:
                        front(u + 1, layer, 0)
                if ffn:
                    hidden_low(v, MC - 1)
                if attn:
                    second_rstd(u, G - 2)
                if nxt:
                    front(u + 1, layer, 1)
                if attn:
                    second_rstd(u, G - 1)
                if ffn and layer == 0:
                    for h in range(2):
                        pool.wait_ge(f2_read, upto(v, 2, h + 1))
                        part = slice(2 * h, 2 * h + 2)
                        pool.tensor_tensor(x1m[:, part, :], gate_bc[1][:, part, :], x1m[:, part, :], ALU.add)\
                            .then_inc(f2_added, 1)

            for layer in range(2):
                layer_steps(pool, layer, setup, front, step)

        @block.scalar
        def _(act):
            def setup(layer):
                loads_in(act, layer)
                for n in range(NSPLIT):
                    s = slice(n * SPLIT, (n + 1) * SPLIT)
                    nc.scalar.copy(wgt[0][:, s], w_raw[:, s]).then_inc(w_hi, 1)
                if layer == 0:
                    act.wait_ge(pe_setup, 2)
                    nc.scalar.activation(hact[:, 1, :], C[:, :], ACT.Tanh).then_inc(act_setup, 1)

            def front(u, layer, c=None):
                for c in range(KC) if c is None else (c,):
                    act.wait_ge(y_aff, upto(u, KC, c + 1))
                    if not first(u):
                        act.wait_ge(pe_v, upto(u, 2, 0))
                    nc.scalar.copy(yb[0][:, c, :], aff[:, c, :]).then_inc(y_hi, 1)

            def second_norm(v, c):
                act.wait_ge(z_aff, upto(v, KC, c + 1))
                if not first(v):
                    act.wait_ge(pe_f1, upto(v, MC, 0))
                nc.scalar.copy(zb[0][:, c, :], aff[:, c, :]).then_inc(z_hi, 1)

            def chunk(i):
                return (i % KC, i < KC)

            def before_rotation(u, i):
                c, keys = chunk(i)
                act.wait_ge(pe_qk, upto(u, 4, i + 1))
                if not (known(u) and u == NT):
                    act.wait_ge(qk_lo, upto(u, 4, i - 3))
                col = KC * keys + c
                nc.scalar.activation(rot_t[:, i, :], (A + B)[i][:, :], ACT.Identity,
                                     bias=qk_bias[:, col:col + 1]).then_inc(rot_ready, 1)

            def high_qk(u, layer, i):
                c, keys = chunk(i)
                if layer == 0:
                    act.wait_ge(pe_qk, upto(u, 4, i + 1))
                    src = (A + B)[i]
                    bias = qk_bias[:, KC * keys + c:KC * keys + c + 1]
                else:
                    act.wait_ge(rot_sum, upto(u - NT, 4, i + 1))
                    src = rot_t[:, i, :]
                    bias = None
                if keys:
                    if not first(u):
                        act.wait_ge(kb_in, upto(u, NKB, 0))
                    parts = [(slice(0, P), by_seq(kflat[:, c, 0, :]))]
                else:
                    if not first(u):
                        act.wait_ge(pe_s, upto(u, 2 * G, 0))
                    if first(u) and i == KC:
                        act.wait_ge(sem_zero, NZERO)
                    parts = [(slice(x * 64, x * 64 + 64), qb[0][x * 64:x * 64 + 64, c, :, x, :]) for x in range(NX)]
                for n, (r, dst) in enumerate(parts):
                    if bias is not None:
                        ins = nc.scalar.activation(dst, by_seq(src[r, :]), ACT.Identity, bias=bias[r, :])
                    else:
                        ins = nc.scalar.copy(dst, by_seq(src[r, :]))
                    if n == len(parts) - 1:
                        ins.then_inc(qk_hi, 1)

            def values(u, pair):
                if first(u):
                    act.wait_ge(sem_zero, NZERO)
                else:
                    act.wait_ge(pe_pv, upto(u, 2 * G, 0))
                act.wait_ge(pe_v, upto(u, 2, pair + 1))
                for b in range(2):
                    for h in range(2):
                        dst, src = value_views(pair, b, h)
                        nc.scalar.copy(dst, src).then_inc(v_moved, 1)

            def hidden(v, m):
                act.wait_ge(pe_f1, upto(v, MC, m + 1))
                if not (first(v) and m < 2):
                    act.wait_ge(h_lo, upto(v, MC, max(m - 1, 0)))
                nc.scalar.activation(hact[:, m % 2, :], C[:, :], ACT.Gelu, bias=b1_col[:, m:m + 1])\
                    .then_inc(gelu, 1)
                act.wait_ge(gelu, upto(v, MC, m + 1))
                if not (first(v) and m < 2):
                    act.wait_ge(pe_f2, upto(v, MC, max(m - 1, 0)))
                nc.scalar.copy(hb[0][:, m % 2, :], hact[:, m % 2, :]).then_inc(h_hi, 1)

            def exponentials(u, g):
                for b in range(2):
                    act.wait_ge(s_sub, upto(u, 2 * G, 2 * g + b + 1))
                    nc.scalar.activation(exps[:, b, :], exps[:, b, :], ACT.Exp, scale=SCORE_SCALE)\
                        .then_inc(s_exp, 1)

            def move_probs(u, g):
                for b in range(2):
                    act.wait_ge(pe_pt, upto(u, 2 * G, 2 * g + b + 1))
                    if not (first(u) and g == 0):
                        act.wait_ge(pe_pv, upto(u, 2 * G, max(2 * (g - 1) + b + 1, 0)))
                    nc.scalar.copy(pt[:, b, :], B[b][:, :]).then_inc(pt_moved, 1)

            def high_heads(u, g):
                act.wait_ge(pe_ot, upto(u, G, g + 1))
                if not (first(u) and g == 0):
                    act.wait_ge(pe_proj, upto(u, G, g))
                for x in range(NX):
                    nc.scalar.activation(ot[0][:, x, :].rearrange("p (b q) -> p b q", b=2), head_rows(x), ACT.Identity,
                                         bias=v_bias[:, x:x + 1]).then_inc(ot_hi, 1)

            def step(u, layer, attn, ffn, nxt):
                v = u - 1
                if attn:
                    for i in range(2 * KC - 1):
                        if layer == 0:
                            high_qk(u, layer, i)
                        else:
                            before_rotation(u, i)
                if ffn:
                    second_norm(v, 0)
                if attn and layer == 0:
                    high_qk(u, layer, 2 * KC - 1)
                if attn and layer == 1:
                    before_rotation(u, 2 * KC - 1)
                if ffn:
                    second_norm(v, 1)
                if attn and layer == 0:
                    values(u, 0)
                    values(u, 1)
                for i in range(KC):
                    if attn and layer == 1:
                        high_qk(u, layer, i)
                for i in range(KC):
                    if ffn:
                        hidden(v, i)
                    if attn and layer == 1:
                        values(u, i)
                        high_qk(u, layer, KC + i)
                if attn and layer == 0:
                    exponentials(u, 0)
                if ffn:
                    hidden(v, 2)
                if attn and layer == 1:
                    exponentials(u, 0)
                for g in range(G):
                    if attn:
                        move_probs(u, g)
                    if attn and g > 0:
                        high_heads(u, g - 1)
                    if attn and g < G - 1:
                        exponentials(u, g + 1)
                    if ffn:
                        hidden(v, 3 + g)
                    if nxt and g == G - 2:
                        front(u + 1, layer, 0)
                if ffn:
                    hidden(v, MC - 1)
                if nxt:
                    front(u + 1, layer, 1)
                if attn:
                    high_heads(u, G - 1)

            for layer in range(2):
                layer_steps(act, layer, setup, front, step)

        @block.tensor
        def _(pe):
            def product(dst, pairs, first_start=True, last_stop=True, **kw):
                todo = [(l[p], r[q]) for l, r in pairs for p, q in PASSES]
                for n, (l, r) in enumerate(todo):
                    ins = nc.tensor.matmul(dst, l, r, start=first_start and n == 0,
                                           stop=last_stop and n == len(todo) - 1, **kw)
                return ins

            def w(base, width, k, lo, n):
                return [w_slice(p, base, width, k, lo, n) for p in range(2)]

            def setup(layer):
                if layer == 0:
                    pe.wait_ge(sem_ident, 2)
                loads_in(pe, layer)
                for k in range(KC):
                    ins = nc.tensor.transpose(E[:, k * P:(k + 1) * P], cond_sb[:, k * P:(k + 1) * P], ident[:, :])
                ins.then_inc(pe_setup, 1)
                pe.wait_ge(dve_setup, (SET_CONDT, SET_CONDT1)[layer])
                if layer == 1:
                    nc.tensor.transpose(E[:, 0:P], mask01[:, :, :].rearrange("p a s -> p (a s)"), ident[:, :])\
                        .then_inc(pe_setup, 1)
                for n in range(2):
                    for k in range(2):
                        for c in range(KC):
                            dst = Dk[n][:, (2 * k + c) * P:(2 * k + c + 1) * P]
                            for q in range(KC):
                                ins = nc.tensor.matmul(dst, mod_raw[2 * n + k][:, q, c * P:(c + 1) * P], condT[:, q, :],
                                                       start=(q == 0), stop=(q == KC - 1))
                if layer == 0:
                    pe.wait_ge(sem_zero, NZERO)
                    for n in range(2):
                        dst = C[:, n * D:(n + 1) * D]
                        for q in range(KC):
                            nc.tensor.matmul(dst, condT[:, q, :], mod_raw[4 + n][:, q, :], start=(q == 0), stop=False)
                        ins = nc.tensor.matmul(dst, ones[:, :], gate_row[:, n, :], start=False, stop=True)
                ins.then_inc(pe_setup, 1)
                pe.wait_ge(w_hi, NSPLIT * (layer + 1))
                pe.wait_ge(w_lo, NSPLIT * (layer + 1))
                pe.wait_ge(dve_setup, (SET_MOD0, SET_MASKT)[layer])

            def front(u, layer, c=None):
                for c in range(KC) if c is None else (c,):
                    pe.wait_ge(xn_ready, upto(u, G, G))
                    if c == 1:
                        pe.wait_ge(y_aff, upto(u, KC, 1))
                    if not (known(u) and u % NT == 0):
                        pe.wait_ge(proj_read, upto(u - 1, G, G - KC + c))
                    for g in range(G):
                        ins = nc.tensor.transpose(E[:, g * P:(g + 1) * P], xn[:, g, c * P:(c + 1) * P], ident[:, :])
                    ins.then_inc(pe_yt, 1)

            def second_norm(v, c, attn):
                pe.wait_ge(zn_ready, upto(v, G, G))
                if c == 0:
                    pe.wait_ge(proj_read, upto(v, G, G))
                    if attn:
                        pe.wait_ge(y_aff, upto(v + 1, KC, KC))
                else:
                    pe.wait_ge(z_aff, upto(v, KC, 1))
                for g in range(G):
                    ins = nc.tensor.transpose(E[:, g * P:(g + 1) * P], zn[:, g, c * P:(c + 1) * P], ident[:, :])
                ins.then_inc(pe_zt, 1)

            def queries_keys(u, i):
                c, keys = i % KC, i < KC
                if i == 0:
                    pe.wait_ge(y_hi, upto(u, KC, KC))
                    pe.wait_ge(y_lo, upto(u, KC, KC))
                if not first(u):
                    if i < 2:
                        pe.wait_ge(s_sub, upto(u, 2 * G, 0))
                    else:
                        pe.wait_ge(pv_norm, upto(u, 2 * G, 0))
                product((A + B)[i][:, :], [(w(W_QKV, 3 * D, k, D * keys + c * P, P), [yb[q][:, k, :] for q in range(2)])
                                           for k in range(KC)]).then_inc(pe_qk, 1)

            def chunk_taken(u, layer, i):
                if layer == 0:
                    pe.wait_ge(qk_lo, upto(u, 4, i + 1))
                else:
                    pe.wait_ge(rot_ready, upto(u - NT, 4, i + 1))

            def values(u, layer, pair):
                chunk_taken(u, layer, pair)
                for g in (2 * pair, 2 * pair + 1):
                    ins = product(A[pair][:, (g % 2) * D:(g % 2 + 1) * D],
                                  [([yb[p][:, k, g * P:(g + 1) * P] for p in range(2)], w(W_QKV, 3 * D, k, 2 * D, D))
                                   for k in range(KC)])
                ins.then_inc(pe_v, 1)

            def scores(u, layer, g):
                if g == 0:
                    pe.wait_ge(qk_hi, upto(u, 4, 4))
                    pe.wait_ge(qk_lo, upto(u, 4, 4))
                    pe.wait_ge(kb_in, upto(u, NKB, NKB))
                    pe.wait_ge(v_moved, upto(u, 8, 8))
                    if layer == 1:
                        pe.wait_ge(mrow_in, upto(u - NT, 16, 16))
                for b in range(2):
                    if g > 0:
                        pe.wait_ge(s_sub, upto(u, 2 * G, 2 * g + b - 1))
                    s = slice((2 * g + b) * S, (2 * g + b + 1) * S)
                    for c in range(KC):
                        dst = A[b][:, c * 256:(c + 1) * 256]
                        ins = product(dst, [([qb[p][:, c, 2 * g + b, :, :].rearrange("p x s -> p (x s)") for p in range(2)],
                                             [kb[:, c, q, :, s] for q in range(2)])], last_stop=(layer == 0))
                        if layer == 1:
                            row = mrow[:, s].rearrange("p (o s) -> p o s", o=1).to_broadcast([P, NJ, S])
                            ins = nc.tensor.matmul(dst, mean_w[:, :], row, start=False, stop=True)
                    ins.then_inc(pe_s, 1)

            def turn_probs(u, layer, g):
                for b in range(2):
                    if g == 0:
                        chunk_taken(u, layer, 2 + b)
                    else:
                        pe.wait_ge(pv_norm, upto(u, 2 * G, 2 * g + b - 1))
                    pe.wait_ge(s_exp, upto(u, 2 * G, 2 * g + b + 1))
                    for n in range(4):
                        ins = nc.tensor.transpose(B[b][:, n * P:(n + 1) * P], exps[:, b, n * P:(n + 1) * P], ident[:, :])
                    ins.then_inc(pe_pt, 1)

            def weigh_values(u, layer, g):
                if layer == 1 and g == 0:
                    pe.wait_ge(v_ones, upto(u - NT, 2, 2))
                for b in range(2):
                    pe.wait_ge(pt_moved, upto(u, 2 * G, 2 * g + b + 1))
                    for c in range(KC):
                        for jp in range(2):
                            n = 2 * c + jp
                            moving = vb[:, 2 * g + b, c * 136:(c + 1) * 136].rearrange("p (x e) -> p x e", x=NX)[
                                :, :, jp * 34:(jp + 1) * 34]
                            ins = nc.tensor.matmul(B[b][:, n * 68:(n + 1) * 68], pt[:, b, n * P:(n + 1) * P], moving,
                                                   start=True, stop=True)
                    ins.then_inc(pe_pv, 1)

            def turn_heads(u, g, ffn, nxt):
                if g == 0:
                    pe.wait_ge(y_aff, upto(u, KC, KC))
                    if ffn:
                        pe.wait_ge(z_aff, upto(u - 1, KC, KC))
                else:
                    pe.wait_ge(proj_read, upto(u, G, g))
                    if g >= G - KC and nxt:
                        pe.wait_ge(y_aff, upto(u + 1, KC, g - (G - KC) + 1))
                pe.wait_ge(pv_norm, upto(u, 2 * G, 2 * g + 2))
                for b in range(2):
                    ins = nc.tensor.transpose(E[:, b * P:(b + 1) * P], o_sb[:, b, :], ident[:, :])
                ins.then_inc(pe_ot, 1)

            def project(u, g):
                pe.wait_ge(ot_hi, upto(u, 8, 2 * g + 2))
                pe.wait_ge(ot_lo, upto(u, 8, 2 * g + 2))
                product(E[:, D:2 * D], [([ot[p][:, x, :] for p in range(2)], w(W_PROJ, D, x, 0, D)) for x in range(NX)])\
                    .then_inc(pe_proj, 1)

            def hidden(v, m):
                if m == 0:
                    pe.wait_ge(z_hi, upto(v, KC, KC))
                    pe.wait_ge(z_lo, upto(v, KC, KC))
                if not (first(v) and m == 0):
                    pe.wait_ge(gelu, upto(v, MC, m))
                product(C[:, :], [(w(W_FF1, FF, k, m * P, P), [zb[q][:, k, :] for q in range(2)]) for k in range(KC)])\
                    .then_inc(pe_f1, 1)

            def back(v, m):
                pe.wait_ge(h_lo, upto(v, MC, m + 1))
                if m == 0 and not first(v):
                    pe.wait_ge(f2_read, upto(v, 2, 0))
                for g in range(G):
                    ins = product(Dk[g // 2][:, (g % 2) * D:(g % 2 + 1) * D],
                                  [([hb[p][:, m % 2, g * P:(g + 1) * P] for p in range(2)], w(W_FF2, D, m, 0, D))],
                                  first_start=(m == 0 and g % 2 == 0), last_stop=(m == MC - 1), skip_group_check=True)
                ins.then_inc(pe_f2, 1)

            def step(u, layer, attn, ffn, nxt):
                v = u - 1
                if attn:
                    queries_keys(u, 0)
                    queries_keys(u, 1)
                    queries_keys(u, 2)
                if ffn:
                    second_norm(v, 0, attn)
                if attn:
                    queries_keys(u, 3)
                if ffn:
                    second_norm(v, 1, attn)
                if attn:
                    values(u, layer, 0)
                    values(u, layer, 1)
                if ffn:
                    hidden(v, 0)
                if ffn and layer == 0:
                    hidden(v, 1)
                if attn and layer == 0:
                    scores(u, layer, 0)
                if ffn:
                    if layer == 1:
                        hidden(v, 1)
                    back(v, 0)
                    hidden(v, 2)
                    back(v, 1)
                if attn and layer == 1:
                    scores(u, layer, 0)
                for g in range(G):
                    if ffn and layer == 1 and g == 0:
                        hidden(v, 3 + g)
                    if attn:
                        turn_probs(u, layer, g)
                    if attn and 0 < g < G - 1:
                        turn_heads(u, g - 1, ffn, nxt)
                    if attn and g < G - 1:
                        scores(u, layer, g + 1)
                    if ffn and g == G - 1:
                        hidden(v, 3 + g)
                    if attn and g == G - 1:
                        turn_heads(u, g - 1, ffn, nxt)
                    if ffn and g == G - 1:
                        back(v, 2 + g)
                    if attn:
                        weigh_values(u, layer, g)
                    if attn and g > 0:
                        project(u, g - 1)
                    if ffn and g < G - 1 and not (layer == 1 and g == 0):
                        hidden(v, 3 + g)
                    if nxt and g == G - 2:
                        front(u + 1, layer, 0)
                    if ffn and g < G - 1:
                        back(v, 2 + g)
                if ffn:
                    hidden(v, MC - 1)
                if nxt:
                    front(u + 1, layer, 1)
                if ffn:
                    back(v, MC - 2)
                if attn:
                    turn_heads(u, G - 1, ffn, nxt)
                if ffn:
                    back(v, MC - 1)
                if attn:
                    project(u, G - 1)

            for layer in range(2):
                layer_steps(pe, layer, setup, front, step)

        @block.vector
        def _(dve):
            for buf in (qb[0], qb[1], kb):
                nc.vector.memset(buf[...].bitcast(F32), 0.0).then_inc(sem_zero, 1)
            nc.vector.memset(vb[...], 0.0).then_inc(sem_zero, 1)
            dve.wait_ge(sem_zero, 4)
            for h in range(2):
                dst = vb[h * S:(h + 1) * S, :, :].rearrange("p b (n e) -> p b n e", e=2 * VB)[:, :, :, h * VB + HD]
                nc.vector.memset(dst, 1.0).then_inc(sem_zero, 1)
            nc.vector.memset(mean_w[:, :].bitcast(F32), 1.0 / P).then_inc(sem_zero, 1)
            nc.vector.memset(ones[:, :], 1.0).then_inc(sem_zero, 1)

            def modulations(at):
                n_done = at
                for n in range(2):
                    for c in range(KC):
                        s_psum, t_psum = Dk[n][:, c * P:(c + 1) * P], Dk[n][:, (2 + c) * P:(3 + c) * P]
                        scale, shift = mod[:, n, c, 0, :], mod[:, n, c, 1, :]
                        nc.vector.tensor_scalar(scale, s_psum, mod_col[:, n, 0, c:c + 1], 1.0, ALU.add, ALU.add)\
                            .then_inc(dve_setup, 1)
                        nc.vector.tensor_scalar(shift, t_psum, mod_col[:, n, 1, c:c + 1], None, ALU.add)\
                            .then_inc(dve_setup, 1)
                        dve.wait_ge(dve_setup, n_done + 2)
                        nc.vector.scalar_tensor_tensor(out=shift, in0=scale, scalar=ln_col[:, n, 1, c:c + 1], in1=shift,
                                                       op0=ALU.mult, op1=ALU.add).then_inc(dve_setup, 1)
                        nc.vector.tensor_scalar(scale, scale, ln_col[:, n, 0, c:c + 1], None, ALU.mult)\
                            .then_inc(dve_setup, 1)
                        n_done += 4
                dve.wait_ge(dve_setup, n_done)

            def setup(layer):
                loads_in(dve, layer)
                if layer == 1:
                    nc.vector.tensor_scalar(mask_add, mask_u8[:, :], BIG, -BIG, ALU.mult, ALU.add)\
                        .then_inc(dve_setup, 1)
                    for n in range(2):
                        nc.vector.tensor_copy(mask01[:, n, :], mask_u8[:, :]).then_inc(dve_setup, 1)
                for n in range(NSPLIT):
                    s = slice(n * SPLIT, (n + 1) * SPLIT)
                    dve.wait_ge(w_hi, NSPLIT * layer + n + 1)
                    nc.vector.tensor_tensor(wgt[1][:, s], w_raw[:, s], wgt[0][:, s].bitcast(F32), ALU.subtract)\
                        .then_inc(w_lo, 1)
                dve.wait_ge(pe_setup, (1, 3)[layer])
                nc.vector.tensor_copy(condT, E[:, 0:KC * P].rearrange("p (k b) -> p k b", k=KC)).then_inc(dve_setup, 1)
                if layer == 0:
                    dve.wait_ge(pe_setup, 2)
                    modulations(SET_CONDT)
                    dve.wait_ge(act_setup, 1)
                    nc.vector.tensor_scalar(hact[:, 1, :], hact[:, 1, :], GATE, None, ALU.mult).then_inc(dve_setup, 1)
                else:
                    dve.wait_ge(pe_setup, 5)
                    modulations(SET_CONDT1)
                    nc.vector.tensor_copy(maskT[:, :], E[:, 0:P]).then_inc(dve_setup, 1)

            def normalise(dst, src, mean, rstd):
                return nc.vector.tensor_scalar(dst, src, mean, rstd, ALU.subtract, ALU.mult)

            def first_statistics(u):
                dve.wait_ge(x_loaded, upto(u, 16, 16))
                for g in range(G):
                    nc.vector.bn_stats(st1[:, g, :], x_in[:, g, :]).then_inc(ln1_chain, 1)
                wait_apart(dve, dve_passed, (ln1_chain, upto(u, 9, 4)))
                for g in range(G):
                    nc.vector.bn_aggr(mv1[:, g, :], st1[:, g, :]).then_inc(ln1_chain, 1)
                dve.wait_ge(ln1_chain, upto(u, 9, 8))
                nc.vector.tensor_scalar(rs1[:, :], mv1[:, :, 1], EPS, None, ALU.add).then_inc(ln1_chain, 1)

            def first_norm(u):
                dve.wait_ge(ln1_rstd, upto(u, 1, 1))
                if not first(u):
                    dve.wait_ge(pe_yt, upto(u, KC, 0))
                for g in range(G):
                    normalise(xn[:, g, :], x_in[:, g, :], mv1[:, g, 0:1], rs1[:, g:g + 1]).then_inc(xn_ready, 1)

            def tile_modulation(u, layer, n, done):
                if not first(u):
                    dve.wait_ge(done, upto(u, KC, 0))
                nc.vector.tensor_copy(mod_tile[:, n, :, :, :],
                                      mod[:, n, :, :, bass.ds((u - layer * NT) * TB, TB)]).then_inc(mod_ready[n], 1)

            def modulate(u, n, c, turned, chain, done):
                part = by_seq(aff[:, c, :])
                scale, shift = (mod_tile[:, n, c, k, :].rearrange("p (b o) -> p b o", o=1).to_broadcast([P, TB, S])
                                for k in range(2))
                dve.wait_ge(mod_ready[n], upto(u, 1, 1))
                dve.wait_ge(turned, upto(u, KC, c + 1))
                nc.vector.tensor_tensor(part, by_seq(E[:, :]), scale, ALU.mult).then_inc(chain, 1)
                dve.wait_ge(chain, upto(u, KC, c + 1))
                nc.vector.tensor_tensor(part, part, shift, ALU.add).then_inc(done, 1)

            def first_modulated(u, c):
                if c == 0 and not (known(u) and u % NT < 2):
                    dve.wait_ge(z_lo, upto(u - 2, KC, KC))
                if c == 0 and known(u) and u % NT == 1:
                    dve.wait_ge(y_lo, upto(u, KC, 0))
                modulate(u, 0, c, pe_yt, y_scaled, y_aff)

            def second_modulated(v, c, attn):
                if c == 0:
                    dve.wait_ge(y_lo, upto(v, KC, 2 * KC if attn else KC))
                modulate(v, 1, c, pe_zt, z_scaled, z_aff)

            def front(u, layer):
                tile_modulation(u, layer, 0, y_aff)
                first_statistics(u)
                first_norm(u)
                for c in range(KC):
                    first_modulated(u, c)

            def low_qk(u, layer, i):
                c, keys = i % KC, i < KC
                col = KC * keys + c
                dve.wait_ge(qk_hi, upto(u, 4, i + 1))
                rows = [slice(0, P)] if keys else [slice(0, 64), slice(64, 128)]
                for x, r in enumerate(rows):
                    hi = by_seq(kflat[:, c, 0, :]) if keys else qb[0][r, c, :, x, :]
                    lo = by_seq(kflat[:, c, 1, :]) if keys else qb[1][r, c, :, x, :]
                    if layer == 0:
                        ins = nc.vector.scalar_tensor_tensor(out=lo, in0=by_seq((A + B)[i][r, :]), scalar=qk_bias[r, col:col + 1],
                                                             in1=hi.bitcast(F32), op0=ALU.add, op1=ALU.subtract)
                    else:
                        ins = nc.vector.tensor_tensor(lo, by_seq(rot_t[r, i, :]), hi.bitcast(F32), ALU.subtract)
                ins.then_inc(qk_lo, 1)

            def cosine(u, i):
                dve.wait_ge(swapped[i], upto(u - NT, 32, 32))
                part = rot_t[:, i, :].rearrange("p (b s) -> p b s", b=TB)
                nc.vector.tensor_tensor(part, part, rtab[:, 0:1, :].to_broadcast([P, TB, S]), ALU.mult)\
                    .then_inc(rot_cos, 1)

            def rotated(u, i):
                dve.wait_ge(rot_cos, upto(u - NT, 4, i + 1))
                dve.wait_ge(rot_sin, upto(u - NT, 4, i + 1))
                nc.vector.tensor_tensor(rot_t[:, i, :], rot_t[:, i, :], rot_s[:, i, :], ALU.add)\
                    .then_inc(rot_sum, 1)

            def subtract_max(u, g):
                for b in range(2):
                    dve.wait_ge(pe_s, upto(u, 2 * G, 2 * g + b + 1))
                    s = A[b][:, :].rearrange("p (h k) -> p h k", k=S)
                    nc.vector.tensor_reduce(mx[:, b, :], s, AX.X, ALU.max).then_inc(s_max, 1)
                    dve.wait_ge(s_max, upto(u, 2 * G, 2 * g + b + 1))
                    if not (first(u) and g == 0):
                        dve.wait_ge(pe_pt, upto(u, 2 * G, max(2 * (g - 1) + b + 1, 0)))
                    nc.vector.tensor_tensor(exps[:, b, :].rearrange("p (h k) -> p h k", k=S), s,
                                            mx[:, b, :].rearrange("p (h o) -> p h o", o=1).to_broadcast([P, 8, S]),
                                            ALU.subtract).then_inc(s_sub, 1)

            def normalise_heads(u, g):
                if not (first(u) and g == 0):
                    dve.wait_ge(pe_ot, upto(u, G, g))
                for b in range(2):
                    dve.wait_ge(pe_pv, upto(u, 2 * G, 2 * g + b + 1))
                    sums = B[b][:, 0:4 * 68].rearrange("p (n x j e) -> p n x j e", n=4, x=NX, e=VB)
                    r = rden[:, b, :].rearrange("p (n j) -> p n j", n=4)
                    nc.vector.reciprocal(r, sums[:, :, 0, :, HD]).then_inc(pv_rden, 1)
                    dve.wait_ge(pv_rden, upto(u, 2 * G, 2 * g + b + 1))
                    for x in range(NX):
                        p = slice(x * 64, x * 64 + 64)
                        ins = nc.vector.tensor_tensor(
                            o_sb[p, b, :].rearrange("p (n j d) -> p n j d", n=4, j=2), sums[p, :, x, :, 0:HD],
                            rden[p, b, :].rearrange("p (n j o) -> p n j o", n=4, o=1).to_broadcast([64, 4, 2, HD]),
                            ALU.mult)
                    ins.then_inc(pv_norm, 1)

            def low_heads(u, g):
                dve.wait_ge(ot_hi, upto(u, 8, 2 * g + 2))
                for x in range(NX):
                    as_rows = [ot[p][:, x, :].rearrange("p (b q) -> p b q", b=2) for p in range(2)]
                    nc.vector.scalar_tensor_tensor(out=as_rows[1], in0=head_rows(x), scalar=v_bias[:, x:x + 1],
                                                   in1=as_rows[0].bitcast(F32), op0=ALU.add, op1=ALU.subtract)\
                        .then_inc(ot_lo, 1)

            def residual(u, layer, g):
                dve.wait_ge(pe_proj, upto(u, G, g + 1))
                if g == 0:
                    dve.wait_ge(xres_ready, upto(u, 1, 1))
                if layer == 0:
                    gate = gate_bc[0][:, g, :]
                    nc.vector.tensor_tensor(gate, E[:, D:2 * D], gate, ALU.mult).then_inc(proj_read, 1)
                    dve.wait_ge(proj_read, upto(u, G, g + 1))
                    nc.vector.tensor_tensor(x_res[:, g, :], gate, x_res[:, g, :], ALU.add).then_inc(x1_added, 1)
                else:
                    nc.vector.tensor_tensor(x_res[:, g, :], E[:, D:2 * D], x_res[:, g, :], ALU.add)\
                        .then_inc(proj_read, 1)

            def second_statistics(u, layer, g):
                dve.wait_ge(x1_done[layer], upto(u, G, g + 1))
                nc.vector.bn_stats(st2[:, g, :], x_res[:, g, :]).then_inc(ln2_chain, 1)
                wait_apart(dve, dve_passed, (ln2_chain, upto(u, 3 * G, 3 * g + 1)))
                nc.vector.bn_aggr(mv2[:, g, :], st2[:, g, :]).then_inc(ln2_chain, 1)
                dve.wait_ge(ln2_chain, upto(u, 3 * G, 3 * g + 2))
                nc.vector.tensor_scalar(rs2[:, g:g + 1], mv2[:, g, 1:2], EPS, None, ALU.add).then_inc(ln2_chain, 1)

            def second_normalise(u, g, ffn):
                dve.wait_ge(ln2_rstd, upto(u, G, g + 1))
                if g == 0 and ffn:
                    dve.wait_ge(pe_zt, upto(u, KC, 0))
                normalise(zn[:, g, :], x_res[:, g, :], mv2[:, g, 0:1], rs2[:, g:g + 1]).then_inc(zn_ready, 1)

            def layer_output(v, layer, h):
                if h == 0:
                    dve.wait_ge(pe_f2, upto(v, MC, MC))
                    dve.wait_ge(x1m_ready, upto(v, 1, 1))
                acc = Dk[h][:, :].rearrange("p (g d) -> p g d", g=2)
                part = slice(2 * h, 2 * h + 2)
                if layer == 0:
                    gate = gate_bc[1][:, part, :]
                    nc.vector.tensor_tensor(gate, acc, gate, ALU.mult).then_inc(f2_read, 1)
                else:
                    nc.vector.tensor_tensor(x1m[:, part, :], acc, x1m[:, part, :], ALU.add).then_inc(f2_read, 1)

            def step(u, layer, attn, ffn, nxt):
                v = u - 1
                if ffn:
                    tile_modulation(v, layer, 1, z_aff)
                if attn and layer == 0:
                    low_qk(u, layer, 0)
                    low_qk(u, layer, 1)
                if ffn:
                    second_modulated(v, 0, attn)
                if ffn:
                    second_modulated(v, 1, attn)
                if attn and layer == 0:
                    low_qk(u, layer, 2)
                if attn and layer == 1:
                    cosine(u, 0)
                if ffn:
                    dve.wait_ge(z_hi, upto(v, KC, KC))
                    nc.vector.tensor_tensor(zb[1][:, KC - 1, :], aff[:, KC - 1, :], zb[0][:, KC - 1, :].bitcast(F32),
                                            ALU.subtract).then_inc(z_lo, 1)
                if attn and layer == 0:
                    low_qk(u, layer, 3)
                if attn and layer == 1:
                    cosine(u, 1)
                    rotated(u, 0)
                    cosine(u, 2)
                    rotated(u, 1)
                    low_qk(u, layer, 0)
                    low_qk(u, layer, 1)
                    cosine(u, 3)
                    rotated(u, 2)
                if nxt:
                    first_statistics(u + 1)
                if attn and layer == 1:
                    rotated(u, 3)
                    low_qk(u, layer, 2)
                    low_qk(u, layer, 3)
                if attn:
                    subtract_max(u, 0)
                for g in range(G):
                    if attn and g > 0:
                        low_heads(u, g - 1)
                    if attn and g > 1:
                        second_normalise(u, g - 2, ffn)
                    if attn and g < G - 1:
                        subtract_max(u, g + 1)
                    if attn and g == G - 1:
                        normalise_heads(u, g)
                    if attn and g > 0:
                        residual(u, layer, g - 1)
                    if attn and g < G - 1:
                        normalise_heads(u, g)
                    if g >= G - KC and nxt:
                        first_modulated(u + 1, g - (G - KC))
                    if g == 0 and nxt:
                        tile_modulation(u + 1, layer, 0, y_aff)
                        first_norm(u + 1)
                    if attn and g > 0:
                        second_statistics(u, layer, g - 1)
                if attn:
                    second_normalise(u, G - 2, ffn)
                    low_heads(u, G - 1)
                if ffn:
                    layer_output(v, layer, 0)
                if attn:
                    residual(u, layer, G - 1)
                    second_statistics(u, layer, G - 1)
                if ffn:
                    layer_output(v, layer, 1)
                if attn:
                    second_normalise(u, G - 1, ffn)

            for layer in range(2):
                layer_steps(dve, layer, setup, front, step)


_INS = ["x", "cond_1024", "mask_BxS_bf1"] + [
    "L0_cond_" + n for n in ("g1_w", "g1_b", "b1_w", "b1_b", "a1_w", "a1_b", "g2_w", "g2_b", "b2_w", "b2_b", "a2_w",
                             "a2_b", "ln1_g", "ln1_b", "ln2_g", "ln2_b", "qkv_w", "qkv_b", "proj_w", "proj_b", "fc1_w",
                             "fc1_b", "fc2_w", "fc2_b")] + [
    "L1_cond_" + n for n in ("wq", "bq", "wk", "bk", "wv", "bv", "wo", "bo", "ln1_g", "ln1_b", "ada1_w", "ada1_b",
                             "ln2_g", "ln2_b", "ada2_w", "ada2_b", "ff_w1", "ff_b1", "ff_w2", "ff_b2")]


def rotary_table():
    import numpy as np
    inv = np.float32(1.0) / np.float32(10000.0) ** (np.arange(ROT, dtype=np.float32) / np.float32(ROT))
    angle = np.arange(S, dtype=np.float32)[:, None] * inv[None, :].astype(np.float32)
    d = np.arange(P) % HD
    sign = np.where(d % 2 == 0, -1.0, 1.0).astype(np.float32)
    cos, sin = np.cos(angle).T[d // 2], np.sin(angle).T[d // 2] * sign[:, None]
    return np.ascontiguousarray(np.stack([cos, sin], axis=1).astype(np.float32))


def kernel(**inputs):
    import numpy as np
    import concourse.bacc as bacc
    from concourse.bass_utils import run_bass_kernel_spmd

    nc = bacc.Bacc("TRN2", target_bir_lowering=False, num_devices=1)
    arrays, tensors = {}, {}
    for name in _INS + ["rotary"]:
        a = rotary_table() if name == "rotary" else np.ascontiguousarray(inputs[name])
        if a.dtype == np.bool_:
            a = a.view(np.uint8)
        arrays[f"in_{name}"] = a
        tensors[name] = nc.dram_tensor(f"in_{name}", a.shape, mybir.dt.from_np(a.dtype), kind="ExternalInput").ap()
    out = nc.dram_tensor("out", (NB, S, D), F32, kind="ExternalOutput").ap()
    build(nc, tensors, out)
    r = run_bass_kernel_spmd(nc, [arrays], core_ids=[0])
    return r.results[0]["out"]
```

```python
from contextlib import ExitStack

import concourse.bass as bass
from concourse import mybir

F32 = mybir.dt.float32
F32R = mybir.dt.float32r
U8 = mybir.dt.uint8
ALU = mybir.AluOpType
ACT = mybir.ActivationFunctionType
AX = mybir.AxisListType

P = 128
NB, S, D = 128, 64, 256
H, HD = 16, 16
FF = 4 * D
KC = D // P
MC = FF // P
TILE = 512
G = TILE // P
TB = TILE // S
NT = NB * S // TILE
NX, NJ = 2, 4
VB = HD + 1
VROW = H * VB
EPS = 1e-5
GATE = 0.1
SCORE_SCALE = HD ** -0.5
BIG = 2.0 ** 100
ROT = HD // 2

W_QKV, W_PROJ = 0, KC * 3 * D
W_FF1 = W_PROJ + KC * D
W_FF2 = W_FF1 + KC * FF
W_ALL = W_FF2 + MC * D
PASSES = ((0, 0), (1, 0), (0, 1))


def build(nc, t, out):
    ctx = ExitStack()
    with ctx:
        def sb(name, shape, dt=F32):
            return ctx.enter_context(nc.sbuf_tensor(name, shape, dt))

        def bank(name):
            return ctx.enter_context(nc.psum_tensor(name, [P, 512], F32))

        def sem(name):
            return ctx.enter_context(nc.semaphore(name))

        x_tiles = t["x"].rearrange("b s d -> (b s) d").rearrange("(t g p) d -> t p g d", g=G, p=P)
        mid = nc.dram_tensor("mid", [NB * S, D], F32, kind="Internal").ap()
        mid_tiles = mid.rearrange("(t g p) d -> t p g d", g=G, p=P)
        out_tiles = out.rearrange("b s d -> (b s) d").rearrange("(t g p) d -> t p g d", g=G, p=P)
        gates = [nc.dram_tensor(f"gates{n}", [NB, D], F32, kind="Internal").ap() for n in range(2)]
        gate_tiles = [g.rearrange("(t g b) d -> t b g d", g=G, b=2) for g in gates]
        mask_rows = nc.dram_tensor("mask_rows", [NB, S], F32, kind="Internal").ap()
        mask_tiles = mask_rows.rearrange("(t b) s -> t (b s)", b=TB)

        wgt = [sb("wgt_hi", [P, W_ALL], F32R), sb("wgt_lo", [P, W_ALL], F32R)]
        TE = G * D
        arena = sb("arena", [P, 11 * TE])

        def view(n, k=1):
            return arena[:, n * TE:(n + k) * TE]

        def tokens(n):
            return view(n).rearrange("p (g d) -> p g d", g=G)

        x_in, xn, x_res, x1m, zn = (tokens(n) for n in range(5))
        aff = view(5).rearrange("p (c n) -> p c n", c=KC)
        exps = view(6).rearrange("p (b n) -> p b n", b=2)
        gate_bc = [tokens(7), tokens(8)]
        rot_t = view(7, 2).rearrange("p (r n) -> p r n", r=4)
        rot_s = view(9, 2).rearrange("p (r n) -> p r n", r=4)
        gated_bo = tokens(9)
        yb = [sb("y_hi", [P, KC, TILE], F32R), sb("y_lo", [P, KC, TILE], F32R)]
        zb = [sb("z_hi", [P, KC, TILE], F32R), sb("z_lo", [P, KC, TILE], F32R)]
        qb = [sb("q_hi", [P, KC, TB, NX, S], F32R), sb("q_lo", [P, KC, TB, NX, S], F32R)]
        kflat = sb("k_flat", [P, KC, 2, TILE], F32R)
        kb = sb("k_blocks", [P, KC, 2, NJ, TILE], F32R)
        vb = sb("v_blocks", [P, TB, VROW])
        w_raw = [view(9, 2), vb[...].rearrange("p b r -> p (b r)")[:, 0:2 * TE], view(6, 2)]
        mod_raw = [view((4, 3)[n // 4], (2, 1)[n // 4])[:, n % 4 * KC * D:(n % 4 + 1) * KC * D]
                   .rearrange("p (k n) -> p k n", k=KC) for n in range(6)]
        pt = sb("probs_turned", [P, 2, 512])
        o_sb = sb("o_sb", [P, 2, P])
        ot = [sb("ot_hi", [P, NX, P], F32R), sb("ot_lo", [P, NX, P], F32R)]
        hact = sb("hact", [P, 2, TILE])
        hb = [sb("h_hi", [P, 2, TILE], F32R), sb("h_lo", [P, 2, TILE], F32R)]
        mod = sb("mod", [P, 2, KC, 2, NB])
        ident = sb("ident", [P, P])
        ones = sb("ones", [1, P])
        mod_tile = sb("mod_tile", [P, 2, KC, 2, TB])
        bo_bc = sb("bo_bc", [P, 2, D])
        b2_bc = sb("b2_bc", [P, 2, D])
        qk_bias = sb("qk_bias", [P, 2, 2 * KC])
        v_bias = sb("v_bias", [P, 2, NX])
        b1_col = sb("b1_col", [P, 2, MC])
        ln_col = sb("ln_col", [P, 2, 2, KC])
        mod_col = sb("mod_col", [P, 2, 2, KC])
        mx = sb("mx", [P, 2, 8])
        rden = sb("rden", [P, 2, 8])
        st1 = sb("st1", [P, G, 6])
        mv1 = sb("mv1", [P, G, 2])
        rs1 = sb("rs1", [P, G])
        st2 = sb("st2", [P, G, 6])
        mv2 = sb("mv2", [P, G, 2])
        rs2 = sb("rs2", [P, G])
        minus_half = sb("minus_half", [P, G])
        rtab = sb("rtab", [P, 2, S])
        mrow = sb("mrow", [P, TILE], F32R)
        mean_w = sb("mean_w", [P, P], F32R)
        mask_u8 = sb("mask_u8", [P, S], U8)
        mask01 = view(2)[:, 0:2 * S].rearrange("p (a s) -> p a s", a=2)
        mask_add = view(2)[:, 2 * S:3 * S]
        maskT = sb("maskT", [P, NB])
        condT = sb("condT", [P, KC, NB])
        cond_sb = hact[:, 0, 0:D]
        gate_row = hact[0:1, 1, :].rearrange("p (n d) -> p n d", n=2)
        gate_rows = hact[:, 1, :].rearrange("p (n d) -> p n d", n=2)

        A = [bank("A0"), bank("A1")]
        B = [bank("B0"), bank("B1")]
        C = bank("C")
        Dk = [bank("D0"), bank("D1")]
        E = bank("E")

        cond_in, mods_in, ln_in, bias_in = sem("cond_in"), sem("mods_in"), sem("ln_in"), sem("bias_in")
        w_in = [sem("w_attention_in"), sem("w_ff1_in"), sem("w_ff2_in")]
        sem_ident = sem("consts_ready")
        sem_zero, k_zero = sem("zeros_ready"), sem("k_zero")
        v_blank = sem("v_blank")
        w_hi, w_lo = sem("w_hi"), sem("w_lo")
        pe_setup, dve_setup, act_setup = sem("pe_setup"), sem("dve_setup"), sem("act_setup")
        gates_out = sem("gates_out")
        x_loaded, xres_loaded, x_stored = sem("x_loaded"), sem("xres_loaded"), sem("x_stored")
        gate1_in, gate2_in, mrow_in = sem("gate1_in"), sem("gate2_in"), sem("mrow_in")
        kb_in = sem("kb_in")
        swapped = [sem(f"swapped{i}") for i in range(4)]
        xn_ready, ln1_chain, ln1_rstd = sem("xn_ready"), sem("ln1_chain"), sem("ln1_rstd")
        pe_yt, y_scaled, y_aff, y_hi, y_lo = sem("pe_yt"), sem("y_scaled"), sem("y_aff"), sem("y_hi"), sem("y_lo")
        pe_qk, qk_hi, qk_lo = sem("pe_qk"), sem("qk_hi"), sem("qk_lo")
        rot_ready, rot_cos, rot_sin, rot_sum = sem("rot_ready"), sem("rot_cos"), sem("rot_sin"), sem("rot_sum")
        pe_v, v_moved, v_ones = sem("pe_v"), sem("v_moved"), sem("v_ones")
        pe_s, s_max, s_sub, s_exp = sem("pe_s"), sem("s_max"), sem("s_sub"), sem("s_exp")
        pe_pt, pt_moved = sem("pe_pt"), sem("pt_moved")
        pe_pv, pv_rden, pv_norm = sem("pe_pv"), sem("pv_rden"), sem("pv_norm")
        pe_ot, ot_hi, ot_lo = sem("pe_ot"), sem("ot_hi"), sem("ot_lo")
        pe_proj, proj_read, x1_added = sem("pe_proj"), sem("proj_read"), sem("x1_added")
        ln2_chain, zn_ready, ln2_rstd = sem("ln2_chain"), sem("zn_ready"), sem("ln2_rstd")
        xres_chain, xres_ready, x1m_chain, x1m_ready = (sem("xres_chain"), sem("xres_ready"),
                                                        sem("x1m_chain"), sem("x1m_ready"))
        pe_zt, z_scaled, z_aff, z_hi, z_lo = sem("pe_zt"), sem("z_scaled"), sem("z_aff"), sem("z_hi"), sem("z_lo")
        pe_f1, gelu, h_hi, h_lo, pe_f2 = sem("pe_f1"), sem("gelu"), sem("h_hi"), sem("h_lo"), sem("pe_f2")
        f2_read, f2_added = sem("f2_read"), sem("f2_added")
        sp_passed, dve_passed = sem("sp_passed"), sem("dve_passed")
        mod_ready = [sem("mod1_ready"), sem("mod2_ready")]
        x1_done = [x1_added, proj_read]
        f2_done = [f2_added, f2_read]

        block = ctx.enter_context(nc.Block())

        def upto(u, n, k):
            return u * n + k

        def known(u):
            return isinstance(u, int)

        def wait_apart(eng, passed, *waits):
            for semaphore, count in waits:
                eng.wait_ge(semaphore, count)
                eng.sem_inc(passed, 1)

        def w_slice(part, base, width, k, lo, n):
            return wgt[part][:, base + k * width + lo:base + k * width + lo + n]

        def by_seq(ap):
            return ap.rearrange("p (b s) -> p b s", s=S)

        def value_views(pair, b, h):
            dst = vb[h * S:(h + 1) * S, 4 * pair + b:4 * pair + b + 3:2, :].rearrange(
                "p g (n e) -> p g n e", e=2 * VB)[:, :, :, h * VB:h * VB + HD]
            src = A[pair][b * S:(b + 1) * S, :].rearrange("p (g n h d) -> p g n h d", g=2, h=2, d=HD)[:, :, :, h, :]
            return dst, src

        def head_rows(x):
            return E[:, 0:2 * P].rearrange("p (b x q) -> p b x q", b=2, x=NX)[:, :, x, :]

        def first(u):
            return known(u) and u == 0

        def layer_steps(eng, layer, setup, front, finish, step):
            u0 = layer * NT
            setup(layer)
            front(u0, layer)
            finish(layer)
            step(u0, layer, True, False, True)
            step(u0 + 1, layer, True, True, True)
            with eng.Fori(u0 + 2, u0 + NT - 1) as u:
                step(u, layer, True, True, True)
            step(u0 + NT - 1, layer, True, True, False)
            step(u0 + NT, layer, False, True, False)

        N_MODS, N_W, N_BIAS = (6, 4), ((3, 5), (1, 1), (1, 1)), (9, 8)
        N_LN = 8
        NZERO = 4
        SPLITS = (slice(0, W_FF1), slice(W_FF1, W_FF2), slice(W_FF2, W_ALL))
        NSPLIT = len(SPLITS)
        NMOD = 16
        SET_MASKS, SET_MASKT = 4, 5
        SET_MOD = (5 + NMOD, 6 + 2 * NMOD)
        SET_GATES = 6 + NMOD
        PE_CONDT, PE_MASKT, PE_GATES, PE_MOD = 1, 2, 4, (3, 5)
        NKB = 16 * NX * NJ

        def all_of(eng, semaphore, counts, layer):
            eng.wait_ge(semaphore, 16 * sum(counts[:layer + 1]))

        @block.sync
        def _(sp):
            def tokens_of(u, layer):
                return x_tiles[u] if layer == 0 else mid_tiles[u - NT]

            def load_tokens(u, layer):
                sp.dma_start(x_in, tokens_of(u, layer)).then_inc(x_loaded, 16)

            def load_weights(layer):
                def ld(done, dst, src, **kw):
                    sp.dma_start(dst, src, **kw).then_inc(done, 16)

                def rows(m):
                    return m.rearrange("(k p) n -> p k n", p=P)

                def ld_column(done, dst, vec, p=P):
                    ld(done, dst, vec.rearrange("(c p) -> p c", p=p), allow_slow_non_contiguous=True)

                def row(vec):
                    return vec.rearrange("(o n) -> o n", o=1)

                w = {k[8:]: v for k, v in t.items() if k.startswith(f"L{layer}_cond_")}

                def ld_columns(mod_bias):
                    for n in range(2):
                        for k, what in enumerate("gb"):
                            ld_column(ln_in, ln_col[:, n, k, :], w[f"ln{n + 1}_{what}"])
                            ld_column(ln_in, mod_col[:, n, k, :], mod_bias[n][k])

                qkv = w_raw[0][:, W_QKV:W_PROJ].rearrange("p (k n) -> p k n", k=KC)
                if layer == 0:
                    for n, m in enumerate(("g1", "b1", "g2", "b2", "a1", "a2")):
                        ld(mods_in, mod_raw[n], rows(w[m + "_w"]))
                    ld_columns([[w["g1_b"], w["b1_b"]], [w["g2_b"], w["b2_b"]]])
                    ld(w_in[0], qkv, rows(w["qkv_w"]))
                    qbias, kbias, vbias = (w["qkv_b"][n * D:(n + 1) * D] for n in range(3))
                    proj_w, proj_b, w1, b1, w2, b2 = (w[n] for n in ("proj_w", "proj_b", "fc1_w", "fc1_b", "fc2_w",
                                                                     "fc2_b"))
                else:
                    ld_columns([[w[f"ada{n}_b"][D:2 * D], w[f"ada{n}_b"][0:D]] for n in (1, 2)])
                    for n, m in enumerate("qkv"):
                        ld(w_in[0], qkv[:, :, n * D:(n + 1) * D], rows(w["w" + m]))
                    qbias, kbias, vbias = w["bq"], w["bk"], w["bv"]
                    proj_w, proj_b, w1, b1, w2, b2 = (w[n] for n in ("wo", "bo", "ff_w1", "ff_b1", "ff_w2", "ff_b2"))
                half = NJ * HD
                for c in range(KC):
                    ld(w_in[0], w_raw[0][c * half:(c + 1) * half, W_PROJ:W_FF1].rearrange("r (x n) -> r x n", x=NX),
                       proj_w[c * P:(c + 1) * P, :].rearrange("(x r) n -> r x n", x=NX))
                ld(w_in[1], w_raw[1].rearrange("p (k n) -> p k n", k=KC), rows(w1))
                ld(w_in[2], w_raw[2].rearrange("p (k n) -> p k n", k=MC), rows(w2))
                if layer == 1:
                    sp.wait_ge(z_lo, KC * NT)
                    for n in range(2):
                        for k in range(2):
                            ld(mods_in, mod_raw[2 * n + k], rows(w[f"ada{n + 1}_w"][:, (1 - k) * D:(2 - k) * D]))
                for c in range(KC):
                    ld_column(bias_in, v_bias[c * half:(c + 1) * half, layer, :], vbias[c * P:(c + 1) * P], half)
                ld_column(bias_in, qk_bias[:, layer, 0:KC], qbias)
                ld_column(bias_in, qk_bias[:, layer, KC:2 * KC], kbias)
                ld_column(bias_in, b1_col[:, layer, :], b1)
                ld(bias_in, bo_bc[:, layer, :], proj_b.partition_broadcast(P))
                ld(bias_in, b2_bc[:, layer, :], b2.partition_broadcast(P))
                if layer == 0:
                    for n in range(2):
                        ld(bias_in, gate_row[:, n, :], row(w[f"a{n + 1}_b"]))
                else:
                    ld(bias_in, rtab[:, :, :], t["rotary"])

            def setup(layer):
                if layer == 0:
                    sp.dma_start(cond_sb, t["cond_1024"]).then_inc(cond_in, 16)
                    sp.dma_start(mask_u8[:, :], t["mask_BxS_bf1"]).then_inc(cond_in, 16)
                    load_tokens(0, 0)
                    load_weights(0)

            def front(u, layer):
                pass

            def finish(layer):
                if layer == 0:
                    sp.wait_ge(dve_setup, SET_MASKS)
                    sp.dma_start(mask_rows, mask_add).then_inc(gates_out, 16)
                    sp.wait_ge(dve_setup, SET_GATES)
                    for n in range(2):
                        sp.dma_start(gates[n], gate_rows[:, n, :]).then_inc(gates_out, 16)
                    sp.wait_ge(gates_out, 48)
                    sp.wait_ge(w_lo, NSPLIT)
                else:
                    sp.wait_ge(x_stored, 16 * NT)

            def spread_keys(u):
                waits = [(qk_hi, upto(u, 4, KC)), (qk_lo, upto(u, 4, KC))]
                if not first(u):
                    waits.append((pe_s, upto(u, 2 * G, 0)))
                else:
                    waits.append((k_zero, 1))
                wait_apart(sp, sp_passed, *waits)
                for r in range(0, P, HD):
                    sp.dma_start(kb[r:r + HD, :, :, r // HD % NJ, :].rearrange("p c q n -> p (c q) n").bitcast(F32),
                                 kflat[r:r + HD, :, :, :].rearrange("p c q n -> p (c q) n").bitcast(F32))\
                      .then_inc(kb_in, 16)

            def step(u, layer, attn, ffn, nxt):
                v = u - 1
                if nxt:
                    wait_apart(sp, sp_passed, (xn_ready, upto(u, G, G)))
                    load_tokens(u + 1, layer)
                if attn and layer == 0:
                    spread_keys(u)
                if attn and layer == 0:
                    if not first(u):
                        wait_apart(sp, sp_passed, (x1_added, upto(u, G, 0)))
                    for b in range(2):
                        sp.dma_start(gate_bc[0][b * S:(b + 1) * S, :, :],
                                     gate_tiles[0][u, b].partition_broadcast(S)).then_inc(gate1_in, 16)
                if ffn and layer == 0:
                    if not first(v):
                        wait_apart(sp, sp_passed, (f2_added, upto(v, 2, 0)))
                    for b in range(2):
                        sp.dma_start(gate_bc[1][b * S:(b + 1) * S, :, :],
                                     gate_tiles[1][v, b].partition_broadcast(S)).then_inc(gate2_in, 16)
                if attn and layer == 1:
                    wait_apart(sp, sp_passed, (pe_s, upto(u, 2 * G, 0)))
                    sp.dma_start(mrow[:, :].bitcast(F32), mask_tiles[u - NT].partition_broadcast(P))\
                      .then_inc(mrow_in, 16)
                    for i in range(2 * KC):
                        waits = [(rot_ready, upto(u - NT, 4, i + 1))]
                        if not (known(u) and u == NT):
                            waits.append((rot_sum, upto(u - NT, 4, i - 3)))
                        wait_apart(sp, sp_passed, *waits)
                        for e in range(2):
                            sp.dma_start(rot_s[e:P:2, i, :], rot_t[1 - e:P:2, i, :]).then_inc(swapped[i], 16)
                    spread_keys(u)
                if attn:
                    if ffn:
                        wait_apart(sp, sp_passed, (x1m_ready, upto(v, 1, 1)))
                    sp.dma_start(x_res, tokens_of(u, layer)).then_inc(xres_loaded, 16)
                if layer == 0 and not attn:
                    sp.wait_ge(pe_pv, 2 * G * NT)
                    sp.wait_ge(x1_added, G * NT)
                    sp.wait_ge(xn_ready, G * NT)
                    sp.wait_ge(x_stored, 16)
                    load_tokens(NT, 1)
                    load_weights(1)
                if ffn:
                    wait_apart(sp, sp_passed, (f2_done[layer], upto(v, 2, 2)))
                    sp.dma_start(mid_tiles[v] if layer == 0 else out_tiles[v - NT], x1m).then_inc(x_stored, 16)

            for layer in range(2):
                layer_steps(sp, layer, setup, front, finish, step)
            sp.wait_ge(x_stored, 16 * 2 * NT)

        @block.gpsimd
        def _(pool):
            pool.memset(ident[:, :], 0.0).then_inc(sem_ident, 1)
            pool.wait_ge(sem_ident, 1)
            pool.affine_select(out=ident[:, :], in_=ident[:, :], compare_op=ALU.not_equal, fill=1.0, base=0,
                               pattern=[[-1, P]], channel_multiplier=1).then_inc(sem_ident, 1)
            pool.memset(minus_half[:, :], -0.5).then_inc(sem_ident, 1)
            pool.wait_ge(sem_ident, 3)
            pool.memset(kb[...].bitcast(F32), 0.0).then_inc(k_zero, 1)

            def setup(layer):
                first_rstd(layer * NT)

            def finish(layer):
                all_of(pool, bias_in, N_BIAS, layer)
                pool.wait_ge(w_lo, NSPLIT * layer + 2)
                pool.memset(vb[...], 0.0).then_inc(v_blank, 1)
                if layer == 0:
                    for h in range(2):
                        pool.wait_ge(v_blank, h + 1)
                        dst = vb[h * S:(h + 1) * S, :, :].rearrange("p b (n e) -> p b n e", e=2 * VB)[
                            :, :, :, h * VB + HD]
                        pool.memset(dst, 1.0).then_inc(v_blank, 1)
                    pool.wait_ge(v_blank, 3)

            def first_rstd(u):
                pool.wait_ge(ln1_chain, upto(u, 9, 9))
                pool.tensor_tensor(rs1[:, :], rs1[:, :], minus_half[:, :], ALU.pow).then_inc(ln1_rstd, 1)

            def second_rstd(u, g):
                pool.wait_ge(ln2_chain, upto(u, 3 * G, 3 * g + 3))
                pool.tensor_tensor(rs2[:, g:g + 1], rs2[:, g:g + 1], minus_half[:, g:g + 1], ALU.pow)\
                    .then_inc(ln2_rstd, 1)

            def low_part(u, c, hi_sem, dst, done):
                pool.wait_ge(hi_sem, upto(u, KC, c + 1))
                pool.tensor_tensor(dst[1][:, c, :], aff[:, c, :], dst[0][:, c, :].bitcast(F32), ALU.subtract)\
                    .then_inc(done, 1)

            def front(u, layer, c=None):
                for c in range(KC) if c is None else (c,):
                    low_part(u, c, y_hi, yb, y_lo)

            def bias_rows(bias, layer):
                return bias[:, layer, :].rearrange("p (o d) -> p o d", o=1).to_broadcast([P, G, D])

            def gated_bias(dst, gate, bias, done):
                pool.tensor_tensor(dst, gate, bias_rows(bias, 0), ALU.mult).then_inc(done, 1)

            def sine(u, i):
                pool.wait_ge(swapped[i], upto(u - NT, 32, 32))
                part = rot_s[:, i, :].rearrange("p (b s) -> p b s", b=TB)
                pool.tensor_tensor(part, part, rtab[:, 1:2, :].to_broadcast([P, TB, S]), ALU.mult)\
                    .then_inc(rot_sin, 1)

            def hidden_low(v, m):
                if not (first(v) and m < 2):
                    pool.wait_ge(pe_f2, upto(v, MC, max(m - 1, 0)))
                pool.wait_ge(h_hi, upto(v, MC, m + 1))
                pool.tensor_tensor(hb[1][:, m % 2, :], hact[:, m % 2, :], hb[0][:, m % 2, :].bitcast(F32),
                                   ALU.subtract).then_inc(h_lo, 1)

            def step(u, layer, attn, ffn, nxt):
                v = u - 1
                if ffn:
                    low_part(v, 0, z_hi, zb, z_lo)
                if attn and layer == 1:
                    sine(u, 0)
                if attn and layer == 1:
                    sine(u, 1)
                    sine(u, 2)
                if ffn:
                    hidden_low(v, 0)
                if attn and layer == 1:
                    sine(u, 3)
                if ffn:
                    hidden_low(v, 1)
                if nxt:
                    first_rstd(u + 1)
                if attn and layer == 0:
                    pool.wait_ge(gate1_in, upto(u, 32, 32))
                    if not first(u):
                        pool.wait_ge(xres_ready, upto(u, 1, 0))
                    gated_bias(gated_bo, gate_bc[0], bo_bc, xres_chain)
                if ffn:
                    pool.wait_ge(x1_done[layer], upto(v, G, G))
                    pool.wait_ge(zn_ready, upto(v, G, G))
                    if not first(v):
                        pool.wait_ge(x_stored, upto(v, 16, 0))
                    if layer == 0:
                        pool.wait_ge(gate2_in, upto(v, 32, 32))
                        gated_bias(x1m, gate_bc[1], b2_bc, x1m_chain)
                        hidden_low(v, 2)
                        pool.wait_ge(x1m_chain, upto(v, 1, 1))
                        pool.tensor_tensor(x1m, x1m, x_res, ALU.add).then_inc(x1m_ready, 1)
                    else:
                        pool.tensor_tensor(x1m, x_res, bias_rows(b2_bc, layer), ALU.add).then_inc(x1m_ready, 1)
                        hidden_low(v, 2)
                if ffn and layer == 0:
                    hidden_low(v, 3)
                if attn:
                    pool.wait_ge(xres_loaded, upto(u, 16, 16))
                    if layer == 0:
                        pool.wait_ge(xres_chain, upto(u, 1, 1))
                    pool.tensor_tensor(x_res, x_res, gated_bo if layer == 0 else bias_rows(bo_bc, layer), ALU.add)\
                        .then_inc(xres_ready, 1)
                if attn and layer == 1:
                    pool.wait_ge(pe_pv, upto(u, 2 * G, 0))
                    if known(u) and u == NT:
                        pool.wait_ge(dve_setup, SET_MASKT)
                    pool.wait_ge(xres_ready, upto(u, 1, 1))
                    if ffn:
                        pool.wait_ge(h_lo, upto(v, MC, 3))
                    for h in range(2):
                        r = slice(h * S, (h + 1) * S)
                        dst = vb[r, :, :].rearrange("p b (n e) -> p b n e", e=2 * VB)[:, :, :, h * VB + HD]
                        src = maskT[r, bass.ds((u - NT) * TB, TB)].rearrange("p (b o) -> p b o", o=1)
                        pool.tensor_copy(dst, src.to_broadcast([S, TB, H // 2])).then_inc(v_ones, 1)
                        pool.wait_ge(v_ones, upto(u - NT, 2, h + 1))
                for g in range(G):
                    if ffn and not (layer == 0 and g == 0):
                        hidden_low(v, 3 + g)
                    if attn and 0 < g < G - 1:
                        second_rstd(u, g - 1)
                    if nxt and g == G - 2:
                        front(u + 1, layer, 0)
                if ffn:
                    hidden_low(v, MC - 1)
                if attn:
                    second_rstd(u, G - 2)
                if nxt:
                    front(u + 1, layer, 1)
                if attn:
                    second_rstd(u, G - 1)
                if ffn and layer == 0:
                    for h in range(2):
                        pool.wait_ge(f2_read, upto(v, 2, h + 1))
                        part = slice(2 * h, 2 * h + 2)
                        pool.tensor_tensor(x1m[:, part, :], gate_bc[1][:, part, :], x1m[:, part, :], ALU.add)\
                            .then_inc(f2_added, 1)

            for layer in range(2):
                layer_steps(pool, layer, setup, front, finish, step)

        @block.scalar
        def _(act):
            def setup(layer):
                for n, part in enumerate(SPLITS):
                    all_of(act, w_in[n], N_W[n], layer)
                    if layer == 1 and n == 0:
                        act.wait_ge(pe_proj, G * NT)
                    if layer == 1 and n > 0:
                        act.wait_ge(pe_f2, MC * NT)
                    nc.scalar.copy(wgt[0][:, part], w_raw[n]).then_inc(w_hi, 1)

            def finish(layer):
                if layer == 0:
                    act.wait_ge(pe_setup, PE_GATES)
                    nc.scalar.activation(hact[:, 1, :], C[:, :], ACT.Tanh).then_inc(act_setup, 1)
                all_of(act, bias_in, N_BIAS, layer)
                act.wait_ge(w_lo, NSPLIT * (layer + 1))

            def front(u, layer, c=None):
                for c in range(KC) if c is None else (c,):
                    act.wait_ge(y_aff, upto(u, KC, c + 1))
                    if not first(u):
                        act.wait_ge(pe_v, upto(u, 2, 0))
                    nc.scalar.copy(yb[0][:, c, :], aff[:, c, :]).then_inc(y_hi, 1)

            def second_norm(v, c):
                act.wait_ge(z_aff, upto(v, KC, c + 1))
                if not first(v):
                    act.wait_ge(pe_f1, upto(v, MC, 0))
                nc.scalar.copy(zb[0][:, c, :], aff[:, c, :]).then_inc(z_hi, 1)

            def chunk(i):
                return (i % KC, i < KC)

            def before_rotation(u, i):
                c, keys = chunk(i)
                act.wait_ge(pe_qk, upto(u, 4, i + 1))
                if not (known(u) and u == NT):
                    act.wait_ge(qk_lo, upto(u, 4, i - 3))
                col = KC * keys + c
                nc.scalar.activation(rot_t[:, i, :], (A + B)[i][:, :], ACT.Identity,
                                     bias=qk_bias[:, 1, col:col + 1]).then_inc(rot_ready, 1)

            def high_qk(u, layer, i):
                c, keys = chunk(i)
                if layer == 0:
                    act.wait_ge(pe_qk, upto(u, 4, i + 1))
                    src = (A + B)[i]
                    bias = qk_bias[:, 0, KC * keys + c:KC * keys + c + 1]
                else:
                    act.wait_ge(rot_sum, upto(u - NT, 4, i + 1))
                    src = rot_t[:, i, :]
                    bias = None
                if keys:
                    if not first(u):
                        act.wait_ge(kb_in, upto(u, NKB, 0))
                    parts = [(slice(0, P), by_seq(kflat[:, c, 0, :]))]
                else:
                    if not first(u):
                        act.wait_ge(pe_s, upto(u, 2 * G, 0))
                    if first(u) and i == KC:
                        act.wait_ge(sem_zero, NZERO)
                    parts = [(slice(x * 64, x * 64 + 64), qb[0][x * 64:x * 64 + 64, c, :, x, :]) for x in range(NX)]
                for n, (r, dst) in enumerate(parts):
                    if bias is not None:
                        ins = nc.scalar.activation(dst, by_seq(src[r, :]), ACT.Identity, bias=bias[r, :])
                    else:
                        ins = nc.scalar.copy(dst, by_seq(src[r, :]))
                    if n == len(parts) - 1:
                        ins.then_inc(qk_hi, 1)

            def values(u, pair):
                if known(u) and u % NT == 0:
                    act.wait_ge(v_blank, (3, 4)[u // NT])
                else:
                    act.wait_ge(pe_pv, upto(u, 2 * G, 0))
                act.wait_ge(pe_v, upto(u, 2, pair + 1))
                for b in range(2):
                    for h in range(2):
                        dst, src = value_views(pair, b, h)
                        nc.scalar.copy(dst, src).then_inc(v_moved, 1)

            def hidden(v, layer, m):
                act.wait_ge(pe_f1, upto(v, MC, m + 1))
                if not (first(v) and m < 2):
                    act.wait_ge(h_lo, upto(v, MC, max(m - 1, 0)))
                nc.scalar.activation(hact[:, m % 2, :], C[:, :], ACT.Gelu, bias=b1_col[:, layer, m:m + 1])\
                    .then_inc(gelu, 1)
                act.wait_ge(gelu, upto(v, MC, m + 1))
                if not (first(v) and m < 2):
                    act.wait_ge(pe_f2, upto(v, MC, max(m - 1, 0)))
                nc.scalar.copy(hb[0][:, m % 2, :], hact[:, m % 2, :]).then_inc(h_hi, 1)

            def exponentials(u, g):
                for b in range(2):
                    act.wait_ge(s_sub, upto(u, 2 * G, 2 * g + b + 1))
                    nc.scalar.activation(exps[:, b, :], exps[:, b, :], ACT.Exp, scale=SCORE_SCALE)\
                        .then_inc(s_exp, 1)

            def move_probs(u, g):
                for b in range(2):
                    act.wait_ge(pe_pt, upto(u, 2 * G, 2 * g + b + 1))
                    if not (first(u) and g == 0):
                        act.wait_ge(pe_pv, upto(u, 2 * G, max(2 * (g - 1) + b + 1, 0)))
                    nc.scalar.copy(pt[:, b, :], B[b][:, :]).then_inc(pt_moved, 1)

            def high_heads(u, layer, g):
                act.wait_ge(pe_ot, upto(u, G, g + 1))
                if not (first(u) and g == 0):
                    act.wait_ge(pe_proj, upto(u, G, g))
                for x in range(NX):
                    nc.scalar.activation(ot[0][:, x, :].rearrange("p (b q) -> p b q", b=2), head_rows(x), ACT.Identity,
                                         bias=v_bias[:, layer, x:x + 1]).then_inc(ot_hi, 1)

            def step(u, layer, attn, ffn, nxt):
                v = u - 1
                if attn:
                    for i in range(2 * KC - 1):
                        if layer == 0:
                            high_qk(u, layer, i)
                        else:
                            before_rotation(u, i)
                if ffn:
                    second_norm(v, 0)
                if attn and layer == 0:
                    high_qk(u, layer, 2 * KC - 1)
                if attn and layer == 1:
                    before_rotation(u, 2 * KC - 1)
                if ffn:
                    second_norm(v, 1)
                if attn and layer == 0:
                    values(u, 0)
                    values(u, 1)
                for i in range(KC):
                    if attn and layer == 1:
                        high_qk(u, layer, i)
                for i in range(KC):
                    if ffn:
                        hidden(v, layer, i)
                    if attn and layer == 1:
                        values(u, i)
                        high_qk(u, layer, KC + i)
                if attn and layer == 0:
                    exponentials(u, 0)
                if ffn:
                    hidden(v, layer, 2)
                if attn and layer == 1:
                    exponentials(u, 0)
                for g in range(G):
                    if attn:
                        move_probs(u, g)
                    if attn and g > 0:
                        high_heads(u, layer, g - 1)
                    if attn and g < G - 1:
                        exponentials(u, g + 1)
                    if ffn:
                        hidden(v, layer, 3 + g)
                    if nxt and g == G - 2:
                        front(u + 1, layer, 0)
                if ffn:
                    hidden(v, layer, MC - 1)
                if nxt:
                    front(u + 1, layer, 1)
                if attn:
                    high_heads(u, layer, G - 1)

            for layer in range(2):
                layer_steps(act, layer, setup, front, finish, step)

        @block.tensor
        def _(pe):
            def product(dst, pairs, first_start=True, last_stop=True, **kw):
                todo = [(l[p], r[q]) for l, r in pairs for p, q in PASSES]
                for n, (l, r) in enumerate(todo):
                    ins = nc.tensor.matmul(dst, l, r, start=first_start and n == 0,
                                           stop=last_stop and n == len(todo) - 1, **kw)
                return ins

            def w(base, width, k, lo, n):
                return [w_slice(p, base, width, k, lo, n) for p in range(2)]

            def setup(layer):
                if layer == 0:
                    pe.wait_ge(sem_ident, 2)
                    pe.wait_ge(cond_in, 32)
                    for k in range(KC):
                        ins = nc.tensor.transpose(E[:, k * P:(k + 1) * P], cond_sb[:, k * P:(k + 1) * P], ident[:, :])
                    ins.then_inc(pe_setup, 1)
                    pe.wait_ge(dve_setup, SET_MASKS)
                    nc.tensor.transpose(E[:, 0:P], mask01[:, :, :].rearrange("p a s -> p (a s)"), ident[:, :])\
                        .then_inc(pe_setup, 1)
                else:
                    pe.wait_ge(f2_read, 2 * NT)
                all_of(pe, mods_in, N_MODS, layer)
                for n in range(2):
                    for k in range(2):
                        for c in range(KC):
                            dst = Dk[n][:, (2 * k + c) * P:(2 * k + c + 1) * P]
                            for q in range(KC):
                                ins = nc.tensor.matmul(dst, mod_raw[2 * n + k][:, q, c * P:(c + 1) * P], condT[:, q, :],
                                                       start=(q == 0), stop=(q == KC - 1))
                ins.then_inc(pe_setup, 1)
                if layer == 0:
                    pe.wait_ge(dve_setup, SET_MASKT)

            def finish(layer):
                if layer == 0:
                    pe.wait_ge(sem_zero, NZERO)
                    all_of(pe, bias_in, N_BIAS, layer)
                    for n in range(2):
                        dst = C[:, n * D:(n + 1) * D]
                        for q in range(KC):
                            nc.tensor.matmul(dst, condT[:, q, :], mod_raw[4 + n][:, q, :], start=(q == 0), stop=False)
                        ins = nc.tensor.matmul(dst, ones[:, :], gate_row[:, n, :], start=False, stop=True)
                    ins.then_inc(pe_setup, 1)
                pe.wait_ge(w_lo, NSPLIT * layer + 1)

            def front(u, layer, c=None):
                for c in range(KC) if c is None else (c,):
                    pe.wait_ge(xn_ready, upto(u, G, G))
                    if c == 1:
                        pe.wait_ge(y_aff, upto(u, KC, 1))
                    if not (known(u) and u % NT == 0):
                        pe.wait_ge(proj_read, upto(u - 1, G, G - KC + c))
                    for g in range(G):
                        ins = nc.tensor.transpose(E[:, g * P:(g + 1) * P], xn[:, g, c * P:(c + 1) * P], ident[:, :])
                    ins.then_inc(pe_yt, 1)

            def second_norm(v, c, attn):
                pe.wait_ge(zn_ready, upto(v, G, G))
                if c == 0:
                    pe.wait_ge(proj_read, upto(v, G, G))
                    if attn:
                        pe.wait_ge(y_aff, upto(v + 1, KC, KC))
                else:
                    pe.wait_ge(z_aff, upto(v, KC, 1))
                for g in range(G):
                    ins = nc.tensor.transpose(E[:, g * P:(g + 1) * P], zn[:, g, c * P:(c + 1) * P], ident[:, :])
                ins.then_inc(pe_zt, 1)

            def queries_keys(u, i):
                c, keys = i % KC, i < KC
                if i == 0:
                    pe.wait_ge(y_hi, upto(u, KC, KC))
                    pe.wait_ge(y_lo, upto(u, KC, KC))
                if not first(u):
                    if i < 2:
                        pe.wait_ge(s_sub, upto(u, 2 * G, 0))
                    else:
                        pe.wait_ge(pv_norm, upto(u, 2 * G, 0))
                product((A + B)[i][:, :], [(w(W_QKV, 3 * D, k, D * keys + c * P, P), [yb[q][:, k, :] for q in range(2)])
                                           for k in range(KC)]).then_inc(pe_qk, 1)

            def chunk_taken(u, layer, i):
                if layer == 0:
                    pe.wait_ge(qk_lo, upto(u, 4, i + 1))
                else:
                    pe.wait_ge(rot_ready, upto(u - NT, 4, i + 1))

            def values(u, layer, pair):
                chunk_taken(u, layer, pair)
                for g in (2 * pair, 2 * pair + 1):
                    ins = product(A[pair][:, (g % 2) * D:(g % 2 + 1) * D],
                                  [([yb[p][:, k, g * P:(g + 1) * P] for p in range(2)], w(W_QKV, 3 * D, k, 2 * D, D))
                                   for k in range(KC)])
                ins.then_inc(pe_v, 1)

            def scores(u, layer, g):
                if g == 0:
                    pe.wait_ge(qk_hi, upto(u, 4, 4))
                    pe.wait_ge(qk_lo, upto(u, 4, 4))
                    pe.wait_ge(kb_in, upto(u, NKB, NKB))
                    pe.wait_ge(v_moved, upto(u, 8, 8))
                    if layer == 1:
                        pe.wait_ge(mrow_in, upto(u - NT, 16, 16))
                for b in range(2):
                    if g > 0:
                        pe.wait_ge(s_sub, upto(u, 2 * G, 2 * g + b - 1))
                    s = slice((2 * g + b) * S, (2 * g + b + 1) * S)
                    for c in range(KC):
                        dst = A[b][:, c * 256:(c + 1) * 256]
                        ins = product(dst, [([qb[p][:, c, 2 * g + b, :, :].rearrange("p x s -> p (x s)") for p in range(2)],
                                             [kb[:, c, q, :, s] for q in range(2)])], last_stop=(layer == 0))
                        if layer == 1:
                            row = mrow[:, s].rearrange("p (o s) -> p o s", o=1).to_broadcast([P, NJ, S])
                            ins = nc.tensor.matmul(dst, mean_w[:, :], row, start=False, stop=True)
                    ins.then_inc(pe_s, 1)

            def turn_probs(u, layer, g):
                for b in range(2):
                    if g == 0:
                        chunk_taken(u, layer, 2 + b)
                    else:
                        pe.wait_ge(pv_norm, upto(u, 2 * G, 2 * g + b - 1))
                    pe.wait_ge(s_exp, upto(u, 2 * G, 2 * g + b + 1))
                    for n in range(4):
                        ins = nc.tensor.transpose(B[b][:, n * P:(n + 1) * P], exps[:, b, n * P:(n + 1) * P], ident[:, :])
                    ins.then_inc(pe_pt, 1)

            def weigh_values(u, layer, g):
                if layer == 1 and g == 0:
                    pe.wait_ge(v_ones, upto(u - NT, 2, 2))
                for b in range(2):
                    pe.wait_ge(pt_moved, upto(u, 2 * G, 2 * g + b + 1))
                    for c in range(KC):
                        for jp in range(2):
                            n = 2 * c + jp
                            moving = vb[:, 2 * g + b, c * 136:(c + 1) * 136].rearrange("p (x e) -> p x e", x=NX)[
                                :, :, jp * 34:(jp + 1) * 34]
                            ins = nc.tensor.matmul(B[b][:, n * 68:(n + 1) * 68], pt[:, b, n * P:(n + 1) * P], moving,
                                                   start=True, stop=True)
                    ins.then_inc(pe_pv, 1)

            def turn_heads(u, g, ffn, nxt):
                if g == 0:
                    pe.wait_ge(y_aff, upto(u, KC, KC))
                    if ffn:
                        pe.wait_ge(z_aff, upto(u - 1, KC, KC))
                else:
                    pe.wait_ge(proj_read, upto(u, G, g))
                    if g >= G - KC and nxt:
                        pe.wait_ge(y_aff, upto(u + 1, KC, g - (G - KC) + 1))
                pe.wait_ge(pv_norm, upto(u, 2 * G, 2 * g + 2))
                for b in range(2):
                    ins = nc.tensor.transpose(E[:, b * P:(b + 1) * P], o_sb[:, b, :], ident[:, :])
                ins.then_inc(pe_ot, 1)

            def project(u, g):
                pe.wait_ge(ot_hi, upto(u, 8, 2 * g + 2))
                pe.wait_ge(ot_lo, upto(u, 8, 2 * g + 2))
                product(E[:, D:2 * D], [([ot[p][:, x, :] for p in range(2)], w(W_PROJ, D, x, 0, D)) for x in range(NX)])\
                    .then_inc(pe_proj, 1)

            def hidden(v, m):
                if m == 0 and known(v) and v % NT == 0:
                    pe.wait_ge(w_lo, NSPLIT * (v // NT + 1))
                    pe.wait_ge(dve_setup, (SET_GATES, SET_MOD[1])[v // NT])
                if m == 0:
                    pe.wait_ge(z_hi, upto(v, KC, KC))
                    pe.wait_ge(z_lo, upto(v, KC, KC))
                if not (first(v) and m == 0):
                    pe.wait_ge(gelu, upto(v, MC, m))
                product(C[:, :], [(w(W_FF1, FF, k, m * P, P), [zb[q][:, k, :] for q in range(2)]) for k in range(KC)])\
                    .then_inc(pe_f1, 1)

            def back(v, m):
                pe.wait_ge(h_lo, upto(v, MC, m + 1))
                if m == 0 and not first(v):
                    pe.wait_ge(f2_read, upto(v, 2, 0))
                for g in range(G):
                    ins = product(Dk[g // 2][:, (g % 2) * D:(g % 2 + 1) * D],
                                  [([hb[p][:, m % 2, g * P:(g + 1) * P] for p in range(2)], w(W_FF2, D, m, 0, D))],
                                  first_start=(m == 0 and g % 2 == 0), last_stop=(m == MC - 1), skip_group_check=True)
                ins.then_inc(pe_f2, 1)

            def step(u, layer, attn, ffn, nxt):
                v = u - 1
                if attn:
                    queries_keys(u, 0)
                    queries_keys(u, 1)
                    queries_keys(u, 2)
                if ffn:
                    second_norm(v, 0, attn)
                if attn:
                    queries_keys(u, 3)
                if ffn:
                    second_norm(v, 1, attn)
                if attn:
                    values(u, layer, 0)
                    values(u, layer, 1)
                if ffn:
                    hidden(v, 0)
                if ffn and layer == 0:
                    hidden(v, 1)
                if attn and layer == 0:
                    scores(u, layer, 0)
                if ffn:
                    if layer == 1:
                        hidden(v, 1)
                    back(v, 0)
                    hidden(v, 2)
                    back(v, 1)
                if attn and layer == 1:
                    scores(u, layer, 0)
                for g in range(G):
                    if ffn and layer == 1 and g == 0:
                        hidden(v, 3 + g)
                    if attn:
                        turn_probs(u, layer, g)
                    if attn and 0 < g < G - 1:
                        turn_heads(u, g - 1, ffn, nxt)
                    if attn and g < G - 1:
                        scores(u, layer, g + 1)
                    if ffn and g == G - 1:
                        hidden(v, 3 + g)
                    if attn and g == G - 1:
                        turn_heads(u, g - 1, ffn, nxt)
                    if ffn and g == G - 1:
                        back(v, 2 + g)
                    if attn:
                        weigh_values(u, layer, g)
                    if attn and g > 0:
                        project(u, g - 1)
                    if ffn and g < G - 1 and not (layer == 1 and g == 0):
                        hidden(v, 3 + g)
                    if nxt and g == G - 2:
                        front(u + 1, layer, 0)
                    if ffn and g < G - 1:
                        back(v, 2 + g)
                if ffn:
                    hidden(v, MC - 1)
                if nxt:
                    front(u + 1, layer, 1)
                if ffn:
                    back(v, MC - 2)
                if attn:
                    turn_heads(u, G - 1, ffn, nxt)
                if ffn:
                    back(v, MC - 1)
                if attn:
                    project(u, G - 1)

            for layer in range(2):
                layer_steps(pe, layer, setup, front, finish, step)

        @block.vector
        def _(dve):
            for buf in qb:
                nc.vector.memset(buf[...].bitcast(F32), 0.0).then_inc(sem_zero, 1)
            nc.vector.memset(mean_w[:, :].bitcast(F32), 1.0 / P).then_inc(sem_zero, 1)
            nc.vector.memset(ones[:, :], 1.0).then_inc(sem_zero, 1)

            def modulations(at):
                n_done = at
                for n in range(2):
                    for c in range(KC):
                        s_psum, t_psum = Dk[n][:, c * P:(c + 1) * P], Dk[n][:, (2 + c) * P:(3 + c) * P]
                        scale, shift = mod[:, n, c, 0, :], mod[:, n, c, 1, :]
                        nc.vector.tensor_scalar(scale, s_psum, mod_col[:, n, 0, c:c + 1], 1.0, ALU.add, ALU.add)\
                            .then_inc(dve_setup, 1)
                        nc.vector.tensor_scalar(shift, t_psum, mod_col[:, n, 1, c:c + 1], None, ALU.add)\
                            .then_inc(dve_setup, 1)
                        dve.wait_ge(dve_setup, n_done + 2)
                        nc.vector.scalar_tensor_tensor(out=shift, in0=scale, scalar=ln_col[:, n, 1, c:c + 1], in1=shift,
                                                       op0=ALU.mult, op1=ALU.add).then_inc(dve_setup, 1)
                        nc.vector.tensor_scalar(scale, scale, ln_col[:, n, 0, c:c + 1], None, ALU.mult)\
                            .then_inc(dve_setup, 1)
                        n_done += 4
                dve.wait_ge(dve_setup, n_done)

            def setup(layer):
                if layer == 0:
                    dve.wait_ge(pe_setup, PE_CONDT)
                    nc.vector.tensor_copy(condT[:, :, :], E[:, 0:KC * P].rearrange("p (k b) -> p k b", k=KC))\
                        .then_inc(dve_setup, 1)
                    dve.wait_ge(cond_in, 32)
                    nc.vector.tensor_scalar(mask_add, mask_u8[:, :], BIG, -BIG, ALU.mult, ALU.add)\
                        .then_inc(dve_setup, 1)
                    for n in range(2):
                        nc.vector.tensor_copy(mask01[:, n, :], mask_u8[:, :]).then_inc(dve_setup, 1)
                first_statistics(layer * NT)
                if layer == 0:
                    dve.wait_ge(pe_setup, PE_MASKT)
                    nc.vector.tensor_copy(maskT[:, :], E[:, 0:P]).then_inc(dve_setup, 1)
                if layer == 1:
                    low_weights(layer, 0)
                first_norm(layer * NT)
                dve.wait_ge(ln_in, 16 * N_LN * (layer + 1))
                dve.wait_ge(pe_setup, PE_MOD[layer])
                modulations(SET_MOD[layer] - NMOD)
                if layer == 0:
                    low_weights(layer, 0)

            def low_weights(layer, n):
                dve.wait_ge(w_hi, NSPLIT * layer + n + 1)
                nc.vector.tensor_tensor(wgt[1][:, SPLITS[n]], w_raw[n], wgt[0][:, SPLITS[n]].bitcast(F32),
                                        ALU.subtract).then_inc(w_lo, 1)

            def finish(layer):
                if layer == 0:
                    dve.wait_ge(act_setup, 1)
                    nc.vector.tensor_scalar(hact[:, 1, :], hact[:, 1, :], GATE, None, ALU.mult).then_inc(dve_setup, 1)
                low_weights(layer, 1)
                low_weights(layer, 2)
                all_of(dve, bias_in, N_BIAS, layer)

            def normalise(dst, src, mean, rstd):
                return nc.vector.tensor_scalar(dst, src, mean, rstd, ALU.subtract, ALU.mult)

            def first_statistics(u):
                dve.wait_ge(x_loaded, upto(u, 16, 16))
                for g in range(G):
                    nc.vector.bn_stats(st1[:, g, :], x_in[:, g, :]).then_inc(ln1_chain, 1)
                wait_apart(dve, dve_passed, (ln1_chain, upto(u, 9, 4)))
                for g in range(G):
                    nc.vector.bn_aggr(mv1[:, g, :], st1[:, g, :]).then_inc(ln1_chain, 1)
                dve.wait_ge(ln1_chain, upto(u, 9, 8))
                nc.vector.tensor_scalar(rs1[:, :], mv1[:, :, 1], EPS, None, ALU.add).then_inc(ln1_chain, 1)

            def first_norm(u):
                dve.wait_ge(ln1_rstd, upto(u, 1, 1))
                if not first(u):
                    dve.wait_ge(pe_yt, upto(u, KC, 0))
                for g in range(G):
                    normalise(xn[:, g, :], x_in[:, g, :], mv1[:, g, 0:1], rs1[:, g:g + 1]).then_inc(xn_ready, 1)

            def tile_modulation(u, layer, n, done):
                if not first(u):
                    dve.wait_ge(done, upto(u, KC, 0))
                nc.vector.tensor_copy(mod_tile[:, n, :, :, :],
                                      mod[:, n, :, :, bass.ds((u - layer * NT) * TB, TB)]).then_inc(mod_ready[n], 1)

            def modulate(u, n, c, turned, chain, done):
                part = by_seq(aff[:, c, :])
                scale, shift = (mod_tile[:, n, c, k, :].rearrange("p (b o) -> p b o", o=1).to_broadcast([P, TB, S])
                                for k in range(2))
                dve.wait_ge(mod_ready[n], upto(u, 1, 1))
                dve.wait_ge(turned, upto(u, KC, c + 1))
                nc.vector.tensor_tensor(part, by_seq(E[:, :]), scale, ALU.mult).then_inc(chain, 1)
                dve.wait_ge(chain, upto(u, KC, c + 1))
                nc.vector.tensor_tensor(part, part, shift, ALU.add).then_inc(done, 1)

            def first_modulated(u, c):
                if c == 0 and not (known(u) and u % NT < 2):
                    dve.wait_ge(z_lo, upto(u - 2, KC, KC))
                if c == 0 and known(u) and u % NT == 1:
                    dve.wait_ge(y_lo, upto(u, KC, 0))
                modulate(u, 0, c, pe_yt, y_scaled, y_aff)

            def second_modulated(v, c, attn):
                if c == 0:
                    dve.wait_ge(y_lo, upto(v, KC, 2 * KC if attn else KC))
                modulate(v, 1, c, pe_zt, z_scaled, z_aff)

            def front(u, layer):
                tile_modulation(u, layer, 0, y_aff)
                for c in range(KC):
                    first_modulated(u, c)

            def low_qk(u, layer, i):
                c, keys = i % KC, i < KC
                col = KC * keys + c
                dve.wait_ge(qk_hi, upto(u, 4, i + 1))
                rows = [slice(0, P)] if keys else [slice(0, 64), slice(64, 128)]
                for x, r in enumerate(rows):
                    hi = by_seq(kflat[:, c, 0, :]) if keys else qb[0][r, c, :, x, :]
                    lo = by_seq(kflat[:, c, 1, :]) if keys else qb[1][r, c, :, x, :]
                    if layer == 0:
                        ins = nc.vector.scalar_tensor_tensor(out=lo, in0=by_seq((A + B)[i][r, :]), scalar=qk_bias[r, 0, col:col + 1],
                                                             in1=hi.bitcast(F32), op0=ALU.add, op1=ALU.subtract)
                    else:
                        ins = nc.vector.tensor_tensor(lo, by_seq(rot_t[r, i, :]), hi.bitcast(F32), ALU.subtract)
                ins.then_inc(qk_lo, 1)

            def cosine(u, i):
                dve.wait_ge(swapped[i], upto(u - NT, 32, 32))
                part = rot_t[:, i, :].rearrange("p (b s) -> p b s", b=TB)
                nc.vector.tensor_tensor(part, part, rtab[:, 0:1, :].to_broadcast([P, TB, S]), ALU.mult)\
                    .then_inc(rot_cos, 1)

            def rotated(u, i):
                dve.wait_ge(rot_cos, upto(u - NT, 4, i + 1))
                dve.wait_ge(rot_sin, upto(u - NT, 4, i + 1))
                nc.vector.tensor_tensor(rot_t[:, i, :], rot_t[:, i, :], rot_s[:, i, :], ALU.add)\
                    .then_inc(rot_sum, 1)

            def subtract_max(u, g):
                for b in range(2):
                    dve.wait_ge(pe_s, upto(u, 2 * G, 2 * g + b + 1))
                    s = A[b][:, :].rearrange("p (h k) -> p h k", k=S)
                    nc.vector.tensor_reduce(mx[:, b, :], s, AX.X, ALU.max).then_inc(s_max, 1)
                    dve.wait_ge(s_max, upto(u, 2 * G, 2 * g + b + 1))
                    if not (first(u) and g == 0):
                        dve.wait_ge(pe_pt, upto(u, 2 * G, max(2 * (g - 1) + b + 1, 0)))
                    nc.vector.tensor_tensor(exps[:, b, :].rearrange("p (h k) -> p h k", k=S), s,
                                            mx[:, b, :].rearrange("p (h o) -> p h o", o=1).to_broadcast([P, 8, S]),
                                            ALU.subtract).then_inc(s_sub, 1)

            def normalise_heads(u, g):
                if not (first(u) and g == 0):
                    dve.wait_ge(pe_ot, upto(u, G, g))
                for b in range(2):
                    dve.wait_ge(pe_pv, upto(u, 2 * G, 2 * g + b + 1))
                    sums = B[b][:, 0:4 * 68].rearrange("p (n x j e) -> p n x j e", n=4, x=NX, e=VB)
                    r = rden[:, b, :].rearrange("p (n j) -> p n j", n=4)
                    nc.vector.reciprocal(r, sums[:, :, 0, :, HD]).then_inc(pv_rden, 1)
                    dve.wait_ge(pv_rden, upto(u, 2 * G, 2 * g + b + 1))
                    for x in range(NX):
                        p = slice(x * 64, x * 64 + 64)
                        ins = nc.vector.tensor_tensor(
                            o_sb[p, b, :].rearrange("p (n j d) -> p n j d", n=4, j=2), sums[p, :, x, :, 0:HD],
                            rden[p, b, :].rearrange("p (n j o) -> p n j o", n=4, o=1).to_broadcast([64, 4, 2, HD]),
                            ALU.mult)
                    ins.then_inc(pv_norm, 1)

            def low_heads(u, layer, g):
                dve.wait_ge(ot_hi, upto(u, 8, 2 * g + 2))
                for x in range(NX):
                    as_rows = [ot[p][:, x, :].rearrange("p (b q) -> p b q", b=2) for p in range(2)]
                    nc.vector.scalar_tensor_tensor(out=as_rows[1], in0=head_rows(x), scalar=v_bias[:, layer, x:x + 1],
                                                   in1=as_rows[0].bitcast(F32), op0=ALU.add, op1=ALU.subtract)\
                        .then_inc(ot_lo, 1)

            def residual(u, layer, g):
                dve.wait_ge(pe_proj, upto(u, G, g + 1))
                if g == 0:
                    dve.wait_ge(xres_ready, upto(u, 1, 1))
                if layer == 0:
                    gate = gate_bc[0][:, g, :]
                    nc.vector.tensor_tensor(gate, E[:, D:2 * D], gate, ALU.mult).then_inc(proj_read, 1)
                    dve.wait_ge(proj_read, upto(u, G, g + 1))
                    nc.vector.tensor_tensor(x_res[:, g, :], gate, x_res[:, g, :], ALU.add).then_inc(x1_added, 1)
                else:
                    nc.vector.tensor_tensor(x_res[:, g, :], E[:, D:2 * D], x_res[:, g, :], ALU.add)\
                        .then_inc(proj_read, 1)

            def second_statistics(u, layer, g):
                dve.wait_ge(x1_done[layer], upto(u, G, g + 1))
                nc.vector.bn_stats(st2[:, g, :], x_res[:, g, :]).then_inc(ln2_chain, 1)
                wait_apart(dve, dve_passed, (ln2_chain, upto(u, 3 * G, 3 * g + 1)))
                nc.vector.bn_aggr(mv2[:, g, :], st2[:, g, :]).then_inc(ln2_chain, 1)
                dve.wait_ge(ln2_chain, upto(u, 3 * G, 3 * g + 2))
                nc.vector.tensor_scalar(rs2[:, g:g + 1], mv2[:, g, 1:2], EPS, None, ALU.add).then_inc(ln2_chain, 1)

            def second_normalise(u, g, ffn):
                dve.wait_ge(ln2_rstd, upto(u, G, g + 1))
                if g == 0 and ffn:
                    dve.wait_ge(pe_zt, upto(u, KC, 0))
                normalise(zn[:, g, :], x_res[:, g, :], mv2[:, g, 0:1], rs2[:, g:g + 1]).then_inc(zn_ready, 1)

            def layer_output(v, layer, h):
                if h == 0:
                    dve.wait_ge(pe_f2, upto(v, MC, MC))
                    dve.wait_ge(x1m_ready, upto(v, 1, 1))
                acc = Dk[h][:, :].rearrange("p (g d) -> p g d", g=2)
                part = slice(2 * h, 2 * h + 2)
                if layer == 0:
                    gate = gate_bc[1][:, part, :]
                    nc.vector.tensor_tensor(gate, acc, gate, ALU.mult).then_inc(f2_read, 1)
                else:
                    nc.vector.tensor_tensor(x1m[:, part, :], acc, x1m[:, part, :], ALU.add).then_inc(f2_read, 1)

            def step(u, layer, attn, ffn, nxt):
                v = u - 1
                if ffn:
                    tile_modulation(v, layer, 1, z_aff)
                if attn and layer == 0:
                    low_qk(u, layer, 0)
                    low_qk(u, layer, 1)
                if ffn:
                    second_modulated(v, 0, attn)
                if ffn:
                    second_modulated(v, 1, attn)
                if attn and layer == 0:
                    low_qk(u, layer, 2)
                if attn and layer == 1:
                    cosine(u, 0)
                if ffn:
                    dve.wait_ge(z_hi, upto(v, KC, KC))
                    nc.vector.tensor_tensor(zb[1][:, KC - 1, :], aff[:, KC - 1, :], zb[0][:, KC - 1, :].bitcast(F32),
                                            ALU.subtract).then_inc(z_lo, 1)
                if attn and layer == 0:
                    low_qk(u, layer, 3)
                if attn and layer == 1:
                    cosine(u, 1)
                    rotated(u, 0)
                    cosine(u, 2)
                    rotated(u, 1)
                    low_qk(u, layer, 0)
                    low_qk(u, layer, 1)
                    cosine(u, 3)
                    rotated(u, 2)
                if nxt:
                    first_statistics(u + 1)
                if attn and layer == 1:
                    rotated(u, 3)
                    low_qk(u, layer, 2)
                    low_qk(u, layer, 3)
                if attn:
                    subtract_max(u, 0)
                for g in range(G):
                    if attn and g > 0:
                        low_heads(u, layer, g - 1)
                    if attn and g > 1:
                        second_normalise(u, g - 2, ffn)
                    if attn and g < G - 1:
                        subtract_max(u, g + 1)
                    if attn and g == G - 1:
                        normalise_heads(u, g)
                    if attn and g > 0:
                        residual(u, layer, g - 1)
                    if attn and g < G - 1:
                        normalise_heads(u, g)
                    if g >= G - KC and nxt:
                        first_modulated(u + 1, g - (G - KC))
                    if g == 0 and nxt:
                        tile_modulation(u + 1, layer, 0, y_aff)
                        first_norm(u + 1)
                    if attn and g > 0:
                        second_statistics(u, layer, g - 1)
                if attn:
                    second_normalise(u, G - 2, ffn)
                    low_heads(u, layer, G - 1)
                if ffn:
                    layer_output(v, layer, 0)
                if attn:
                    residual(u, layer, G - 1)
                    second_statistics(u, layer, G - 1)
                if ffn:
                    layer_output(v, layer, 1)
                if attn:
                    second_normalise(u, G - 1, ffn)

            for layer in range(2):
                layer_steps(dve, layer, setup, front, finish, step)


_INS = ["x", "cond_1024", "mask_BxS_bf1"] + [
    "L0_cond_" + n for n in ("g1_w", "g1_b", "b1_w", "b1_b", "a1_w", "a1_b", "g2_w", "g2_b", "b2_w", "b2_b", "a2_w",
                             "a2_b", "ln1_g", "ln1_b", "ln2_g", "ln2_b", "qkv_w", "qkv_b", "proj_w", "proj_b", "fc1_w",
                             "fc1_b", "fc2_w", "fc2_b")] + [
    "L1_cond_" + n for n in ("wq", "bq", "wk", "bk", "wv", "bv", "wo", "bo", "ln1_g", "ln1_b", "ada1_w", "ada1_b",
                             "ln2_g", "ln2_b", "ada2_w", "ada2_b", "ff_w1", "ff_b1", "ff_w2", "ff_b2")]


def rotary_table():
    import numpy as np
    inv = np.float32(1.0) / np.float32(10000.0) ** (np.arange(ROT, dtype=np.float32) / np.float32(ROT))
    angle = np.arange(S, dtype=np.float32)[:, None] * inv[None, :].astype(np.float32)
    d = np.arange(P) % HD
    sign = np.where(d % 2 == 0, -1.0, 1.0).astype(np.float32)
    cos, sin = np.cos(angle).T[d // 2], np.sin(angle).T[d // 2] * sign[:, None]
    return np.ascontiguousarray(np.stack([cos, sin], axis=1).astype(np.float32))


def kernel(**inputs):
    import numpy as np
    import concourse.bacc as bacc
    from concourse.bass_utils import run_bass_kernel_spmd

    nc = bacc.Bacc("TRN2", target_bir_lowering=False, num_devices=1)
    arrays, tensors = {}, {}
    for name in _INS + ["rotary"]:
        a = rotary_table() if name == "rotary" else np.ascontiguousarray(inputs[name])
        if a.dtype == np.bool_:
            a = a.view(np.uint8)
        arrays[f"in_{name}"] = a
        tensors[name] = nc.dram_tensor(f"in_{name}", a.shape, mybir.dt.from_np(a.dtype), kind="ExternalInput").ap()
    out = nc.dram_tensor("out", (NB, S, D), F32, kind="ExternalOutput").ap()
    build(nc, tensors, out)
    r = run_bass_kernel_spmd(nc, [arrays], core_ids=[0])
    return r.results[0]["out"]
```
